# Optimizing a Trainium2 kernel written in Bass

```python
import numpy as np
import jax
import jax.numpy as jnp

def _softmax(x, axis=-1):
    return jax.nn.softmax(x, axis=axis)

def _gelu(x):
    return jax.nn.gelu(x, approximate=True)

def _silu(x):
    return jax.nn.silu(x)

def _sigmoid(x):
    return jax.nn.sigmoid(x)

def _layernorm(x, axis=-1, eps=1e-05):
    m = jnp.mean(x, axis=axis, keepdims=True)
    v = jnp.var(x, axis=axis, keepdims=True)
    return (x - m) / jnp.sqrt(v + eps)

def _scatter_add(tgt, idx, src, axis=0):
    return tgt.at[idx].add(src)

def _segment_sum(src, seg, n):
    return jax.ops.segment_sum(src, seg, n)
kernel_name = 'mk_gnn_preln_d4_gnn_r32_9dc3d6'

def setup_inputs(seed: int=0):
    np.random.seed(seed)
    _w = jnp.asarray

    def _rec_inputs():
        import jax
        import jax.numpy as jnp
        _gk = jax.random.key(seed)
        x = -0.000202 + 1 * jax.random.normal(jax.random.fold_in(_gk, 1), (3125, 128), jnp.float32)
        src = jax.random.randint(jax.random.fold_in(_gk, 2), (50000,), 0, 3125, jnp.int32)
        dst = jax.random.randint(jax.random.fold_in(_gk, 3), (50000,), 0, 3125, jnp.int32)
        _o = jnp.argsort(dst, stable=True)
        src = src[_o]
        dst = dst[_o]
        edge_attr_256 = -6.47781e-05 + 0.999943 * jax.random.normal(jax.random.fold_in(_gk, 11), (50000, 256), jnp.float32)
        edge_weight = jax.random.uniform(jax.random.fold_in(_gk, 13), (50000,), jnp.float32, 0.0, 5)
        edge_weight1 = jax.random.uniform(jax.random.fold_in(_gk, 14), (50000, 1), jnp.float32, 0.0, 0.999998)
        return (x, src, dst, edge_attr_256, edge_weight, edge_weight1)
    x, src, dst, edge_attr_256, edge_weight, edge_weight1 = _rec_inputs()

    def _L0_gnn_setup():
        import jax, jax.numpy as jnp
        import numpy as np
        N_NODES = 50000
        N_EDGES = 31250

        def _gat_layer(x, edge_index, edge_prob, W, Wt, a_src, a_trg, a_tp, b, Wskip, concat):
            N = x.shape[0]
            H, F = (a_src.shape[1], a_src.shape[2])
            src, trg = (edge_index[0], edge_index[1])
            proj = (x @ W).reshape(N, H, F)
            tp_proj = (edge_prob @ Wt).reshape(-1, H, F)
            s_src = jnp.sum(proj * a_src, axis=-1)
            s_trg = jnp.sum(proj * a_trg, axis=-1)
            s_tp = jnp.sum(tp_proj * a_tp, axis=-1)
            scores = jax.nn.leaky_relu(s_src[src] + s_trg[trg] + s_tp, 0.2)
            exp_s = jnp.exp(scores - jnp.max(scores))
            denom = jax.ops.segment_sum(exp_s, trg, num_segments=N)[trg]
            att = (exp_s / (denom + 1e-16))[:, :, None]
            out = jax.ops.segment_sum(proj[src] * att, trg, num_segments=N)
            if Wskip is None:
                out = out + x[:, None, :]
            else:
                out = out + (x @ Wskip).reshape(N, H, F)
            out = out.reshape(N, H * F) if concat else out.mean(axis=1)
            return jax.nn.elu(out + b)
        key = jax.random.key(seed)
        ks = jax.random.split(key, 16)
        s = 0.05
        return {'x': jax.random.normal(ks[0], (N_NODES, 128), jnp.float32), 'edge_index': jax.random.randint(ks[1], (2, N_EDGES), 0, N_NODES, jnp.int32), 'edge_prob': jax.random.uniform(ks[2], (N_EDGES, 1), jnp.float32), 'W1': jax.random.normal(ks[3], (128, 128), jnp.float32) * s, 'Wt1': jax.random.normal(ks[4], (1, 128), jnp.float32) * s, 'a_src1': jax.random.normal(ks[5], (1, 8, 16), jnp.float32) * s, 'a_trg1': jax.random.normal(ks[6], (1, 8, 16), jnp.float32) * s, 'a_tp1': jax.random.normal(ks[7], (1, 8, 16), jnp.float32) * s, 'b1': jnp.zeros((128,), jnp.float32), 'Wskip1': jax.random.normal(ks[8], (128, 128), jnp.float32) * s, 'W2': jax.random.normal(ks[9], (128, 128), jnp.float32) * s, 'Wt2': jax.random.normal(ks[10], (1, 128), jnp.float32) * s, 'a_src2': jax.random.normal(ks[11], (1, 1, 128), jnp.float32) * s, 'a_trg2': jax.random.normal(ks[12], (1, 1, 128), jnp.float32) * s, 'a_tp2': jax.random.normal(ks[13], (1, 1, 128), jnp.float32) * s, 'b2': jnp.zeros((128,), jnp.float32)}
    _L0_gnn_all = _L0_gnn_setup()
    _L0_gnn_in = {k: v for k, v in _L0_gnn_all.items() if k in ('W1', 'Wt1', 'a_src1', 'a_trg1', 'a_tp1', 'b1', 'Wskip1', 'W2', 'Wt2', 'a_src2', 'a_trg2', 'a_tp2', 'b2')}
    del _L0_gnn_all

    def _L1_gnn_setup():
        import jax, jax.numpy as jnp
        import numpy as np
        N, E, D, L = (50000, 20000, 128, 3)
        EPS = 1e-05
        key = jax.random.key(seed)
        ks = jax.random.split(key, 8)
        x = jax.random.normal(ks[0], (N, D), dtype=jnp.float32)
        edge_index = jax.random.randint(ks[1], (2, E), 0, N, dtype=jnp.int64)
        scale = 1.0 / np.sqrt(D)
        Ws = jax.random.normal(ks[2], (L, D, D), dtype=jnp.float32) * scale
        bs = jax.random.normal(ks[3], (L, D), dtype=jnp.float32) * 0.01
        inner = (L + 1) * D
        bn_gamma = jnp.ones((inner,), dtype=jnp.float32)
        bn_beta = jnp.zeros((inner,), dtype=jnp.float32)
        Wout = jax.random.normal(ks[4], (inner, D), dtype=jnp.float32) / np.sqrt(inner)
        bout = jax.random.normal(ks[5], (D,), dtype=jnp.float32) * 0.01
        return {'x': x, 'edge_index': edge_index, 'Ws': Ws, 'bs': bs, 'bn_gamma': bn_gamma, 'bn_beta': bn_beta, 'Wout': Wout, 'bout': bout}
    _L1_gnn_all = _L1_gnn_setup()
    _L1_gnn_in = {k: v for k, v in _L1_gnn_all.items() if k in ('Ws', 'bs', 'bn_gamma', 'bn_beta', 'Wout', 'bout')}
    del _L1_gnn_all

    def _L2_gnn_setup():
        import jax, jax.numpy as jnp
        import numpy as np
        N_NODES = 3125
        N_EDGES = 25000
        FEAT = 128
        key = jax.random.key(seed)
        k1, k2, k3, k4 = jax.random.split(key, 4)
        node_attr = jax.random.normal(k1, (N_NODES, FEAT), dtype=jnp.float32)
        edge_attr = jax.random.normal(k2, (N_EDGES, 2 * FEAT), dtype=jnp.float32)
        edge_index = jax.random.randint(k3, (2, N_EDGES), 0, N_NODES, dtype=jnp.int64)
        W = jax.random.normal(k4, (2 * FEAT, FEAT), dtype=jnp.float32) * (1.0 / np.sqrt(2 * FEAT))
        b = jnp.zeros((FEAT,), dtype=jnp.float32)
        return {'node_attr': node_attr, 'edge_attr': edge_attr, 'edge_index': edge_index, 'W': W, 'b': b}
    _L2_gnn_all = _L2_gnn_setup()
    _L2_gnn_in = {k: v for k, v in _L2_gnn_all.items() if k in ('W', 'b')}
    del _L2_gnn_all

    def _L3_gnn_setup():
        import jax, jax.numpy as jnp
        import numpy as np
        N_NODES = 50000
        N_EDGES = 46875
        FEAT = 128
        CUTOFF = 5.0
        key = jax.random.key(seed)
        k_x, k_ei, k_el, k_w = jax.random.split(key, 4)
        x = jax.random.normal(k_x, (N_NODES, FEAT), dtype=jnp.float32)
        edge_index = jax.random.randint(k_ei, (2, N_EDGES), 0, N_NODES, dtype=jnp.int64)
        edge_len = jax.random.uniform(k_el, (N_EDGES,), dtype=jnp.float32) * CUTOFF
        W_mix = jax.random.normal(k_w, (FEAT, FEAT), dtype=jnp.float32) / np.sqrt(FEAT)
        log_scale = jnp.asarray(np.log(6.0), dtype=jnp.float32)
        filter_w = jnp.asarray(0.7, dtype=jnp.float32)
        filter_b = jnp.asarray(0.1, dtype=jnp.float32)
        return {'x': x, 'edge_index': edge_index, 'edge_len': edge_len, 'W_mix': W_mix, 'log_scale': log_scale, 'filter_w': filter_w, 'filter_b': filter_b}
    _L3_gnn_all = _L3_gnn_setup()
    _L3_gnn_in = {k: v for k, v in _L3_gnn_all.items() if k in ('W_mix', 'log_scale', 'filter_w', 'filter_b')}
    del _L3_gnn_all
    return {'x': x, 'src': src, 'dst': dst, 'edge_attr_256': edge_attr_256, 'edge_weight': edge_weight, 'edge_weight1': edge_weight1, 'L0_gnn_W1': _L0_gnn_in['W1'], 'L0_gnn_Wt1': _L0_gnn_in['Wt1'], 'L0_gnn_a_src1': _L0_gnn_in['a_src1'], 'L0_gnn_a_trg1': _L0_gnn_in['a_trg1'], 'L0_gnn_a_tp1': _L0_gnn_in['a_tp1'], 'L0_gnn_b1': _L0_gnn_in['b1'], 'L0_gnn_Wskip1': _L0_gnn_in['Wskip1'], 'L0_gnn_W2': _L0_gnn_in['W2'], 'L0_gnn_Wt2': _L0_gnn_in['Wt2'], 'L0_gnn_a_src2': _L0_gnn_in['a_src2'], 'L0_gnn_a_trg2': _L0_gnn_in['a_trg2'], 'L0_gnn_a_tp2': _L0_gnn_in['a_tp2'], 'L0_gnn_b2': _L0_gnn_in['b2'], 'L1_gnn_Ws': _L1_gnn_in['Ws'], 'L1_gnn_bs': _L1_gnn_in['bs'], 'L1_gnn_bn_gamma': _L1_gnn_in['bn_gamma'], 'L1_gnn_bn_beta': _L1_gnn_in['bn_beta'], 'L1_gnn_Wout': _L1_gnn_in['Wout'], 'L1_gnn_bout': _L1_gnn_in['bout'], 'L2_gnn_W': _L2_gnn_in['W'], 'L2_gnn_b': _L2_gnn_in['b'], 'L3_gnn_W_mix': _L3_gnn_in['W_mix'], 'L3_gnn_log_scale': _L3_gnn_in['log_scale'], 'L3_gnn_filter_w': _L3_gnn_in['filter_w'], 'L3_gnn_filter_b': _L3_gnn_in['filter_b']}

def reference(x, src, dst, edge_attr_256, edge_weight, edge_weight1, L0_gnn_W1, L0_gnn_Wt1, L0_gnn_a_src1, L0_gnn_a_trg1, L0_gnn_a_tp1, L0_gnn_b1, L0_gnn_Wskip1, L0_gnn_W2, L0_gnn_Wt2, L0_gnn_a_src2, L0_gnn_a_trg2, L0_gnn_a_tp2, L0_gnn_b2, L1_gnn_Ws, L1_gnn_bs, L1_gnn_bn_gamma, L1_gnn_bn_beta, L1_gnn_Wout, L1_gnn_bout, L2_gnn_W, L2_gnn_b, L3_gnn_W_mix, L3_gnn_log_scale, L3_gnn_filter_w, L3_gnn_filter_b):
    import jax
    import jax.numpy as jnp

    def _L0_gnn_ref(x, edge_index, edge_prob, W1, Wt1, a_src1, a_trg1, a_tp1, b1, Wskip1, W2, Wt2, a_src2, a_trg2, a_tp2, b2):
        import jax, jax.numpy as jnp
        import numpy as np
        N_NODES = 50000
        N_EDGES = 31250

        def _gat_layer(x, edge_index, edge_prob, W, Wt, a_src, a_trg, a_tp, b, Wskip, concat):
            N = x.shape[0]
            H, F = (a_src.shape[1], a_src.shape[2])
            src, trg = (edge_index[0], edge_index[1])
            proj = (x @ W).reshape(N, H, F)
            tp_proj = (edge_prob @ Wt).reshape(-1, H, F)
            s_src = jnp.sum(proj * a_src, axis=-1)
            s_trg = jnp.sum(proj * a_trg, axis=-1)
            s_tp = jnp.sum(tp_proj * a_tp, axis=-1)
            scores = jax.nn.leaky_relu(s_src[src] + s_trg[trg] + s_tp, 0.2)
            exp_s = jnp.exp(scores - jnp.max(scores))
            denom = jax.ops.segment_sum(exp_s, trg, num_segments=N)[trg]
            att = (exp_s / (denom + 1e-16))[:, :, None]
            out = jax.ops.segment_sum(proj[src] * att, trg, num_segments=N)
            if Wskip is None:
                out = out + x[:, None, :]
            else:
                out = out + (x @ Wskip).reshape(N, H, F)
            out = out.reshape(N, H * F) if concat else out.mean(axis=1)
            return jax.nn.elu(out + b)
        h = _gat_layer(x, edge_index, edge_prob, W1, Wt1, a_src1, a_trg1, a_tp1, b1, Wskip1, concat=True)
        out = _gat_layer(h, edge_index, edge_prob, W2, Wt2, a_src2, a_trg2, a_tp2, b2, None, concat=False)
        return out

    def _L1_gnn_ref(x, edge_index, Ws, bs, bn_gamma, bn_beta, Wout, bout):
        import jax, jax.numpy as jnp
        import numpy as np
        N, E, D, L = (50000, 20000, 128, 3)
        EPS = 1e-05
        n = x.shape[0]
        src, dst = (edge_index[0], edge_index[1])
        ones_e = jnp.ones((src.shape[0],), dtype=x.dtype)
        deg = jax.ops.segment_sum(ones_e, dst, num_segments=n) + 1.0
        dinv = jax.lax.rsqrt(deg)
        enorm = (dinv[src] * dinv[dst])[:, None]
        self_norm = (dinv * dinv)[:, None]
        out_cnt = jax.ops.segment_sum(ones_e, src, num_segments=n)
        out_cnt = jnp.maximum(out_cnt, 1.0)[:, None]
        x_cat = [x]
        for i in range(L):
            h = x @ Ws[i]
            agg = jax.ops.segment_sum(h[src] * enorm, dst, num_segments=n)
            x_ = jax.nn.relu(agg + self_norm * h + bs[i])
            tau = x_
            diff2 = (tau[src] - tau[dst]) ** 2
            gg = jnp.tanh(jax.ops.segment_sum(diff2, src, num_segments=n) / out_cnt)
            x = (1.0 - gg) * x + gg * x_
            x_cat.append(x)
        xc = jnp.concatenate(x_cat, axis=-1)
        mean = jnp.mean(xc, axis=0)
        var = jnp.var(xc, axis=0)
        xn = (xc - mean) * jax.lax.rsqrt(var + EPS) * bn_gamma + bn_beta
        return xn @ Wout + bout

    def _L2_gnn_ref(node_attr, edge_attr, edge_index, W, b):
        import jax, jax.numpy as jnp
        import numpy as np
        N_NODES = 3125
        N_EDGES = 25000
        FEAT = 128
        N, F = node_attr.shape
        two_edge = jnp.concatenate(jnp.split(edge_attr, 2, axis=-1), axis=0)
        senders, receivers = (edge_index[0], edge_index[1])
        out_idx = jnp.concatenate([receivers, senders], axis=0)
        scale = jnp.sqrt(jnp.asarray(F, dtype=node_attr.dtype))
        logits = jnp.sum(two_edge * node_attr[out_idx], axis=1, keepdims=True) / scale
        seg_max = jax.ops.segment_max(logits, out_idx, num_segments=N)
        ex = jnp.exp(logits - seg_max[out_idx])
        denom = jax.ops.segment_sum(ex, out_idx, num_segments=N)
        attn = ex / denom[out_idx]
        agg = jax.ops.segment_sum(two_edge * attn, out_idx, num_segments=N)
        x = jnp.concatenate([agg, node_attr], axis=1) @ W + b
        return x

    def _L3_gnn_ref(x, edge_index, edge_len, W_mix, log_scale, filter_w, filter_b):
        import jax, jax.numpy as jnp
        import numpy as np
        N_NODES = 50000
        N_EDGES = 46875
        FEAT = 128
        CUTOFF = 5.0
        sender = edge_index[0]
        receiver = edge_index[1]
        n_nodes = x.shape[0]
        scale = jnp.exp(log_scale).astype(edge_len.dtype)
        decay = jnp.exp(-jnp.maximum(edge_len / (scale + 1e-06), 0.0) ** 2)
        gate = jax.nn.sigmoid(edge_len * filter_w + filter_b)
        weights = jnp.nan_to_num(decay * gate, nan=0.0, posinf=0.0, neginf=0.0)
        messages = weights[:, None].astype(x.dtype) * x[sender]
        agg = jax.ops.segment_sum(messages, receiver, num_segments=n_nodes)
        degree = jax.ops.segment_sum(jnp.ones_like(edge_len), receiver, num_segments=n_nodes)
        agg = agg / jnp.maximum(degree, 1.0)[:, None].astype(x.dtype)
        return x + agg @ W_mix
    edge_index = jnp.stack([src, dst])
    h = jnp.maximum(_layernorm(x, axis=-1), 0.0)
    x = x + _L0_gnn_ref(h, edge_index, edge_weight1, L0_gnn_W1, L0_gnn_Wt1, L0_gnn_a_src1, L0_gnn_a_trg1, L0_gnn_a_tp1, L0_gnn_b1, L0_gnn_Wskip1, L0_gnn_W2, L0_gnn_Wt2, L0_gnn_a_src2, L0_gnn_a_trg2, L0_gnn_a_tp2, L0_gnn_b2)
    h = jnp.maximum(_layernorm(x, axis=-1), 0.0)
    x = x + _L1_gnn_ref(h, edge_index, L1_gnn_Ws, L1_gnn_bs, L1_gnn_bn_gamma, L1_gnn_bn_beta, L1_gnn_Wout, L1_gnn_bout)
    h = jnp.maximum(_layernorm(x, axis=-1), 0.0)
    x = x + _L2_gnn_ref(h, edge_attr_256, edge_index, L2_gnn_W, L2_gnn_b)
    h = jnp.maximum(_layernorm(x, axis=-1), 0.0)
    x = x + _L3_gnn_ref(h, edge_index, edge_weight, L3_gnn_W_mix, L3_gnn_log_scale, L3_gnn_filter_w, L3_gnn_filter_b)
    return x

_drawn_inputs = setup_inputs


def setup_inputs(seed=0):
    import zlib

    import numpy as np

    out = dict(_drawn_inputs(seed))
    spreads = {'L0_gnn_b1': (0.0, 0.1),
     'L0_gnn_b2': (0.0, 0.1),
     'L1_gnn_bn_gamma': (1.0, 0.2),
     'L1_gnn_bn_beta': (0.0, 0.1),
     'L2_gnn_b': (0.0, 0.1)}
    factors = {'edge_weight': 113.174,
     'edge_weight1': 8.0,
     'L0_gnn_Wt1': 8.0,
     'L0_gnn_a_src1': 8.0,
     'L0_gnn_a_trg1': 43.499,
     'L0_gnn_a_tp1': 8.0,
     'L0_gnn_Wt2': 8.0,
     'L0_gnn_a_src2': 23.63,
     'L0_gnn_a_trg2': 122.482,
     'L0_gnn_a_tp2': 161.394,
     'L1_gnn_bs': 175.51,
     'L1_gnn_bout': 7.36,
     'L3_gnn_W_mix': 3.884}
    for name, (base, spread) in spreads.items():
        noise = np.random.default_rng([zlib.crc32(name.encode()), seed]).standard_normal(out[name].shape)
        drawn = base * np.exp(spread * noise) if base else spread * noise
        out[name] = jnp.asarray(drawn.astype(out[name].dtype))
    for name, factor in factors.items():
        out[name] = (out[name] * factor).astype(out[name].dtype)
    return out
```

```python
import concourse.bass as bass
from concourse import mybir
from contextlib import ExitStack

dt = mybir.dt
F32, I32, BF16 = dt.float32, dt.int32, dt.bfloat16
ALU = mybir.AluOpType
ACT = mybir.ActivationFunctionType
AX = mybir.AxisListType

P = 128
N, E, F = 3125, 50000, 128
NT = -(-N // P)
NP = NT * P
LAST = N - (NT - 1) * P
G = 4
GS = G * P
NG = (E + NT * (GS - 1)) // GS
T = NG * G
SLOTS = T * P
EC = E // P
ER = E - EC * P
CB = 8
CC = -(-(EC + 1) // (2 * CB)) * 2 * CB
RW = 8
BIG = 1.0e30
HUGE_SLOT = 1.0e6
NB = 5
EPS = 1e-5


class Chain:

    def __init__(self, eng, sem, base=0):
        self.eng, self.sem, self.base, self.n = eng, sem, base, 0

    def __call__(self, ins):
        self.n += 1
        ins.then_inc(self.sem, 1)
        self.eng.wait_ge(self.sem, self.base + self.n)


def wait_apart(eng, sem, value):
    eng.wait_ge(sem, value)
    eng.sem_inc(PASSED[0], 1)


PASSED = []
SPENT = []


def clear_semaphores(nc):
    nc.clear_and_free_semaphores(SPENT)
    nc.all_engine_barrier()
    SPENT.clear()


class Phase:

    def __init__(self, nc, name):
        self.nc, self.name, self.ctx, self.sems = nc, name, ExitStack(), []

    def __enter__(self):
        self.ctx.__enter__()
        return self

    def __exit__(self, *e):
        return self.ctx.__exit__(*e)

    def sb(self, name, shape, d=F32):
        return self.ctx.enter_context(self.nc.sbuf_tensor(f"{self.name}_{name}", shape, d))

    def ps(self, name, shape, d=F32):
        return self.ctx.enter_context(self.nc.psum_tensor(f"{self.name}_{name}", shape, d))

    def sem(self, name):
        s = self.nc.alloc_semaphore(f"{self.name}_{name}")
        SPENT.append(s)
        return s

    def block(self):
        return self.ctx.enter_context(self.nc.Block())


def constants(nc, C):
    with Phase(nc, "cst") as ph:
        made = ph.sem("made")
        block = ph.block()

        @block.gpsimd
        def _(pool):
            link = Chain(pool, made)
            link(nc.gpsimd.iota(C.iota_row[:], [[1, P]], base=0, channel_multiplier=0,
                                allow_small_or_imprecise_dtypes=True))
            link(nc.gpsimd.iota(C.iota_col[:], [[0, 1]], base=0, channel_multiplier=1,
                                allow_small_or_imprecise_dtypes=True))
            link(nc.gpsimd.memset(C.ones[:], 1.0))
            link(nc.gpsimd.memset(C.ident[:], 0.0))
            link(nc.gpsimd.affine_select(out=C.ident[:], in_=C.ident[:], compare_op=ALU.not_equal, fill=1.0,
                                         base=0, pattern=[[-1, P]], channel_multiplier=1))
            link(nc.gpsimd.affine_select(out=C.before[:], in_=C.ones[:], compare_op=ALU.is_ge, fill=0.0,
                                         base=-1, pattern=[[1, P]], channel_multiplier=-1))
            link(nc.gpsimd.memset(C.zerosb[:], 0.0))


def sort_edges(nc, C, name, key, other, attr_row, w1, w, rec, ntile, count, loc_dram, rec_dram):
    with Phase(nc, name) as ph:
        keyi = ph.sb("keyi", [P, CC], I32)
        otheri = ph.sb("otheri", [P, CC], I32)
        w1f = ph.sb("w1f", [P, CC])
        wf = ph.sb("wf", [P, CC])
        bucket = ph.sb("bucket", [P, CC], I32)
        bucketf = ph.sb("bucketf", [P, CC])
        locf = ph.sb("locf", [P, CC])
        zero = ph.sb("zero", [P, CC])
        mask = ph.sb("mask", [P, CC])
        cum = ph.sb("cum", [P, NT, CC])
        maskb = ph.sb("maskb", [P, CC, NT], BF16)
        low = ph.sb("low", [P, 2, CB, P], BF16)
        tot = ph.sb("tot", [P, NT])
        tots = ph.sb("tots", [P, 2, NT])
        toti = ph.sb("toti", [P, NT], I32)
        first = ph.sb("first", [P, NT])
        base = ph.sb("base", [P, NT])
        slot = ph.sb("slot", [P, CC])
        sloti = ph.sb("sloti", [P, CC], I32)
        part = ph.sb("part", [P, CC], I32)
        addr = ph.sb("addr", [P, CC], I32)
        r = ph.sb("r", [P, CC, RW])
        giota = ph.sb("giota", [P, NG])
        nta = ph.sb("nta", [P, NG])
        ring = ph.sb("ring", [P, 2, CB], I32)
        rring = ph.sb("rring", [P, 2, CB, RW])
        loct = ph.sb("loct", [P, G, P])
        p_tot = ph.ps("p_tot", [P, 2, NT])
        p_cnt = ph.ps("p_cnt", [P, NT])
        p_tr = ph.ps("p_tr", [P, G, P])
        loaded, chain, tot_ready, tot_done = (ph.sem(x) for x in ("loaded", "chain", "tot_ready", "tot_done"))
        low_ready, counted, filled = (ph.sem(x) for x in ("low_ready", "counted", "filled"))
        made, addr_ready, ring_ready = (ph.sem(x) for x in ("made", "addr_ready", "ring_ready"))
        scattered = [ph.sem(f"scattered{k}") for k in range(2)]
        rec_loaded, tr_ready, tr_done, pad_stored = (ph.sem(x) for x in ("rec_loaded", "tr_ready", "tr_done", "pad_stored"))
        loc_stored, pads = ph.sem("loc_stored"), ph.sem("pads")
        block = ph.block()
        blocks = CC // CB

        @block.sync
        def _(sp):
            sp.wait_ge(filled, 1)
            for to, frm in ((keyi, key), (otheri, other), (w1f, w1), (wf, w)):
                sp.dma_start(to[:, 0:EC], frm[0:EC * P].rearrange("(p c) -> p c", p=P)).then_inc(loaded, 16)
                sp.dma_start(to[0:ER, EC:EC + 1], frm[EC * P:E].unsqueeze(1)).then_inc(loaded, 16)
            sp.wait_ge(pads, 1)
            sp.dma_start(rec_dram.rearrange("(p t) w -> p (t w)", p=P),
                         rec[:].rearrange("p t w -> p (t w)")).then_inc(pad_stored, 16)
            for k in range(2):
                sp.wait_ge(scattered[k], 16 * CC // 2)
            sp.dma_start(rec[:].rearrange("p t w -> p (t w)"),
                         rec_dram.rearrange("(p t) w -> p (t w)", p=P)).then_inc(rec_loaded, 16)
            sp.wait_ge(tr_done, 1)
            tb = T // G
            for k in range(G):
                sp.dma_start(loc_dram[k * tb:(k + 1) * tb, :], loct[0:tb, k, :]).then_inc(loc_stored, 16)
            sp.wait_ge(loc_stored, 16 * G)

        @block.gpsimd
        def _(pool):
            nc.gpsimd.iota(giota[:], [[G, NG]], base=0, channel_multiplier=0,
                           allow_small_or_imprecise_dtypes=True).then_inc(made, 1)
            pool.wait_ge(filled, 1)
            nc.gpsimd.iota(r[:, 0:EC, 4].bitcast(I32), [[2, EC]], base=attr_row,
                           channel_multiplier=2 * EC).then_inc(made, 1)
            nc.gpsimd.iota(r[:, EC:EC + 1, 4].bitcast(I32), [[0, 1]], base=attr_row + 2 * EC * P,
                           channel_multiplier=2).then_inc(made, 1)
            pool.wait_ge(loaded, 8 * 16)
            nc.gpsimd.tensor_copy(r[:, :, 0].bitcast(I32), otheri[:]).then_inc(made, 1)
            nc.gpsimd.tensor_copy(r[:, :, 2], w1f[:]).then_inc(made, 1)
            nc.gpsimd.tensor_copy(r[:, :, 3], wf[:]).then_inc(made, 1)
            pool.wait_ge(made, 6)
            pool.wait_ge(addr_ready, 1)
            pool.wait_ge(pad_stored, 16)

            def scatter(i, u):
                c0 = i * (2 * CB) + u * CB
                nc.gpsimd.tensor_copy(ring[:, u, :], addr[:, bass.ds(c0, CB)]).then_inc(ring_ready, 1)
                nc.gpsimd.tensor_copy(rring[:, u, :, :], r[:, bass.ds(c0, CB), :]).then_inc(ring_ready, 1)
                wait_apart(pool, ring_ready, i * 4 + 2 * u + 2)
                for k in range(CB):
                    pool.indirect_dma_start(rec_dram, bass.IndirectOffsetOnAxis(ap=ring[:, u, k:k + 1], axis=0),
                                            rring[:, u, k, :], None, bounds_check=SLOTS - 1,
                                            oob_is_err=False).then_inc(scattered[u], 16)

            scatter(0, 0)
            scatter(0, 1)
            with pool.Fori(0, blocks // 2 - 1) as i:
                for u in range(2):
                    wait_apart(pool, scattered[u], i * (16 * CB) + 16 * CB)
                    scatter(i + 1, u)

        @block.vector
        def _(dve):
            link = Chain(dve, chain)
            link(nc.vector.memset(keyi[:], NT * P))
            link(nc.vector.memset(otheri[:], 0))
            link(nc.vector.memset(w1f[:], 0.0))
            link(nc.vector.memset(wf[:], 0.0))
            link(nc.vector.memset(zero[:], 0.0))
            link(nc.vector.memset(r[:], 0.0))
            nc.vector.tensor_copy(slot[:], zero[:]).then_inc(filled, 1)
            link(nc.vector.tensor_copy(nta[:], zero[:, 0:NG]))
            link(nc.vector.memset(rec[:], 0.0))
            nc.vector.memset(rec[:, :, 1], -1.0).then_inc(pads, 1)
            dve.wait_ge(filled, 1)
            dve.wait_ge(loaded, 8 * 16)
            link(nc.vector.tensor_single_scalar(bucket[:], keyi[:], 7, ALU.logical_shift_right))
            link(nc.vector.tensor_single_scalar(part[:], keyi[:], P - 1, ALU.bitwise_and))
            link(nc.vector.tensor_copy(bucketf[:], bucket[:]))
            link(nc.vector.tensor_copy(locf[:], part[:]))
            link(nc.vector.tensor_copy(r[:, :, 1], part[:]))
            for b in range(NT):
                nc.vector.tensor_scalar(maskb[:, :, b], bucketf[:], float(b), None, ALU.is_equal)
                link(nc.vector.tensor_scalar(mask[:], bucketf[:], float(b), None, ALU.is_equal))
                link(nc.vector.tensor_tensor_scan(cum[:, b, :], mask[:], zero[:], 0.0, ALU.add, ALU.add))
            link(nc.vector.tensor_copy(tot[:], cum[:, :, CC - 1]))
            nc.vector.memset(low[:], 0.0).then_inc(tot_ready, 1)
            dve.wait_ge(tot_done, 1)
            link(nc.vector.tensor_copy(tots[:], p_tot[:]))
            link(nc.vector.tensor_scalar(first[:], tots[:, 1, :], float(GS - 1), None, ALU.add))
            link(nc.vector.tensor_copy(toti[:], first[:]))
            link(nc.vector.tensor_single_scalar(toti[:], toti[:], GS.bit_length() - 1, ALU.logical_shift_right))
            link(nc.vector.tensor_copy(tot[:], toti[:]))
            link(nc.vector.tensor_tensor_scan(first[:], tot[:], zero[:, 0:NT], 0.0, ALU.add, ALU.add))
            link(nc.vector.tensor_tensor(first[:], first[:], tot[:], ALU.subtract))
            link(nc.vector.scalar_tensor_tensor(base[:], first[:], float(GS), tots[:, 0, :], ALU.mult, ALU.add))
            link(nc.vector.tensor_scalar(base[:], base[:], -1.0, None, ALU.add))
            for b in range(NT):
                link(nc.vector.scalar_tensor_tensor(cum[:, b, :], cum[:, b, :], base[:, b:b + 1], maskb[:, :, b],
                                                    ALU.add, ALU.mult))
                link(nc.vector.tensor_tensor(slot[:], slot[:], cum[:, b, :], ALU.add))
            link(nc.vector.tensor_copy(sloti[:], slot[:]))
            link(nc.vector.tensor_single_scalar(part[:], sloti[:], P - 1, ALU.bitwise_and))
            link(nc.vector.tensor_single_scalar(sloti[:], sloti[:], 7, ALU.logical_shift_right))
            link(nc.vector.tensor_copy(slot[:], part[:]))
            link(nc.vector.tensor_copy(mask[:], sloti[:]))
            link(nc.vector.scalar_tensor_tensor(slot[:], slot[:], float(T), mask[:], ALU.mult, ALU.add))
            link(nc.vector.tensor_scalar(mask[:], bucketf[:], float(NT), HUGE_SLOT, ALU.is_ge, ALU.mult))
            link(nc.vector.tensor_tensor(slot[:], slot[:], mask[:], ALU.add))
            nc.vector.tensor_copy(addr[:], slot[:]).then_inc(addr_ready, 1)
            dve.wait_ge(made, 1)
            link(nc.vector.tensor_scalar(first[:], first[:], float(G), None, ALU.mult))
            for b in range(1, NT):
                link(nc.vector.scalar_tensor_tensor(nta[:], giota[:], first[:, b:b + 1], nta[:], ALU.is_ge, ALU.add))
            link(nc.vector.tensor_copy(ntile[:], nta[:]))

            with dve.Fori(0, blocks // 2) as i:
                for u in range(2):
                    dve.wait_ge(counted, i * 2 + u + 1)
                    nc.vector.tensor_tensor(low[:, u, :, :], C.iota_row[:].unsqueeze(1).to_broadcast([P, CB, P]),
                                            locf[:, bass.ds(i * (2 * CB) + u * CB, CB)].unsqueeze(2).to_broadcast([P, CB, P]),
                                            ALU.is_equal).then_inc(low_ready, 1)
            dve.wait_ge(counted, blocks + 3)
            link(nc.vector.tensor_copy(count[:], p_cnt[:]))
            dve.wait_ge(tr_ready, 1)
            nc.vector.tensor_copy(loct[0:T // G], p_tr[0:T // G]).then_inc(tr_done, 1)

        @block.tensor
        def _(pe):
            pe.wait_ge(tot_ready, 1)
            nc.tensor.matmul(p_tot[:, 0, :], C.before[:], tot[:], start=True, stop=True)
            nc.tensor.matmul(p_tot[:, 1, :], C.ones[:], tot[:], start=True, stop=True).then_inc(tot_done, 1)
            nc.tensor.matmul(p_cnt[:], low[:, 0, 0, :], maskb[:, 0, :], start=True, stop=False).then_inc(counted, 1)
            pe.wait_ge(counted, 1)
            nc.tensor.nop().then_inc(counted, 1)
            with pe.Fori(0, blocks // 2) as i:
                for u in range(2):
                    pe.wait_ge(low_ready, i * 2 + u + 1)
                    for k in range(CB):
                        last = nc.tensor.matmul(p_cnt[:], low[:, u, k, :],
                                                maskb[:, bass.ds(i * (2 * CB) + u * CB + k, 1), :].squeeze(1),
                                                start=False, stop=False)
                    last.then_inc(counted, 1)
            nc.tensor.matmul(p_cnt[:], C.zerosb[:], maskb[:, 0, :], start=False, stop=True).then_inc(counted, 1)
            pe.wait_ge(rec_loaded, 16)
            tb = T // G
            for k in range(G):
                last = nc.tensor.transpose(p_tr[0:tb, k, :], rec[:, k * tb:(k + 1) * tb, 1], C.ident[:])
            last.then_inc(tr_ready, 1)


def gather_groups(nc, pool, rec, word, ring, copied, table, rows, gathered, used):
    def issue(i, u):
        nc.gpsimd.tensor_copy(ring[:, u, :], rec[:, bass.ds(i * (2 * G) + u * G, G), word].bitcast(I32)).then_inc(copied, 1)
        wait_apart(pool, copied, i * 2 + u + 1)
        for k in range(G):
            pool.indirect_dma_start(rows(u, k), None, table,
                                    bass.IndirectOffsetOnAxis(ap=ring[:, u, k:k + 1], axis=0)).then_inc(gathered[u], 16)

    issue(0, 0)
    issue(0, 1)
    with pool.Fori(0, NG // 2 - 1) as i:
        for u in range(2):
            wait_apart(pool, used, i * 2 + u + 1)
            issue(i + 1, u)


def load_key_rows(sp, loc, rowb, loaded, used):
    def issue(i, u):
        keys = loc[bass.ds(i * (2 * G) + u * G, G), :].rearrange("t p -> (t p)").partition_broadcast(P)
        sp.dma_start(rowb[:, u, :], keys).then_inc(loaded[u], 16)

    issue(0, 0)
    issue(0, 1)
    with sp.Fori(0, NG // 2 - 1) as i:
        for u in range(2):
            sp.wait_ge(used, i * 2 + u + 1)
            issue(i + 1, u)


def node_tile(eng, C, side, i, u):
    return eng.value_load(C.nt[side][0:1, bass.ds(i * 2 + u, 1)], min_val=0, max_val=NT - 1)


def one_hot(nc, C, side, out, i, u):
    keys = C.rec[side][:, bass.ds(i * (2 * G) + u * G, G), 1].unsqueeze(2).to_broadcast([P, G, P])
    return nc.vector.tensor_tensor(out, C.iota_row[:].unsqueeze(1).to_broadcast([P, G, P]), keys, ALU.is_equal)


def sum_pass(nc, C, name, side, table, acc, squares=False, weights=None):
    W = 2 * F if squares else F
    with Phase(nc, name) as ph:
        g = ph.sb("g", [P, 2, G, W])
        oh = ph.sb("oh", [P, 2, G, P])
        ring = ph.sb("ring", [P, 2, G], I32)
        ps = [ph.ps(f"ps{u}", [P, 512]) for u in range(2)]
        copied, oh_ready, raw_ready, acc_done, acc_set, squared = (
            ph.sem(x) for x in ("copied", "oh_ready", "raw_ready", "acc_done", "acc_set", "squared"))
        gathered = [ph.sem(f"gathered{u}") for u in range(2)]
        block = ph.block()

        @block.gpsimd
        def _(pool):
            gather_groups(nc, pool, C.rec[side], 0, ring, copied, table, lambda u, k: g[:, u, k, 0:F], gathered, acc_done)

        if squares:
            @block.scalar
            def _(act):
                with act.Fori(0, NG // 2) as i:
                    for u in range(2):
                        act.wait_ge(gathered[u], i * (16 * G) + 16 * G)
                        nc.scalar.activation(g[:, u, :, F:W], g[:, u, :, 0:F], ACT.Square).then_inc(squared, 1)

        @block.vector
        def _(dve):
            nc.vector.memset(acc[:], 0.0).then_inc(acc_set, 1)

            def build(i, u):
                if weights is None:
                    one_hot(nc, C, side, oh[:, u], i, u).then_inc(oh_ready, 1)
                    return
                one_hot(nc, C, side, oh[:, u], i, u).then_inc(raw_ready, 1)
                dve.wait_ge(raw_ready, i * 2 + u + 1)
                w = weights[:, bass.ds(i * (2 * G) + u * G, G)].unsqueeze(2).to_broadcast([P, G, P])
                nc.vector.tensor_tensor(oh[:, u], oh[:, u], w, ALU.mult).then_inc(oh_ready, 1)

            def add(i, u):
                nt = node_tile(dve, C, side, i, u)
                dve.wait_ge(acc_done, i * 2 + u + 1)
                dve.wait_ge(acc_set, i * 2 + u + 1)
                here = acc[:, bass.ds(nt, 1), :].squeeze(1)
                nc.vector.tensor_tensor(here, here, ps[u][:, 0:W], ALU.add).then_inc(acc_set, 1)

            build(0, 0)
            with dve.Fori(0, NG // 2 - 1) as i:
                build(i, 1)
                add(i, 0)
                build(i + 1, 0)
                add(i, 1)
            build(NG // 2 - 1, 1)
            add(NG // 2 - 1, 0)
            add(NG // 2 - 1, 1)

        @block.tensor
        def _(pe):
            with pe.Fori(0, NG // 2) as i:
                for u in range(2):
                    pe.wait_ge(oh_ready, i * 2 + u + 1)
                    pe.wait_ge(gathered[u], i * (16 * G) + 16 * G)
                    if squares:
                        pe.wait_ge(squared, i * 2 + u + 1)
                    for k in range(G):
                        last = nc.tensor.matmul(ps[u][:, 0:W], oh[:, u, k, :], g[:, u, k, :],
                                                start=(k == 0), stop=(k == G - 1))
                    last.then_inc(acc_done, 1)


def gat_pass(nc, C, name, table, H, strg, stp, acc, macc, negm):
    W = F + H
    with Phase(nc, name) as ph:
        g = ph.sb("g", [P, 2, G, W])
        msg = ph.sb("msg", [P, 2, G, W])
        oh = ph.sb("oh", [P, 2, G, P])
        oht = ph.sb("oht", [P, 2, GS])
        rowb = ph.sb("rowb", [P, 2, GS])
        ring = ph.sb("ring", [P, 2, G], I32)
        z = ph.sb("z", [P, 2, G, H])
        rm = ph.sb("rm", [P, 1])
        rrun = ph.sb("rrun", [P, 1])
        m1 = ph.sb("m1", [1, 1])
        nm = ph.sb("nm", [P, 2])
        f = ph.sb("f", [P, 2])
        ps = [ph.ps(f"ps{u}", [P, 512]) for u in range(2)]
        p_st = ph.ps("p_st", [P, 512])
        p_t = ph.ps("p_t", [P, P])
        p_m = ph.ps("p_m", [P, 1])
        names = ("copied oht_ready oh_ready chain strg_done max_ready turned m1_ready spread negm_ready ex_ready "
                 "f_ready macc_set msg_ready acc_done acc_set")
        (copied, oht_ready, oh_ready, chain, strg_done, max_ready, turned, m1_ready, spread, negm_ready, ex_ready,
         f_ready, macc_set, msg_ready, acc_done, acc_set) = (ph.sem(x) for x in names.split())
        gathered = [ph.sem(f"gathered{u}") for u in range(2)]
        rows_loaded = [ph.sem(f"rows_loaded{u}") for u in range(2)]
        block = ph.block()

        @block.gpsimd
        def _(pool):
            gather_groups(nc, pool, C.rec["D"], 0, ring, copied, table, lambda u, k: g[:, u, k, :], gathered, msg_ready)

        @block.sync
        def _(sp):
            load_key_rows(sp, C.loc["D"], rowb, rows_loaded, oht_ready)

        LINKS = 4

        @block.vector
        def _(dve):
            nc.vector.memset(macc[:], -BIG).then_inc(macc_set, 1)
            nc.vector.memset(rrun[:], -BIG)
            nc.vector.memset(acc[:], 0.0).then_inc(acc_set, 1)
            dve.wait_ge(acc_set, 1)
            with dve.Fori(0, NG // 2) as i:
                for u in range(2):
                    link = Chain(dve, chain, i * (2 * LINKS) + u * LINKS)
                    done = i * 2 + u + 1
                    nt = node_tile(dve, C, "D", i, u)
                    dve.wait_ge(rows_loaded[u], i * 16 + 16)
                    nc.vector.tensor_scalar(oht[:, u], rowb[:, u], C.iota_col[:], None, ALU.is_equal).then_inc(oht_ready, 1)
                    one_hot(nc, C, "D", oh[:, u], i, u).then_inc(oh_ready, 1)
                    dve.wait_ge(gathered[u], i * (16 * G) + 16 * G)
                    dve.wait_ge(strg_done, done)
                    link(nc.vector.tensor_tensor(z[:, u], g[:, u, :, F:W], p_st[:, 0:G * H].rearrange("p (g h) -> p g h", g=G),
                                                 ALU.add))
                    link(nc.vector.tensor_tensor(z[:, u], z[:, u], stp[:, bass.ds(i * (2 * G) + u * G, G), :], ALU.add))
                    link(nc.vector.scalar_tensor_tensor(z[:, u], z[:, u], 0.2, z[:, u], ALU.mult, ALU.max))
                    link(nc.vector.tensor_reduce(rm[:], z[:, u], AX.XY, ALU.max))
                    nc.vector.tensor_tensor(rrun[:], rrun[:], rm[:], ALU.max).then_inc(max_ready, 1)
                    dve.wait_ge(turned, done)
                    nc.vector.tensor_reduce(m1[:], p_t[0:1, :], AX.X, ALU.max).then_inc(m1_ready, 1)
                    dve.wait_ge(spread, done)
                    nc.vector.tensor_scalar(nm[:, u:u + 1], p_m[:], -1.0, None, ALU.mult).then_inc(negm_ready, 1)
                    dve.wait_ge(ex_ready, done)
                    D = F // H
                    nc.vector.tensor_tensor(msg[:, u, :, 0:F].rearrange("p g (h d) -> p g h d", h=H),
                                            g[:, u, :, 0:F].rearrange("p g (h d) -> p g h d", h=H),
                                            msg[:, u, :, F:W].unsqueeze(3).to_broadcast([P, G, H, D]),
                                            ALU.mult).then_inc(msg_ready, 1)
                    dve.wait_ge(acc_done, done)
                    dve.wait_ge(f_ready, done)
                    dve.wait_ge(acc_set, done)
                    here = acc[:, bass.ds(nt, 1), :].squeeze(1)
                    nc.vector.scalar_tensor_tensor(here, here, f[:, u:u + 1], ps[u][:, 0:W], ALU.mult, ALU.add).then_inc(acc_set, 1)
            dve.wait_ge(acc_set, NG + 1)
            nc.vector.tensor_copy(negm[:], nm[:, 1:2]).then_inc(acc_set, 1)

        @block.scalar
        def _(act):
            with act.Fori(0, NG // 2) as i:
                for u in range(2):
                    nt = node_tile(act, C, "D", i, u)
                    act.wait_ge(negm_ready, i * 2 + u + 1)
                    nc.scalar.activation(msg[:, u, :, F:W], z[:, u], ACT.Exp, bias=nm[:, u:u + 1]).then_inc(ex_ready, 1)
                    wait_apart(act, macc_set, i * 2 + u + 1)
                    here = macc[:, bass.ds(nt, 1)]
                    nc.scalar.activation(f[:, u:u + 1], here, ACT.Exp, bias=nm[:, u:u + 1]).then_inc(f_ready, 1)
                    wait_apart(act, f_ready, i * 2 + u + 1)
                    nc.scalar.mul(here, nm[:, u:u + 1], -1.0).then_inc(macc_set, 1)

        @block.tensor
        def _(pe):
            with pe.Fori(0, NG // 2) as i:
                for u in range(2):
                    done = i * 2 + u + 1
                    nt = node_tile(pe, C, "D", i, u)
                    pe.wait_ge(oht_ready, done)
                    for k in range(G):
                        last = nc.tensor.matmul(p_st[:, k * H:(k + 1) * H], oht[:, u, k * P:(k + 1) * P],
                                                strg[:, bass.ds(nt, 1), :].squeeze(1), start=True, stop=True)
                    last.then_inc(strg_done, 1)
                    pe.wait_ge(max_ready, done)
                    nc.tensor.transpose(p_t[0:1, :], rrun[:], C.ident[:]).then_inc(turned, 1)
                    pe.wait_ge(m1_ready, done)
                    nc.tensor.matmul(p_m[:], C.ones[0:1, :], m1[:], start=True, stop=True).then_inc(spread, 1)
                    pe.wait_ge(oh_ready, done)
                    pe.wait_ge(msg_ready, done)
                    for k in range(G):
                        last = nc.tensor.matmul(ps[u][:, 0:W], oh[:, u, k, :], msg[:, u, k, :],
                                                start=(k == 0), stop=(k == G - 1))
                    last.then_inc(acc_done, 1)


def attention_pass(nc, C, name, side, table, h, acc, m, first):
    W = F + 1
    with Phase(nc, name) as ph:
        g = ph.sb("g", [P, 2, G, W])
        oh = ph.sb("oh", [P, 2, G, P])
        oht = ph.sb("oht", [P, 2, GS])
        pen = ph.sb("pen", [P, GS])
        prod = ph.sb("prod", [P, G, F])
        diag = ph.sb("diag", [P, G, P])
        junk = ph.sb("junk", [P, GS])
        rowb = ph.sb("rowb", [P, 2, GS])
        ring = ph.sb("ring", [P, 2, G], I32)
        lg = ph.sb("lg", [P, G])
        keys = ph.sb("keys", [P, G])
        d = ph.sb("d", [P, 2, G])
        ex = ph.sb("ex", [P, 2, G])
        mt = ph.sb("mt", [P, 1])
        mn = ph.sb("mn", [P, 2])
        df = ph.sb("df", [P, 2])
        f = ph.sb("f", [P, 2])
        ps = [ph.ps(f"ps{u}", [P, 512]) for u in range(2)]
        p_x = ph.ps("p_x", [P, G, F])
        p_l = ph.ps("p_l", [P, GS])
        p_e = ph.ps("p_e", [P, G])
        names = ("copied oht_ready chain rows_done diag_ready spread m_ready m_done d_ready f_ready ex_ready "
                 "oh_ready acc_done acc_set")
        (copied, oht_ready, chain, rows_done, diag_ready, spread, m_ready, m_done, d_ready, f_ready, ex_ready,
         oh_ready, acc_done, acc_set) = (ph.sem(x) for x in names.split())
        gathered = [ph.sem(f"gathered{u}") for u in range(2)]
        rows_loaded = [ph.sem(f"rows_loaded{u}") for u in range(2)]
        block = ph.block()
        LINKS = 9

        @block.gpsimd
        def _(pool):
            gather_groups(nc, pool, C.rec[side], 4, ring, copied, table, lambda u, k: g[:, u, k, 0:F], gathered, acc_done)

        @block.sync
        def _(sp):
            load_key_rows(sp, C.loc[side], rowb, rows_loaded, d_ready)

        @block.vector
        def _(dve):
            nc.vector.memset(g[:, :, :, F:W], 1.0)
            if first:
                nc.vector.memset(m[:], -BIG)
                nc.vector.memset(acc[:], 0.0).then_inc(acc_set, 1)
            else:
                nc.vector.memset(pen[:], 0.0).then_inc(acc_set, 1)
            dve.wait_ge(acc_set, 1)
            with dve.Fori(0, NG // 2) as i:
                for u in range(2):
                    link = Chain(dve, chain, i * (2 * LINKS) + u * LINKS)
                    done = i * 2 + u + 1
                    nt = node_tile(dve, C, side, i, u)
                    dve.wait_ge(rows_loaded[u], i * 16 + 16)
                    nc.vector.tensor_scalar(oht[:, u], rowb[:, u], C.iota_col[:], None, ALU.is_equal).then_inc(oht_ready, 1)
                    nc.vector.tensor_scalar(pen[:], rowb[:, u], C.iota_col[:], -BIG, ALU.not_equal, ALU.mult)
                    link(nc.vector.tensor_copy(keys[:], C.rec[side][:, bass.ds(i * (2 * G) + u * G, G), 1]))
                    dve.wait_ge(gathered[u], i * (16 * G) + 16 * G)
                    dve.wait_ge(rows_done, done)
                    link(nc.vector.tensor_tensor(prod[:], g[:, u, :, 0:F], p_x[:], ALU.mult))
                    link(nc.vector.tensor_reduce(lg[:], prod[:], AX.X, ALU.add))
                    link(nc.vector.tensor_scalar(lg[:], lg[:], float(F) ** -0.5, None, ALU.mult))
                    nc.vector.tensor_tensor(diag[:], C.ident[:].unsqueeze(1).to_broadcast([P, G, P]),
                                            lg[:].unsqueeze(2).to_broadcast([P, G, P]), ALU.mult).then_inc(diag_ready, 1)
                    dve.wait_ge(spread, done)
                    link(nc.vector.tensor_tensor(junk[:], p_l[:], pen[:], ALU.add))
                    link(nc.vector.tensor_reduce(mt[:], junk[:], AX.X, ALU.max))
                    here = m[:, bass.ds(nt, 1)]
                    nc.vector.tensor_tensor(mn[:, u:u + 1], here, mt[:], ALU.max).then_inc(m_ready, 1)
                    dve.wait_ge(m_ready, done)
                    link(nc.vector.tensor_tensor(df[:, u:u + 1], here, mn[:, u:u + 1], ALU.subtract))
                    link(nc.vector.tensor_tensor(here, here, mt[:], ALU.max))
                    dve.wait_ge(m_done, done)
                    link(nc.vector.tensor_tensor(d[:, u], lg[:], p_e[:], ALU.subtract))
                    nc.vector.tensor_scalar(d[:, u], d[:, u], 0.0, None, ALU.min).then_inc(d_ready, 1)
                    dve.wait_ge(ex_ready, done)
                    for k in range(G):
                        last = nc.vector.tensor_scalar(oh[:, u, k, :], C.iota_row[:], keys[:, k:k + 1], ex[:, u, k:k + 1],
                                                       ALU.is_equal, ALU.mult)
                    last.then_inc(oh_ready, 1)
                    dve.wait_ge(acc_done, done)
                    dve.wait_ge(f_ready, done)
                    dve.wait_ge(acc_set, done)
                    here = acc[:, bass.ds(nt, 1), :].squeeze(1)
                    nc.vector.scalar_tensor_tensor(here, here, f[:, u:u + 1], ps[u][:, 0:W], ALU.mult, ALU.add).then_inc(acc_set, 1)

        @block.scalar
        def _(act):
            with act.Fori(0, NG // 2) as i:
                for u in range(2):
                    act.wait_ge(d_ready, i * 2 + u + 1)
                    nc.scalar.activation(ex[:, u], d[:, u], ACT.Exp).then_inc(ex_ready, 1)
                    nc.scalar.activation(f[:, u:u + 1], df[:, u:u + 1], ACT.Exp).then_inc(f_ready, 1)

        @block.tensor
        def _(pe):
            with pe.Fori(0, NG // 2) as i:
                for u in range(2):
                    done = i * 2 + u + 1
                    nt = node_tile(pe, C, side, i, u)
                    pe.wait_ge(oht_ready, done)
                    for k in range(G):
                        last = nc.tensor.matmul(p_x[:, k, :], oht[:, u, k * P:(k + 1) * P],
                                                h[:, bass.ds(nt, 1), :].squeeze(1), start=True, stop=True)
                    last.then_inc(rows_done, 1)
                    pe.wait_ge(diag_ready, done)
                    nc.tensor.matmul(p_l[:], C.ones[:], diag[:].rearrange("p g n -> p (g n)"), start=True,
                                     stop=True).then_inc(spread, 1)
                    pe.wait_ge(m_ready, done)
                    for k in range(G):
                        last = nc.tensor.matmul(p_e[:, k:k + 1], oht[:, u, k * P:(k + 1) * P], mn[:, u:u + 1],
                                                start=True, stop=True)
                    last.then_inc(m_done, 1)
                    pe.wait_ge(oh_ready, done)
                    for k in range(G):
                        last = nc.tensor.matmul(ps[u][:, 0:W], oh[:, u, k, :], g[:, u, k, :],
                                                start=(k == 0), stop=(k == G - 1))
                    last.then_inc(acc_done, 1)


def linear(nc, C, name, parts, M, finish):
    with Phase(nc, name) as ph:
        K = len(parts)
        xs = ph.sb("xs", [P, K, NB, F])
        xt = ph.sb("xt", [P, K, NB, P])
        p_t = [ph.ps(f"p_t{q}", [P, 8, P]) for q in range(min(K, 2))]
        p_y = ph.ps("p_y", [P, 8, 256])
        staged, turned, xt_ready, multiplied, finished = (
            ph.sem(x) for x in ("staged", "turned", "xt_ready", "multiplied", "finished"))
        block = ph.block()

        @block.vector
        def _(dve):
            with dve.Fori(0, NT // NB) as i:
                for q, (x, _) in enumerate(parts):
                    nc.vector.tensor_copy(xs[:, q], x[:, bass.ds(i * NB, NB), :]).then_inc(staged, 1)
                wait_apart(dve, multiplied, i + 1)
                finish(i, p_y[:, 0:NB, 0:M]).then_inc(finished, 1)

        @block.scalar
        def _(act):
            with act.Fori(0, NT // NB) as i:
                for q in range(K):
                    act.wait_ge(turned, i * K + q + 1)
                    nc.scalar.copy(xt[:, q], p_t[q % 2][:, 0:NB, :]).then_inc(xt_ready, 1)

        @block.tensor
        def _(pe):
            with pe.Fori(0, NT // NB) as i:
                for q in range(K):
                    pe.wait_ge(staged, i * K + q + 1)
                    if q >= 2:
                        pe.wait_ge(xt_ready, i * K + q - 1)
                    for k in range(NB):
                        last = nc.tensor.transpose(p_t[q % 2][:, k, :], xs[:, q, k, :], C.ident[:])
                    last.then_inc(turned, 1)
                pe.wait_ge(xt_ready, i * K + K)
                for k in range(NB):
                    for q, (_, w) in enumerate(parts):
                        last = nc.tensor.matmul(p_y[:, k, 0:M], xt[:, q, k, :], w, start=(q == 0), stop=(q == K - 1))
                last.then_inc(multiplied, 1)


def per_node(v):
    return v.unsqueeze(2).to_broadcast([P, NT, F])


def per_feature(v):
    return v.unsqueeze(1).to_broadcast([P, NT, F])


class Vector:

    def __init__(self, nc, dve, sem):
        self.v, self.link = nc.vector, Chain(dve, sem)

    def tt(self, out, a, b, op):
        self.link(self.v.tensor_tensor(out, a, b, op))

    def ts(self, out, a, s1, op0, s2=None, op1=ALU.bypass):
        if s2 is None:
            self.link(self.v.tensor_scalar(out, a, s1, None, op0))
        else:
            self.link(self.v.tensor_scalar(out, a, s1, s2, op0, op1))

    def stt(self, out, a, s, b, op0, op1):
        self.link(self.v.scalar_tensor_tensor(out, a, s, b, op0, op1))

    def inverse_root(self, v, root, tmp):
        self.link(self.v.reciprocal(root, root))
        self.tt(tmp, root, root, ALU.mult)
        self.tt(tmp, tmp, v, ALU.mult)
        self.ts(tmp, tmp, -0.5, ALU.mult, 1.5, ALU.add)
        self.tt(root, root, tmp, ALU.mult)

    def sum(self, out, a):
        self.link(self.v.tensor_reduce(out, a, AX.X, ALU.add))


def roots(nc, act, v, root, asked, rooted, times=1):
    for k in range(times):
        act.wait_ge(asked, k + 1)
        nc.scalar.activation(root, v, ACT.Sqrt).then_inc(rooted, 1)


def normalized_relu(V, dve, x, h, tmp, stat, to_root, rooted):
    V.sum(stat[:, 0], x[:])
    V.ts(stat[:, 0], stat[:, 0], 1.0 / F, ALU.mult)
    V.tt(h[:], x[:], per_node(stat[:, 0]), ALU.subtract)
    V.tt(tmp[:], h[:], h[:], ALU.mult)
    V.sum(stat[:, 1], tmp[:])
    V.v.tensor_scalar(stat[:, 1], stat[:, 1], 1.0 / F, EPS, ALU.mult, ALU.add).then_inc(to_root, 1)
    dve.wait_ge(rooted, 1)
    V.inverse_root(stat[:, 1], stat[:, 0], stat[:, 2])
    V.stt(h[:], h[:], 0.0, per_node(stat[:, 0]), ALU.max, ALU.mult)


def save_table(nc, C, name, rows, table):
    with Phase(nc, name) as ph:
        stored = ph.sem("stored")
        block = ph.block()

        @block.sync
        def _(sp):
            sp.dma_start(table.rearrange("(t p) w -> p t w", p=P), rows).then_inc(stored, 16)
            sp.wait_ge(stored, 16)


def gat_layer(nc, C, name, a, W, Wt, asrc, atrg, atp, b, Wskip, H, x, h, table, last_x=None):
    D, WD = F // H, F + H
    with Phase(nc, name) as top:
        tab = top.sb("tab", [P, NT, WD])
        skip = top.sb("skip", [P, NT, F]) if Wskip is not None else h
        acc = top.sb("acc", [P, NT, WD])
        strg = top.sb("strg", [P, NT, H])
        stp = top.sb("stp", [P, T, H])
        macc = top.sb("macc", [P, NT])
        negm = top.sb("negm", [P, 1])
        rows = top.sb("rows", [P, 5, F])
        M = 2 * F if Wskip is not None else F
        w = top.sb("w", [P, M])
        ch = top.sb("ch", [P, H])
        pen = top.sb("pen", [P, T])
        with Phase(nc, name + "a") as ph:
            tmp = ph.sb("tmp", [P, F])
            loaded, chain = ph.sem("loaded"), ph.sem("chain")
            block = ph.block()

            @block.sync
            def _(sp):
                sp.dma_start(w[:, 0:F], W).then_inc(loaded, 16)
                if Wskip is not None:
                    sp.dma_start(w[:, F:M], Wskip).then_inc(loaded, 16)
                for k, v in enumerate((Wt, asrc, atrg, atp, b)):
                    sp.dma_start(rows[:, k, :], v.partition_broadcast(P)).then_inc(loaded, 16)

            @block.vector
            def _(dve):
                V = Vector(nc, dve, chain)
                dve.wait_ge(loaded, 16 * (6 + (Wskip is not None)))
                V.tt(tmp[:], rows[:, 0, :], rows[:, 3, :], ALU.mult)
                V.sum(ch[:], tmp[:].rearrange("p (h d) -> p h d", h=H))
                V.ts(pen[:], C.rec["D"][:, :, 1], 0.0, ALU.is_lt, -BIG, ALU.mult)
                V.tt(stp[:], C.rec["D"][:, :, 2].unsqueeze(2).to_broadcast([P, T, H]),
                     ch[:].unsqueeze(1).to_broadcast([P, T, H]), ALU.mult)
                V.tt(stp[:], stp[:], pen[:].unsqueeze(2).to_broadcast([P, T, H]), ALU.add)

        def finish(i, y):
            if Wskip is not None:
                nc.vector.tensor_copy(skip[:, bass.ds(i * NB, NB), :], y[:, :, F:M])
            return nc.vector.tensor_copy(tab[:, bass.ds(i * NB, NB), 0:F], y[:, :, 0:F])

        linear(nc, C, name + "l", [(h, w[:])], M, finish)
        with Phase(nc, name + "b") as ph:
            tmp = ph.sb("tmp", [P, NT, F])
            chain = ph.sem("chain")
            block = ph.block()

            @block.vector
            def _(dve):
                V = Vector(nc, dve, chain)
                for k, to in ((1, tab[:, :, F:WD]), (2, strg[:])):
                    V.tt(tmp[:], tab[:, :, 0:F], per_feature(rows[:, k, :]), ALU.mult)
                    V.sum(to, tmp[:].rearrange("p t (h d) -> p t h d", h=H))
        save_table(nc, C, name + "s", tab[:], table)
        gat_pass(nc, C, name + "p", table, H, strg, stp, acc, macc, negm)
        with Phase(nc, name + "c") as ph:
            fac = ph.sb("fac", [P, NT])
            den = ph.sb("den", [P, NT, H])
            low = ph.sb("low", [P, NT, F])
            chain, asked, given = ph.sem("chain"), ph.sem("asked"), ph.sem("given")
            block = ph.block()

            @block.scalar
            def _(act):
                nc.scalar.activation(fac[:], macc[:], ACT.Exp, bias=negm[:]).then_inc(given, 1)
                act.wait_ge(asked, 1)
                nc.scalar.activation(low[:], low[:], ACT.Exp).then_inc(given, 1)

            @block.vector
            def _(dve):
                V = Vector(nc, dve, chain)
                dve.wait_ge(given, 1)
                bc = fac[:].unsqueeze(2).to_broadcast([P, NT, H])
                V.tt(den[:], acc[:, :, F:WD], bc, ALU.mult)
                V.ts(den[:], den[:], 1e-16, ALU.add)
                V.link(nc.vector.reciprocal(den[:], den[:]))
                V.tt(den[:], den[:], bc, ALU.mult)
                y = tab[:, :, 0:F]
                V.tt(y.rearrange("p t (h d) -> p t h d", h=H), acc[:, :, 0:F].rearrange("p t (h d) -> p t h d", h=H),
                     den[:].unsqueeze(3).to_broadcast([P, NT, H, D]), ALU.mult)
                V.tt(y, y, skip[:], ALU.add)
                V.tt(y, y, per_feature(rows[:, 4, :]), ALU.add)
                nc.vector.tensor_scalar(low[:], y, 0.0, None, ALU.min).then_inc(asked, 1)
                dve.wait_ge(given, 2)
                V.stt(h[:], y, 0.0, low[:], ALU.max, ALU.add)
                V.ts(h[:], h[:], -1.0, ALU.add)
                if last_x is not None:
                    V.tt(last_x[:], last_x[:], h[:], ALU.add)


def norm_phase(nc, C, name, x, h):
    with Phase(nc, name) as ph:
        tmp = ph.sb("tmp", [P, NT, F])
        stat = ph.sb("stat", [P, 3, NT])
        chain, to_root, rooted = ph.sem("chain"), ph.sem("to_root"), ph.sem("rooted")
        block = ph.block()

        @block.scalar
        def _(act):
            roots(nc, act, stat[:, 1], stat[:, 0], to_root, rooted)

        @block.vector
        def _(dve):
            normalized_relu(Vector(nc, dve, chain), dve, x, h, tmp, stat, to_root, rooted)


def gcn_layers(nc, C, name, a, x, h, table):
    L = 3
    with Phase(nc, name) as top:
        xc = [h] + [top.sb(f"xc{i}", [P, NT, F]) for i in range(1, L + 1)]
        ws = top.sb("ws", [P, L, F])
        bs = top.sb("bs", [P, L + 1, F])
        wout = top.sb("wout", [P, L + 1, F])
        gb = top.sb("gb", [P, 2, (L + 1), F])
        dinv = top.sb("dinv", [P, NT])
        ocnt = top.sb("ocnt", [P, NT])
        real = top.sb("real", [P, NT])
        with Phase(nc, name + "a") as ph:
            deg = ph.sb("deg", [P, 2, NT])
            loaded, chain, to_root, rooted = (ph.sem(v) for v in ("loaded", "chain", "to_root", "rooted"))
            block = ph.block()

            @block.scalar
            def _(act):
                roots(nc, act, deg[:, 0], dinv[:], to_root, rooted)

            @block.sync
            def _(sp):
                sp.dma_start(ws[:], a["L1_gnn_Ws"].rearrange("l k m -> k l m")).then_inc(loaded, 16)
                sp.dma_start(wout[:], a["L1_gnn_Wout"].rearrange("(l k) m -> k l m", k=P)).then_inc(loaded, 16)
                sp.dma_start(bs[:, 0:L, :], a["L1_gnn_bs"].partition_broadcast(P)).then_inc(loaded, 16)
                sp.dma_start(bs[:, L, :], a["L1_gnn_bout"].partition_broadcast(P)).then_inc(loaded, 16)
                for k, v in enumerate(("bn_gamma", "bn_beta")):
                    sp.dma_start(gb[:, k], a["L1_gnn_" + v].rearrange("(l f) -> l f", f=F).partition_broadcast(P)).then_inc(loaded, 16)
                sp.wait_ge(loaded, 96)

            @block.vector
            def _(dve):
                V = Vector(nc, dve, chain)
                nc.vector.tensor_scalar(deg[:, 0], C.cnt["D"][:], 1.0, None, ALU.add).then_inc(to_root, 1)
                dve.wait_ge(rooted, 1)
                V.inverse_root(deg[:, 0], dinv[:], deg[:, 1])
                V.ts(ocnt[:], C.cnt["S"][:], 1.0, ALU.max)
                V.link(nc.vector.reciprocal(ocnt[:], ocnt[:]))
                V.link(nc.vector.memset(real[:], 1.0))
                V.ts(real[:, NT - 1:NT], C.iota_col[:], float(LAST), ALU.is_lt)
        for l in range(L):
            with Phase(nc, f"{name}{l}") as lay:
                hd = lay.sb("hd", [P, NT, F])
                tau = lay.sb("tau", [P, NT, F])

                def finish(i, y):
                    d = dinv[:, bass.ds(i * NB, NB)].unsqueeze(2).to_broadcast([P, NB, F])
                    return nc.vector.tensor_tensor(hd[:, bass.ds(i * NB, NB), :], y, d, ALU.mult)

                linear(nc, C, f"{name}{l}l", [(xc[l], ws[:, l, :])], F, finish)
                save_table(nc, C, f"{name}{l}s", hd[:], table)
                sum_pass(nc, C, f"{name}{l}d", "D", table, tau)
                with Phase(nc, f"{name}{l}b") as ph:
                    chain = ph.sem("chain")
                    block = ph.block()

                    @block.vector
                    def _(dve):
                        V = Vector(nc, dve, chain)
                        V.tt(tau[:], tau[:], hd[:], ALU.add)
                        V.tt(tau[:], tau[:], per_node(dinv[:]), ALU.mult)
                        V.tt(tau[:], tau[:], per_feature(bs[:, l, :]), ALU.add)
                        V.ts(tau[:], tau[:], 0.0, ALU.max)
                save_table(nc, C, f"{name}{l}t", tau[:], table)
                with Phase(nc, f"{name}{l}g") as ph2:
                    acc = ph2.sb("acc", [P, NT, 2 * F])
                    sum_pass(nc, C, f"{name}{l}e", "S", table, acc, squares=True)
                    with Phase(nc, f"{name}{l}c") as ph:
                        chain, asked, given = ph.sem("chain"), ph.sem("asked"), ph.sem("given")
                        block = ph.block()

                        @block.scalar
                        def _(act):
                            act.wait_ge(asked, 1)
                            nc.scalar.activation(hd[:], hd[:], ACT.Tanh).then_inc(given, 1)

                        @block.vector
                        def _(dve):
                            V = Vector(nc, dve, chain)
                            V.tt(hd[:], tau[:], per_node(C.cnt["S"][:]), ALU.mult)
                            V.stt(hd[:], acc[:, :, 0:F], -2.0, hd[:], ALU.mult, ALU.add)
                            V.tt(hd[:], hd[:], tau[:], ALU.mult)
                            V.tt(hd[:], hd[:], acc[:, :, F:2 * F], ALU.add)
                            nc.vector.tensor_tensor(hd[:], hd[:], per_node(ocnt[:]), ALU.mult).then_inc(asked, 1)
                            dve.wait_ge(given, 1)
                            V.tt(tau[:], tau[:], xc[l][:], ALU.subtract)
                            V.tt(tau[:], tau[:], hd[:], ALU.mult)
                            V.tt(tau[:], tau[:], xc[l][:], ALU.add)
                            V.tt(xc[l + 1][:], tau[:], per_node(real[:]), ALU.mult)
        with Phase(nc, name + "n") as ph:
            tmp = ph.sb("tmp", [P, NT, F])
            part = ph.sb("part", [P, 2 * (L + 1), F])
            stat = ph.sb("stat", [P, F])
            var = ph.sb("var", [P, 2, F])
            p_s = ph.ps("p_s", [P, F])
            chain, asked, given, to_root, rooted = (ph.sem(v) for v in ("chain", "asked", "given", "to_root", "rooted"))
            block = ph.block()

            @block.scalar
            def _(act):
                roots(nc, act, var[:, 0], stat[:], to_root, rooted, L + 1)

            @block.vector
            def _(dve):
                V = Vector(nc, dve, chain)
                V.tt(h[:], h[:], per_node(real[:]), ALU.mult)
                for q in range(L + 1):
                    y = xc[q]
                    for s in range(2):
                        src = y if s == 0 else tmp
                        nc.vector.tensor_reduce(part[:, 2 * q + s, :], src[:].rearrange("p t f -> p f t"), AX.X,
                                                ALU.add).then_inc(asked, 1)
                        dve.wait_ge(given, 2 * q + s + 1)
                        if s == 0:
                            V.ts(stat[:], p_s[:], 1.0 / N, ALU.mult)
                            V.tt(y[:], y[:], per_feature(stat[:]), ALU.subtract)
                            V.tt(y[:], y[:], per_node(real[:]), ALU.mult)
                            V.tt(tmp[:], y[:], y[:], ALU.mult)
                        else:
                            nc.vector.tensor_scalar(var[:, 0], p_s[:], 1.0 / N, EPS, ALU.mult, ALU.add).then_inc(to_root, 1)
                            dve.wait_ge(rooted, q + 1)
                            V.inverse_root(var[:, 0], stat[:], var[:, 1])
                            V.tt(stat[:], stat[:], gb[:, 0, q, :], ALU.mult)
                            V.tt(y[:], y[:], per_feature(stat[:]), ALU.mult)
                            V.tt(y[:], y[:], per_feature(gb[:, 1, q, :]), ALU.add)

            @block.tensor
            def _(pe):
                for k in range(2 * (L + 1)):
                    pe.wait_ge(asked, k + 1)
                    nc.tensor.matmul(p_s[:], C.ones[:], part[:, k, :], start=True, stop=True).then_inc(given, 1)

        with Phase(nc, name + "o") as ph:
            y1 = ph.sb("y1", [P, NB, F])
            added = ph.sem("added")

            def finish(i, y):
                nc.vector.tensor_tensor(y1[:], y, bs[:, L, :].unsqueeze(1).to_broadcast([P, NB, F]), ALU.add).then_inc(added, 1)
                nc.vector.wait_ge(added, i + 1)
                at = x[:, bass.ds(i * NB, NB), :]
                return nc.vector.tensor_tensor(at, at, y1[:], ALU.add)

            linear(nc, C, name + "l", [(xc[q], wout[:, q, :]) for q in range(L + 1)], F, finish)


def attention_layer(nc, C, name, a, x, h):
    table = a["edge_attr_256"].rearrange("e (s f) -> (e s) f", s=2)
    with Phase(nc, name) as top:
        acc = top.sb("acc", [P, NT, F + 1])
        agg = top.sb("agg", [P, NT, F])
        m = top.sb("m", [P, NT])
        w = top.sb("w", [P, 2, F])
        b = top.sb("b", [P, F])
        attention_pass(nc, C, name + "d", "D", table, h, acc, m, True)
        attention_pass(nc, C, name + "s", "S", table, h, acc, m, False)
        with Phase(nc, name + "a") as ph:
            den = ph.sb("den", [P, NT])
            loaded, chain = ph.sem("loaded"), ph.sem("chain")
            block = ph.block()

            @block.sync
            def _(sp):
                sp.dma_start(w[:], a["L2_gnn_W"].rearrange("(l k) m -> k l m", k=P)).then_inc(loaded, 16)
                sp.dma_start(b[:], a["L2_gnn_b"].partition_broadcast(P)).then_inc(loaded, 16)
                sp.wait_ge(loaded, 32)

            @block.vector
            def _(dve):
                V = Vector(nc, dve, chain)
                V.ts(den[:], acc[:, :, F], 1e-30, ALU.max)
                V.link(nc.vector.reciprocal(den[:], den[:]))
                V.tt(agg[:], acc[:, :, 0:F], per_node(den[:]), ALU.mult)

        with Phase(nc, name + "o") as ph:
            y1 = ph.sb("y1", [P, NB, F])
            added = ph.sem("added")

            def finish(i, y):
                nc.vector.tensor_tensor(y1[:], y, b[:].unsqueeze(1).to_broadcast([P, NB, F]), ALU.add).then_inc(added, 1)
                nc.vector.wait_ge(added, i + 1)
                at = x[:, bass.ds(i * NB, NB), :]
                return nc.vector.tensor_tensor(at, at, y1[:], ALU.add)

            linear(nc, C, name + "l", [(agg, w[:, 0, :]), (h, w[:, 1, :])], F, finish)


def filter_layer(nc, C, name, a, x, h, table):
    with Phase(nc, name) as top:
        agg = top.sb("agg", [P, NT, F])
        wt = top.sb("wt", [P, T])
        w = top.sb("w", [P, F])
        save_table(nc, C, name + "s", h[:], table)
        with Phase(nc, name + "a") as ph:
            sc = ph.sb("sc", [P, 4])
            v = ph.sb("v", [P, 3, T])
            ok = ph.sb("ok", [P, T])
            oki = ph.sb("oki", [P, T], dt.uint32)
            loaded, chain, asked, given = (ph.sem(x) for x in ("loaded", "chain", "asked", "given"))
            block = ph.block()

            @block.sync
            def _(sp):
                for k, n in enumerate(("log_scale", "filter_w", "filter_b")):
                    sp.dma_start(sc[:, k:k + 1], a["L3_gnn_" + n].partition_broadcast(P)).then_inc(loaded, 16)
                sp.dma_start(w[:], a["L3_gnn_W_mix"]).then_inc(loaded, 16)
                sp.wait_ge(loaded, 64)

            @block.scalar
            def _(act):
                act.wait_ge(loaded, 64)
                nc.scalar.activation(sc[:, 3:4], sc[:, 0:1], ACT.Exp).then_inc(given, 1)
                act.wait_ge(asked, 1)
                nc.scalar.activation(v[:, 0], v[:, 0], ACT.Exp, scale=-1.0).then_inc(given, 1)
                act.wait_ge(asked, 2)
                nc.scalar.activation(v[:, 1], v[:, 1], ACT.Exp, scale=-1.0).then_inc(given, 1)

            @block.vector
            def _(dve):
                V = Vector(nc, dve, chain)
                dve.wait_ge(loaded, 64)
                dve.wait_ge(given, 1)
                length = C.rec["D"][:, :, 3]
                V.ts(sc[:, 3:4], sc[:, 3:4], 1e-6, ALU.add)
                V.link(nc.vector.reciprocal(sc[:, 3:4], sc[:, 3:4]))
                V.ts(v[:, 2], length, sc[:, 3:4], ALU.mult, 0.0, ALU.max)
                nc.vector.tensor_tensor(v[:, 0], v[:, 2], v[:, 2], ALU.mult).then_inc(asked, 1)
                nc.vector.tensor_scalar(v[:, 1], length, sc[:, 1:2], sc[:, 2:3], ALU.mult, ALU.add).then_inc(asked, 1)
                dve.wait_ge(given, 3)
                V.ts(v[:, 1], v[:, 1], 1.0, ALU.add)
                V.link(nc.vector.reciprocal(v[:, 1], v[:, 1]))
                V.tt(v[:, 0], v[:, 0], v[:, 1], ALU.mult)
                V.ts(ok[:], v[:, 0], 3.4e38, ALU.is_le)
                V.ts(v[:, 1], v[:, 0], -3.4e38, ALU.is_ge)
                V.tt(oki[:], ok[:], v[:, 1], ALU.mult)
                V.link(nc.vector.memset(wt[:], 0.0))
                V.link(nc.vector.copy_predicated(wt[:], oki[:], v[:, 0]))

        sum_pass(nc, C, name + "d", "D", table, agg, weights=wt)
        with Phase(nc, name + "b") as ph:
            deg = ph.sb("deg", [P, NT])
            chain = ph.sem("chain")
            block = ph.block()

            @block.vector
            def _(dve):
                V = Vector(nc, dve, chain)
                V.ts(deg[:], C.cnt["D"][:], 1.0, ALU.max)
                V.link(nc.vector.reciprocal(deg[:], deg[:]))
                V.tt(agg[:], agg[:], per_node(deg[:]), ALU.mult)
                V.tt(x[:], x[:], h[:], ALU.add)

        def finish(i, y):
            at = x[:, bass.ds(i * NB, NB), :]
            return nc.vector.tensor_tensor(at, at, y, ALU.add)

        linear(nc, C, name + "l", [(agg, w[:])], F, finish)


class Shared:
    pass


def program(nc, a, out, upto=99):
    ctx = ExitStack()
    with ctx:
        def sb(name, shape, d=F32):
            return ctx.enter_context(nc.sbuf_tensor(name, shape, d))

        C = Shared()
        C.iota_row = sb("iota_row", [P, P])
        C.iota_col = sb("iota_col", [P, 1])
        C.ident = sb("ident", [P, P])
        C.ones = sb("ones", [P, P])
        C.before = sb("before", [P, P])
        C.zerosb = sb("zerosb", [P, P], BF16)
        PASSED[:] = [nc.alloc_semaphore("passed")]
        constants(nc, C)
        C.rec, C.nt, C.cnt, C.loc = {}, {}, {}, {}
        for s, key, other, row in (("D", "dst", "src", 0), ("S", "src", "dst", 1)):
            C.rec[s] = sb(f"rec{s}", [P, T, RW])
            C.nt[s] = sb(f"nt{s}", [P, NG], I32)
            C.cnt[s] = sb(f"cnt{s}", [P, NT])
            C.loc[s] = nc.dram_tensor(f"loc{s}", [T, P], F32).ap()
            recd = nc.dram_tensor(f"recd{s}", [SLOTS, RW], F32).ap()
            sort_edges(nc, C, f"sort{s}", a[key], a[other], row, a["edge_weight1"], a["edge_weight"], C.rec[s], C.nt[s],
                       C.cnt[s], C.loc[s], recd)
        x = sb("x_now", [P, NT, F])
        h = sb("h_now", [P, NT, F])
        t136 = nc.dram_tensor("table_heads", [NP, F + 8], F32).ap()
        t129 = nc.dram_tensor("table_head", [NP, F + 1], F32).ap()
        table = nc.dram_tensor("table", [NP, F], F32).ap()
        with Phase(nc, "in") as ph:
            loaded, cleared = ph.sem("loaded"), ph.sem("cleared")
            block = ph.block()

            @block.vector
            def _(dve):
                nc.vector.memset(x[:, NT - 1, :], 0.0).then_inc(cleared, 1)

            @block.sync
            def _(sp):
                sp.wait_ge(cleared, 1)
                whole = (NT - 1) * P
                sp.dma_start(x[:, 0:NT - 1, :], a["x"][0:whole, :].rearrange("(t p) f -> p t f", p=P)).then_inc(loaded, 16)
                sp.dma_start(x[0:LAST, NT - 1, :], a["x"][whole:N, :]).then_inc(loaded, 16)
                sp.wait_ge(loaded, 32)

        clear_semaphores(nc)
        norm_phase(nc, C, "ln0", x, h)
        g = lambda n: a["L0_gnn_" + n]
        if upto >= 2:
            gat_layer(nc, C, "gatA", a, g("W1"), g("Wt1"), g("a_src1"), g("a_trg1"), g("a_tp1"), g("b1"), g("Wskip1"), 8, x, h, t136)
            clear_semaphores(nc)
        if upto >= 3:
            gat_layer(nc, C, "gatB", a, g("W2"), g("Wt2"), g("a_src2"), g("a_trg2"), g("a_tp2"), g("b2"), None, 1, x, h, t129, x)
            clear_semaphores(nc)
            norm_phase(nc, C, "ln1", x, h)
        if upto >= 4:
            gcn_layers(nc, C, "gcn", a, x, h, table)
            clear_semaphores(nc)
            norm_phase(nc, C, "ln2", x, h)
        if upto >= 5:
            attention_layer(nc, C, "att", a, x, h)
            clear_semaphores(nc)
            norm_phase(nc, C, "ln3", x, h)
        if upto >= 6:
            filter_layer(nc, C, "fil", a, x, h, table)
        with Phase(nc, "out") as ph:
            stored = ph.sem("stored")
            block = ph.block()

            @block.sync
            def _(sp):
                whole = (NT - 1) * P
                sp.dma_start(out[0:whole, :].rearrange("(t p) f -> p t f", p=P), x[:, 0:NT - 1, :]).then_inc(stored, 16)
                sp.dma_start(out[whole:N, :], x[0:LAST, NT - 1, :]).then_inc(stored, 16)
                if upto < 6:
                    sp.dma_start(a["o_h"].rearrange("(t p) f -> p t f", p=P), h[:]).then_inc(stored, 16)
                sp.wait_ge(stored, 32 if upto >= 6 else 48)


_FLAT = ("edge_weight1", "L0_gnn_Wt1", "L0_gnn_a_src1", "L0_gnn_a_trg1", "L0_gnn_a_tp1", "L0_gnn_Wt2", "L0_gnn_a_src2",
         "L0_gnn_a_trg2", "L0_gnn_a_tp2", "L3_gnn_log_scale", "L3_gnn_filter_w", "L3_gnn_filter_b")


def kernel(**inputs):
    import numpy as _np
    import concourse.bacc as _bacc
    from concourse import mybir as _mybir
    from concourse.bass_utils import run_bass_kernel_spmd as _run

    nc = _bacc.Bacc("TRN2", target_bir_lowering=False, num_devices=1)
    arrays, aps = {}, {}
    for name, value in inputs.items():
        v = _np.ascontiguousarray(value)
        if name in _FLAT:
            v = v.reshape(-1)
        arrays[f"in_{name}"] = v
        aps[name] = nc.dram_tensor(f"in_{name}", v.shape, _mybir.dt.from_np(v.dtype), kind="ExternalInput").ap()
    out = nc.dram_tensor("out_x", (N, F), F32, kind="ExternalOutput").ap()
    program(nc, aps, out)
    r = _run(nc, [arrays], core_ids=[0])
    return r.results[0]["out_x"]
```

```python
import concourse.bass as bass
from concourse import mybir
from contextlib import ExitStack

dt = mybir.dt
F32, I32, BF16 = dt.float32, dt.int32, dt.bfloat16
ALU = mybir.AluOpType
ACT = mybir.ActivationFunctionType
AX = mybir.AxisListType

P = 128
N, E, F = 3125, 50000, 128
NT = -(-N // P)
NP = NT * P
LAST = N - (NT - 1) * P
H2 = 2
HS = H2 * P
G = 2 * H2
GS = G * P
U = 4
NG = -(-((E + NT * (HS - 1)) // HS) // (2 * U)) * U
NH = 2 * NG
T = NG * G
TR = [(t, min(P, T - t)) for t in range(0, T, P)]
SLOTS = T * P
EC = E // P
ER = E - EC * P
CB = 8
CC = -(-(EC + 1) // (2 * CB)) * 2 * CB
RW = 8
BIG = 1.0e30
HUGE_SLOT = 1.0e6
NB = 5
EPS = 1e-5


class Chain:

    def __init__(self, eng, sem, base=0):
        self.eng, self.sem, self.base, self.n = eng, sem, base, 0

    def __call__(self, ins, wait=True):
        self.n += 1
        ins.then_inc(self.sem, 1)
        if wait:
            self.eng.wait_ge(self.sem, self.base + self.n)


def wait_apart(eng, sem, value):
    eng.wait_ge(sem, value)
    eng.sem_inc(PASSED[0], 1)


PASSED = []
SPENT = []


def clear_semaphores(nc):
    nc.clear_and_free_semaphores(SPENT)
    nc.all_engine_barrier()
    SPENT.clear()


class Phase:

    def __init__(self, nc, name):
        self.nc, self.name, self.ctx, self.sems = nc, name, ExitStack(), []

    def __enter__(self):
        self.ctx.__enter__()
        return self

    def __exit__(self, *e):
        return self.ctx.__exit__(*e)

    def sb(self, name, shape, d=F32):
        return self.ctx.enter_context(self.nc.sbuf_tensor(f"{self.name}_{name}", shape, d))

    def ps(self, name, shape, d=F32):
        return self.ctx.enter_context(self.nc.psum_tensor(f"{self.name}_{name}", shape, d))

    def sem(self, name):
        s = self.nc.alloc_semaphore(f"{self.name}_{name}")
        SPENT.append(s)
        return s

    def block(self):
        return self.ctx.enter_context(self.nc.Block())


def constants(nc, C):
    with Phase(nc, "cst") as ph:
        made = ph.sem("made")
        block = ph.block()

        @block.gpsimd
        def _(pool):
            link = Chain(pool, made)
            link(nc.gpsimd.iota(C.iota_row[:], [[1, P]], base=0, channel_multiplier=0,
                                allow_small_or_imprecise_dtypes=True))
            link(nc.gpsimd.iota(C.iota_col[:], [[0, 1]], base=0, channel_multiplier=1,
                                allow_small_or_imprecise_dtypes=True))
            link(nc.gpsimd.memset(C.ones[:], 1.0))
            link(nc.gpsimd.memset(C.ident[:], 0.0))
            link(nc.gpsimd.affine_select(out=C.ident[:], in_=C.ident[:], compare_op=ALU.not_equal, fill=1.0,
                                         base=0, pattern=[[-1, P]], channel_multiplier=1))
            link(nc.gpsimd.affine_select(out=C.before[:], in_=C.ones[:], compare_op=ALU.is_ge, fill=0.0,
                                         base=-1, pattern=[[1, P]], channel_multiplier=-1))
            link(nc.gpsimd.memset(C.zerosb[:], 0.0))


def sort_edges(nc, C, name, key, other, attr_row, w1, w, rec, ntile, count, loc_dram, rec_dram):
    with Phase(nc, name) as ph:
        keyi = ph.sb("keyi", [P, CC], I32)
        otheri = ph.sb("otheri", [P, CC], I32)
        w1f = ph.sb("w1f", [P, CC])
        wf = ph.sb("wf", [P, CC])
        bucket = ph.sb("bucket", [P, CC], I32)
        bucketf = ph.sb("bucketf", [P, CC])
        locf = ph.sb("locf", [P, CC])
        zero = ph.sb("zero", [P, CC])
        mask = ph.sb("mask", [P, CC])
        cum = ph.sb("cum", [P, NT, CC])
        maskb = ph.sb("maskb", [P, CC, NT], BF16)
        low = ph.sb("low", [P, 2, CB, P], BF16)
        tot = ph.sb("tot", [P, NT])
        tots = ph.sb("tots", [P, 2, NT])
        toti = ph.sb("toti", [P, NT], I32)
        first = ph.sb("first", [P, NT])
        base = ph.sb("base", [P, NT])
        slot = ph.sb("slot", [P, CC])
        sloti = ph.sb("sloti", [P, CC], I32)
        part = ph.sb("part", [P, CC], I32)
        addr = ph.sb("addr", [P, CC], I32)
        r = ph.sb("r", [P, CC, RW])
        giota = ph.sb("giota", [P, NH])
        nta = ph.sb("nta", [P, NH])
        ring = ph.sb("ring", [P, 2, CB], I32)
        rring = ph.sb("rring", [P, 2, CB, RW])
        loct = ph.sb("loct", [P, len(TR), P])
        p_tot = ph.ps("p_tot", [P, 2, NT])
        p_cnt = ph.ps("p_cnt", [P, NT])
        p_tr = ph.ps("p_tr", [P, 4, P])
        loaded, chain, tot_ready, tot_done = (ph.sem(x) for x in ("loaded", "chain", "tot_ready", "tot_done"))
        low_ready, counted, filled = (ph.sem(x) for x in ("low_ready", "counted", "filled"))
        made, addr_ready, ring_ready = (ph.sem(x) for x in ("made", "addr_ready", "ring_ready"))
        scattered = [ph.sem(f"scattered{k}") for k in range(2)]
        rec_loaded, tr_ready, tr_done, pad_stored = (ph.sem(x) for x in ("rec_loaded", "tr_ready", "tr_done", "pad_stored"))
        loc_stored, pads = ph.sem("loc_stored"), ph.sem("pads")
        block = ph.block()
        blocks = CC // CB

        @block.sync
        def _(sp):
            sp.wait_ge(filled, 1)
            for to, frm in ((keyi, key), (otheri, other), (w1f, w1), (wf, w)):
                sp.dma_start(to[:, 0:EC], frm[0:EC * P].rearrange("(p c) -> p c", p=P)).then_inc(loaded, 16)
                sp.dma_start(to[0:ER, EC:EC + 1], frm[EC * P:E].unsqueeze(1)).then_inc(loaded, 16)
            sp.wait_ge(pads, 1)
            sp.dma_start(rec_dram.rearrange("(p t) w -> p (t w)", p=P),
                         rec[:].rearrange("p t w -> p (t w)")).then_inc(pad_stored, 16)
            for k in range(2):
                sp.wait_ge(scattered[k], 16 * CC // 2)
            sp.dma_start(rec[:].rearrange("p t w -> p (t w)"),
                         rec_dram.rearrange("(p t) w -> p (t w)", p=P)).then_inc(rec_loaded, 16)
            sp.wait_ge(tr_done, 1)
            for k, (t, n) in enumerate(TR):
                sp.dma_start(loc_dram[t:t + n, :], loct[0:n, k, :]).then_inc(loc_stored, 16)
            sp.wait_ge(loc_stored, 16 * len(TR))

        @block.gpsimd
        def _(pool):
            nc.gpsimd.iota(giota[:], [[H2, NH]], base=0, channel_multiplier=0,
                           allow_small_or_imprecise_dtypes=True).then_inc(made, 1)
            pool.wait_ge(filled, 1)
            nc.gpsimd.iota(r[:, 0:EC, 4].bitcast(I32), [[2, EC]], base=attr_row,
                           channel_multiplier=2 * EC).then_inc(made, 1)
            nc.gpsimd.iota(r[:, EC:EC + 1, 4].bitcast(I32), [[0, 1]], base=attr_row + 2 * EC * P,
                           channel_multiplier=2).then_inc(made, 1)
            pool.wait_ge(loaded, 8 * 16)
            nc.gpsimd.tensor_copy(r[:, :, 0].bitcast(I32), otheri[:]).then_inc(made, 1)
            nc.gpsimd.tensor_copy(r[:, :, 2], w1f[:]).then_inc(made, 1)
            nc.gpsimd.tensor_copy(r[:, :, 3], wf[:]).then_inc(made, 1)
            pool.wait_ge(made, 6)
            pool.wait_ge(addr_ready, 1)
            pool.wait_ge(pad_stored, 16)

            def scatter(i, u):
                c0 = i * (2 * CB) + u * CB
                nc.gpsimd.tensor_copy(ring[:, u, :], addr[:, bass.ds(c0, CB)]).then_inc(ring_ready, 1)
                nc.gpsimd.tensor_copy(rring[:, u, :, :], r[:, bass.ds(c0, CB), :]).then_inc(ring_ready, 1)
                wait_apart(pool, ring_ready, i * 4 + 2 * u + 2)
                for k in range(CB):
                    pool.indirect_dma_start(rec_dram, bass.IndirectOffsetOnAxis(ap=ring[:, u, k:k + 1], axis=0),
                                            rring[:, u, k, :], None, bounds_check=SLOTS - 1,
                                            oob_is_err=False).then_inc(scattered[u], 16)

            scatter(0, 0)
            scatter(0, 1)
            with pool.Fori(0, blocks // 2 - 1) as i:
                for u in range(2):
                    wait_apart(pool, scattered[u], i * (16 * CB) + 16 * CB)
                    scatter(i + 1, u)

        @block.vector
        def _(dve):
            link = Chain(dve, chain)
            link(nc.vector.memset(keyi[:], NT * P))
            link(nc.vector.memset(otheri[:], 0))
            link(nc.vector.memset(w1f[:], 0.0))
            link(nc.vector.memset(wf[:], 0.0))
            link(nc.vector.memset(zero[:], 0.0))
            link(nc.vector.memset(r[:], 0.0))
            nc.vector.tensor_copy(slot[:], zero[:]).then_inc(filled, 1)
            link(nc.vector.tensor_copy(nta[:], zero[:, 0:NH]))
            link(nc.vector.memset(rec[:], 0.0))
            nc.vector.memset(rec[:, :, 1], -1.0).then_inc(pads, 1)
            dve.wait_ge(filled, 1)
            dve.wait_ge(loaded, 8 * 16)
            link(nc.vector.tensor_single_scalar(bucket[:], keyi[:], 7, ALU.logical_shift_right))
            link(nc.vector.tensor_single_scalar(part[:], keyi[:], P - 1, ALU.bitwise_and))
            link(nc.vector.tensor_copy(bucketf[:], bucket[:]))
            link(nc.vector.tensor_copy(locf[:], part[:]))
            link(nc.vector.tensor_copy(r[:, :, 1], part[:]))
            for b in range(NT):
                nc.vector.tensor_scalar(maskb[:, :, b], bucketf[:], float(b), None, ALU.is_equal)
                link(nc.vector.tensor_scalar(mask[:], bucketf[:], float(b), None, ALU.is_equal))
                link(nc.vector.tensor_tensor_scan(cum[:, b, :], mask[:], zero[:], 0.0, ALU.add, ALU.add))
            link(nc.vector.tensor_copy(tot[:], cum[:, :, CC - 1]))
            nc.vector.memset(low[:], 0.0).then_inc(tot_ready, 1)
            dve.wait_ge(tot_done, 1)
            link(nc.vector.tensor_copy(tots[:], p_tot[:]))
            link(nc.vector.tensor_scalar(first[:], tots[:, 1, :], float(HS - 1), None, ALU.add))
            link(nc.vector.tensor_copy(toti[:], first[:]))
            link(nc.vector.tensor_single_scalar(toti[:], toti[:], HS.bit_length() - 1, ALU.logical_shift_right))
            link(nc.vector.tensor_copy(tot[:], toti[:]))
            link(nc.vector.tensor_tensor_scan(first[:], tot[:], zero[:, 0:NT], 0.0, ALU.add, ALU.add))
            link(nc.vector.tensor_tensor(first[:], first[:], tot[:], ALU.subtract))
            link(nc.vector.scalar_tensor_tensor(base[:], first[:], float(HS), tots[:, 0, :], ALU.mult, ALU.add))
            link(nc.vector.tensor_scalar(base[:], base[:], -1.0, None, ALU.add))
            for b in range(NT):
                link(nc.vector.scalar_tensor_tensor(cum[:, b, :], cum[:, b, :], base[:, b:b + 1], maskb[:, :, b],
                                                    ALU.add, ALU.mult))
                link(nc.vector.tensor_tensor(slot[:], slot[:], cum[:, b, :], ALU.add))
            link(nc.vector.tensor_copy(sloti[:], slot[:]))
            link(nc.vector.tensor_single_scalar(part[:], sloti[:], P - 1, ALU.bitwise_and))
            link(nc.vector.tensor_single_scalar(sloti[:], sloti[:], 7, ALU.logical_shift_right))
            link(nc.vector.tensor_copy(slot[:], part[:]))
            link(nc.vector.tensor_copy(mask[:], sloti[:]))
            link(nc.vector.scalar_tensor_tensor(slot[:], slot[:], float(T), mask[:], ALU.mult, ALU.add))
            link(nc.vector.tensor_scalar(mask[:], bucketf[:], float(NT), HUGE_SLOT, ALU.is_ge, ALU.mult))
            link(nc.vector.tensor_tensor(slot[:], slot[:], mask[:], ALU.add))
            nc.vector.tensor_copy(addr[:], slot[:]).then_inc(addr_ready, 1)
            dve.wait_ge(made, 1)
            link(nc.vector.tensor_scalar(first[:], first[:], float(H2), None, ALU.mult))
            for b in range(1, NT):
                link(nc.vector.scalar_tensor_tensor(nta[:], giota[:], first[:, b:b + 1], nta[:], ALU.is_ge, ALU.add))
            link(nc.vector.tensor_copy(ntile[:], nta[:]))

            with dve.Fori(0, blocks // 2) as i:
                for u in range(2):
                    dve.wait_ge(counted, i * 2 + u + 1)
                    nc.vector.tensor_tensor(low[:, u, :, :], C.iota_row[:].unsqueeze(1).to_broadcast([P, CB, P]),
                                            locf[:, bass.ds(i * (2 * CB) + u * CB, CB)].unsqueeze(2).to_broadcast([P, CB, P]),
                                            ALU.is_equal).then_inc(low_ready, 1)
            dve.wait_ge(counted, blocks + 3)
            link(nc.vector.tensor_copy(count[:], p_cnt[:]))
            dve.wait_ge(tr_ready, 1)
            for k, (t, n) in enumerate(TR):
                last = nc.vector.tensor_copy(loct[0:n, k, :], p_tr[0:n, k, :])
            last.then_inc(tr_done, 1)

        @block.tensor
        def _(pe):
            pe.wait_ge(tot_ready, 1)
            nc.tensor.matmul(p_tot[:, 0, :], C.before[:], tot[:], start=True, stop=True)
            nc.tensor.matmul(p_tot[:, 1, :], C.ones[:], tot[:], start=True, stop=True).then_inc(tot_done, 1)
            nc.tensor.matmul(p_cnt[:], low[:, 0, 0, :], maskb[:, 0, :], start=True, stop=False).then_inc(counted, 1)
            pe.wait_ge(counted, 1)
            nc.tensor.nop().then_inc(counted, 1)
            with pe.Fori(0, blocks // 2) as i:
                for u in range(2):
                    pe.wait_ge(low_ready, i * 2 + u + 1)
                    for k in range(CB):
                        last = nc.tensor.matmul(p_cnt[:], low[:, u, k, :],
                                                maskb[:, bass.ds(i * (2 * CB) + u * CB + k, 1), :].squeeze(1),
                                                start=False, stop=False)
                    last.then_inc(counted, 1)
            nc.tensor.matmul(p_cnt[:], C.zerosb[:], maskb[:, 0, :], start=False, stop=True).then_inc(counted, 1)
            pe.wait_ge(rec_loaded, 16)
            for k, (t, n) in enumerate(TR):
                last = nc.tensor.transpose(p_tr[0:n, k, :], rec[:, t:t + n, 1], C.ident[:])
            last.then_inc(tr_ready, 1)


def behind(i, u, d):
    return (i + (u + d) // U if (u + d) // U else i), (u + d) % U


def nth(i, u, per=1):
    return i * (U * per) + (u + 1) * per


def tiles(i, u):
    return bass.ds(i * (U * G) + u * G, G)


def gather_groups(nc, pool, ring, indexed, table, rows, gathered, used):
    def issue(i, u):
        wait_apart(pool, indexed, nth(i, u))
        for k in range(G):
            pool.indirect_dma_start(rows(u, k), None, table,
                                    bass.IndirectOffsetOnAxis(ap=ring[:, u, k:k + 1], axis=0)).then_inc(gathered[u], 16)

    for u in range(U):
        issue(0, u)
    with pool.Fori(1, NG // U) as i:
        for u in range(U):
            wait_apart(pool, used, nth(i - 1, u))
            issue(i, u)


def index_ring(nc, act, rec, word, ring, indexed):
    def index(i, u):
        nc.scalar.copy(ring[:, u, :], rec[:, tiles(i, u), word].bitcast(I32)).then_inc(indexed, 1)
    return index


def load_key_rows(sp, loc, rowb, loaded, used):
    def issue(i, u):
        keys = loc[tiles(i, u), :].rearrange("t p -> (t p)").partition_broadcast(P)
        sp.dma_start(rowb[:, u, :], keys).then_inc(loaded[u], 16)

    for u in range(U):
        issue(0, u)
    with sp.Fori(1, NG // U) as i:
        for u in range(U):
            sp.wait_ge(used, nth(i - 1, u))
            issue(i, u)


NODE_TILE_LOADS = [0]


def node_tiles(eng, C, side, i, u):
    NODE_TILE_LOADS[0] += 1
    regs = [eng.alloc_register(f"node_tile{NODE_TILE_LOADS[0]}_{s}") for s in range(2)]
    eng.load(regs, C.nt[side][0:1, bass.ds(i * (2 * U) + 2 * u, 2)])
    return [eng.snap(r, donate=True, min_val=0, max_val=NT - 1) for r in regs]


def one_hot(nc, C, side, out, i, u):
    keys = C.rec[side][:, tiles(i, u), 1].unsqueeze(2).to_broadcast([P, G, P])
    return nc.vector.tensor_tensor(out, C.iota_row[:].unsqueeze(1).to_broadcast([P, G, P]), keys, ALU.is_equal)


def turns(eng, step):
    for u in range(U):
        step(0, u, first=u == 0)
    with eng.Fori(1, NG // U - 1) as i:
        for u in range(U):
            step(i, u)
    for u in range(U):
        step(NG // U - 1, u, last=u == U - 1)


def half_sums(nc, ps, oh, rows, W):
    for k in range(G):
        last = nc.tensor.matmul(ps[:, k // H2, 0:W], oh[:, k, :], rows[:, k, :], start=(k % H2 == 0), stop=(k % H2 == H2 - 1))
    return last


def sum_pass(nc, C, name, side, table, acc, squares=False, weights=None):
    W = 2 * F if squares else F
    with Phase(nc, name) as ph:
        g = ph.sb("g", [P, U, G, W])
        oh = ph.sb("oh", [P, U, G, P])
        ring = ph.sb("ring", [P, U, G], I32)
        ps = [ph.ps(f"ps{u % 2}", [P, 2, 256]) for u in range(2)] * 2
        indexed, oh_ready, raw_ready, acc_done, acc_set, squared = (
            ph.sem(x) for x in ("indexed", "oh_ready", "raw_ready", "acc_done", "acc_set", "squared"))
        gathered = [ph.sem(f"gathered{u}") for u in range(U)]
        block = ph.block()

        @block.gpsimd
        def _(pool):
            gather_groups(nc, pool, ring, indexed, table, lambda u, k: g[:, u, k, 0:F], gathered, acc_done)

        @block.scalar
        def _(act):
            index = index_ring(nc, act, C.rec[side], 0, ring, indexed)

            def step(i, u, first=False, last=False):
                act.wait_ge(gathered[u], i * (16 * G) + 16 * G)
                if squares:
                    nc.scalar.activation(g[:, u, :, F:W], g[:, u, :, 0:F], ACT.Square).then_inc(squared, 1)

            for u in range(U):
                index(0, u)
            with act.Fori(0, NG // U - 1) as i:
                for u in range(U):
                    step(i, u)
                    index(i + 1, u)
            if squares:
                for u in range(U):
                    step(NG // U - 1, u)

        @block.vector
        def _(dve):
            nc.vector.memset(acc[:], 0.0).then_inc(acc_set, 1)

            def build(i, u):
                if weights is None:
                    one_hot(nc, C, side, oh[:, u], i, u).then_inc(oh_ready, 1)
                    return
                one_hot(nc, C, side, oh[:, u], i, u).then_inc(raw_ready, 1)
                dve.wait_ge(raw_ready, nth(i, u))
                w = weights[:, tiles(i, u)].unsqueeze(2).to_broadcast([P, G, P])
                nc.vector.tensor_tensor(oh[:, u], oh[:, u], w, ALU.mult).then_inc(oh_ready, 1)

            def step(i, u, first=False, last=False):
                if not last:
                    build(*behind(i, u, 1))
                nt = node_tiles(dve, C, side, i, u)
                dve.wait_ge(acc_done, nth(i, u))
                for s in range(2):
                    dve.wait_ge(acc_set, nth(i, u, 2) - 1 + s)
                    here = acc[:, bass.ds(nt[s], 1), :].squeeze(1)
                    nc.vector.tensor_tensor(here, here, ps[u][:, s, 0:W], ALU.add).then_inc(acc_set, 1)

            build(0, 0)
            turns(dve, step)

        @block.tensor
        def _(pe):
            with pe.Fori(0, NG // U) as i:
                for u in range(U):
                    pe.wait_ge(oh_ready, nth(i, u))
                    pe.wait_ge(gathered[u], i * (16 * G) + 16 * G)
                    if squares:
                        pe.wait_ge(squared, nth(i, u))
                    half_sums(nc, ps[u], oh[:, u], g[:, u], W).then_inc(acc_done, 1)


def gat_pass(nc, C, name, table, H, strg3, stp, acc, macc, negm):
    W, D = F + H, F // H
    with Phase(nc, name) as ph:
        g = ph.sb("g", [P, U, G, W])
        msg = ph.sb("msg", [P, U, G, W])
        oh = ph.sb("oh", [P, U, G, P])
        oht = ph.sb("oht", [P, U, GS], BF16)
        rowb = ph.sb("rowb", [P, U, GS])
        ring = ph.sb("ring", [P, U, G], I32)
        z = ph.sb("z", [P, U, G, H])
        rm = ph.sb("rm", [P, 1])
        rrun = ph.sb("rrun", [P, 1])
        m1 = ph.sb("m1", [1, 1])
        nm = ph.sb("nm", [P, U])
        f = ph.sb("f", [P, U, 2])
        ps = [ph.ps(f"ps{u % 2}", [P, 2, 256]) for u in range(2)] * 2
        p_st = ph.ps("p_st", [P, 512])
        p_t = ph.ps("p_t", [P, P])
        p_m = ph.ps("p_m", [P, 1])
        names = ("indexed oht_ready oh_ready chain strg_done max_ready turned m1_ready spread negm_ready ex_ready "
                 "f_ready macc_set msg_ready acc_done acc_set")
        (indexed, oht_ready, oh_ready, chain, strg_done, max_ready, turned, m1_ready, spread, negm_ready, ex_ready,
         f_ready, macc_set, msg_ready, acc_done, acc_set) = (ph.sem(x) for x in names.split())
        gathered = [ph.sem(f"gathered{u}") for u in range(U)]
        rows_loaded = [ph.sem(f"rows_loaded{u}") for u in range(U)]
        block = ph.block()

        @block.gpsimd
        def _(pool):
            gather_groups(nc, pool, ring, indexed, table, lambda u, k: g[:, u, k, :], gathered, msg_ready)

        @block.sync
        def _(sp):
            load_key_rows(sp, C.loc["D"], rowb, rows_loaded, oht_ready)

        @block.vector
        def _(dve):
            LINKS = 4
            nc.vector.memset(macc[:], -BIG).then_inc(macc_set, 1)
            nc.vector.memset(rrun[:], -BIG)
            nc.vector.memset(acc[:], 0.0).then_inc(acc_set, 1)
            dve.wait_ge(acc_set, 1)

            def turn_keys(i, u):
                dve.wait_ge(rows_loaded[u], i * 16 + 16)
                nc.vector.tensor_scalar(oht[:, u], rowb[:, u], C.iota_col[:], None, ALU.is_equal).then_inc(oht_ready, 1)

            def score(i, u):
                link = Chain(dve, chain, nth(i, u, LINKS) - LINKS)
                dve.wait_ge(gathered[u], i * (16 * G) + 16 * G)
                dve.wait_ge(strg_done, nth(i, u))
                link(nc.vector.tensor_tensor(z[:, u], g[:, u, :, F:W], p_st[:, 0:G * H].rearrange("p (g h) -> p g h", g=G), ALU.add))
                link(nc.vector.tensor_tensor(z[:, u], z[:, u], stp[:, tiles(i, u), :], ALU.add))
                link(nc.vector.scalar_tensor_tensor(z[:, u], z[:, u], 0.2, z[:, u], ALU.mult, ALU.max))
                link(nc.vector.tensor_reduce(rm[:], z[:, u], AX.XY, ALU.max))
                nc.vector.tensor_tensor(rrun[:], rrun[:], rm[:], ALU.max).then_inc(max_ready, 1)

            def add(i, u):
                nt = node_tiles(dve, C, "D", i, u)
                dve.wait_ge(acc_done, nth(i, u))
                dve.wait_ge(f_ready, nth(i, u, 2))
                for s in range(2):
                    dve.wait_ge(acc_set, nth(i, u, 2) - 1 + s)
                    here = acc[:, bass.ds(nt[s], 1), :].squeeze(1)
                    nc.vector.scalar_tensor_tensor(here, here, f[:, u, s:s + 1], ps[u][:, s, 0:W], ALU.mult,
                                                   ALU.add).then_inc(acc_set, 1)

            def step(i, u, first=False, last=False):
                dve.wait_ge(turned, nth(i, u))
                nc.vector.tensor_reduce(m1[:], p_t[0:1, :], AX.X, ALU.max).then_inc(m1_ready, 1)
                if not last:
                    turn_keys(*behind(i, u, 1))
                dve.wait_ge(spread, nth(i, u))
                nc.vector.tensor_scalar(nm[:, u:u + 1], p_m[:], -1.0, None, ALU.mult).then_inc(negm_ready, 1)
                one_hot(nc, C, "D", oh[:, u], i, u).then_inc(oh_ready, 1)
                if not last:
                    score(*behind(i, u, 1))
                dve.wait_ge(ex_ready, nth(i, u))
                nc.vector.tensor_tensor(msg[:, u, :, 0:F].rearrange("p g (h d) -> p g h d", h=H),
                                        g[:, u, :, 0:F].rearrange("p g (h d) -> p g h d", h=H),
                                        msg[:, u, :, F:W].unsqueeze(3).to_broadcast([P, G, H, D]),
                                        ALU.mult).then_inc(msg_ready, 1)
                if not first:
                    add(*behind(i, u, -1))

            turn_keys(0, 0)
            score(0, 0)
            turns(dve, step)
            add(NG // U - 1, U - 1)
            nc.vector.tensor_copy(negm[:], nm[:, U - 1:U]).then_inc(acc_set, 1)

        @block.scalar
        def _(act):
            index = index_ring(nc, act, C.rec["D"], 0, ring, indexed)

            def step(i, u, first=False, last=False):
                nt = node_tiles(act, C, "D", i, u)
                act.wait_ge(negm_ready, nth(i, u))
                nc.scalar.activation(msg[:, u, :, F:W], z[:, u], ACT.Exp, bias=nm[:, u:u + 1]).then_inc(ex_ready, 1)
                for s in range(2):
                    here = macc[:, bass.ds(nt[s], 1)]
                    wait_apart(act, macc_set, nth(i, u, 2) - 1 + s)
                    nc.scalar.activation(f[:, u, s:s + 1], here, ACT.Exp, bias=nm[:, u:u + 1]).then_inc(f_ready, 1)
                    wait_apart(act, f_ready, nth(i, u, 2) - 1 + s)
                    nc.scalar.mul(here, nm[:, u:u + 1], -1.0).then_inc(macc_set, 1)

            for u in range(U):
                index(0, u)
            with act.Fori(0, NG // U - 1) as i:
                for u in range(U):
                    step(i, u)
                    index(i + 1, u)
            for u in range(U):
                step(NG // U - 1, u)

        @block.tensor
        def _(pe):
            def ahead(i, u):
                nt = node_tiles(pe, C, "D", i, u)
                pe.wait_ge(oht_ready, nth(i, u))
                for k in range(G):
                    for q in range(3):
                        last = nc.tensor.matmul(p_st[:, k * H:(k + 1) * H], oht[:, u, k * P:(k + 1) * P],
                                                strg3[:, q, bass.ds(nt[k // H2], 1), :].squeeze(1), start=(q == 0), stop=(q == 2))
                last.then_inc(strg_done, 1)

            def turn_max(i, u):
                pe.wait_ge(max_ready, nth(i, u))
                nc.tensor.transpose(p_t[0:1, :], rrun[:], C.ident[:]).then_inc(turned, 1)

            def sums(i, u):
                pe.wait_ge(oh_ready, nth(i, u))
                pe.wait_ge(msg_ready, nth(i, u))
                half_sums(nc, ps[u], oh[:, u], msg[:, u], W).then_inc(acc_done, 1)

            def step(i, u, first=False, last=False):
                pe.wait_ge(m1_ready, nth(i, u))
                nc.tensor.matmul(p_m[:], C.ones[0:1, :], m1[:], start=True, stop=True).then_inc(spread, 1)
                if not last:
                    ahead(*behind(i, u, 1))
                if not first:
                    sums(*behind(i, u, -1))
                if not last:
                    turn_max(*behind(i, u, 1))

            ahead(0, 0)
            turn_max(0, 0)
            turns(pe, step)
            sums(NG // U - 1, U - 1)


def attention_pass(nc, C, name, side, table, ht, acc, m, opening):
    W = F + 1
    SCALE = float(F) ** -0.5
    with Phase(nc, name) as ph:
        g = ph.sb("g", [P, U, G, W])
        gt = ph.sb("gt", [P, 2, GS])
        hts = ph.sb("hts", [P, 2, 2, P])
        pen = ph.sb("pen", [P, 2, GS])
        low = ph.sb("low", [P, 2, GS])
        e = ph.sb("e", [P, 2, GS])
        wt = ph.sb("wt", [P, 2, G, P])
        rowb = ph.sb("rowb", [P, U, GS])
        ring = ph.sb("ring", [P, U, G], I32)
        mt = ph.sb("mt", [P, 2])
        mn = ph.sb("mn", [P, 2])
        nmn = ph.sb("nmn", [P, U, 2])
        df = ph.sb("df", [P, U, 2])
        f = ph.sb("f", [P, U, 2])
        ps = [ph.ps(f"ps{u}", [P, 2, 256]) for u in range(2)]
        p_g = [ph.ps(f"p_g{u}", [P, GS]) for u in range(2)]
        p_l = ph.ps("p_l", [P, GS])
        p_w = [ph.ps(f"p_w{u}", [P, G, P]) for u in range(2)]
        names = ("indexed opened chain turned gt_ready pen_ready products m_ready f_ready e_ready weights_turned "
                 "wt_ready acc_done acc_set")
        (indexed, opened, chain, turned, gt_ready, pen_ready, products, m_ready, f_ready, e_ready, weights_turned,
         wt_ready, acc_done, acc_set) = (ph.sem(x) for x in names.split())
        gathered = [ph.sem(f"gathered{u}") for u in range(U)]
        rows_loaded = [ph.sem(f"rows_loaded{u}") for u in range(U)]
        block = ph.block()

        @block.gpsimd
        def _(pool):
            gather_groups(nc, pool, ring, indexed, table, lambda u, k: g[:, u, k, 0:F], gathered, acc_done)

        @block.sync
        def _(sp):
            load_key_rows(sp, C.loc[side], rowb, rows_loaded, pen_ready)

        @block.vector
        def _(dve):
            LINKS = 8
            nc.vector.memset(g[:, :, :, F:W], 1.0).then_inc(opened, 1)
            if opening:
                nc.vector.memset(m[:], -BIG)
                nc.vector.memset(acc[:], 0.0).then_inc(acc_set, 1)
            else:
                nc.vector.memset(mt[:], 0.0).then_inc(acc_set, 1)
            dve.wait_ge(acc_set, 1)

            def prepare(i, u):
                nt = node_tiles(dve, C, side, i, u)
                for s in range(2):
                    nc.vector.tensor_copy(hts[:, u % 2, s, :], ht[:, bass.ds(nt[s], 1), :].squeeze(1))
                dve.wait_ge(rows_loaded[u], i * 16 + 16)
                nc.vector.tensor_scalar(pen[:, u % 2], rowb[:, u], C.iota_col[:], -4.0 * BIG, ALU.not_equal, ALU.mult).then_inc(pen_ready, 1)

            def add(i, u):
                nt = node_tiles(dve, C, side, i, u)
                dve.wait_ge(acc_done, nth(i, u))
                dve.wait_ge(f_ready, nth(i, u))
                for s in range(2):
                    dve.wait_ge(acc_set, nth(i, u, 2) - 1 + s)
                    here = acc[:, bass.ds(nt[s], 1), :].squeeze(1)
                    nc.vector.scalar_tensor_tensor(here, here, f[:, u, s:s + 1], ps[u % 2][:, s, 0:W], ALU.mult,
                                                   ALU.add).then_inc(acc_set, 1)

            def step(i, u, first=False, last=False):
                if not first:
                    take_weights(*behind(i, u, -1))
                link = Chain(dve, chain, nth(i, u, LINKS) - LINKS)
                nt = node_tiles(dve, C, side, i, u)
                wait_apart(dve, products, nth(i, u))
                for s in range(2):
                    half = slice(s * HS, (s + 1) * HS)
                    link(nc.vector.tensor_tensor_reduce(out=low[:, u % 2, half], in0=p_l[:, half], in1=pen[:, u % 2, half],
                                                        scale=1.0, scalar=-3.0e38, op0=ALU.add, op1=ALU.max,
                                                        accum_out=mt[:, s:s + 1]), wait=s == 1)
                for s in range(2):
                    here = m[:, bass.ds(nt[s], 1)]
                    link(nc.vector.tensor_tensor(mn[:, s:s + 1], here, mt[:, s:s + 1], ALU.max))
                    link(nc.vector.tensor_tensor(df[:, u, s:s + 1], here, mn[:, s:s + 1], ALU.subtract))
                    link(nc.vector.tensor_tensor(here, here, mt[:, s:s + 1], ALU.max))
                nc.vector.tensor_scalar(nmn[:, u], mn[:], -SCALE, None, ALU.mult).then_inc(m_ready, 1)
                if not last:
                    prepare(*behind(i, u, 1))
                if not first:
                    add(*behind(i, u, -1))

            def take_weights(i, u):
                dve.wait_ge(weights_turned, nth(i, u))
                nc.vector.tensor_copy(wt[:, u % 2], p_w[u % 2][:]).then_inc(wt_ready, 1)

            prepare(0, 0)
            turns(dve, step)
            take_weights(NG // U - 1, U - 1)
            add(NG // U - 1, U - 1)

        @block.scalar
        def _(act):
            index = index_ring(nc, act, C.rec[side], 4, ring, indexed)

            def take_rows(i, u):
                act.wait_ge(turned, nth(i, u))
                nc.scalar.copy(gt[:, u % 2], p_g[u % 2][:]).then_inc(gt_ready, 1)

            def step(i, u, first=False, last=False, index_next=True):
                act.wait_ge(m_ready, nth(i, u))
                for s in range(2):
                    half = slice(s * HS, (s + 1) * HS)
                    ex = nc.scalar.activation(e[:, u % 2, half], low[:, u % 2, half], ACT.Exp, bias=nmn[:, u, s:s + 1], scale=SCALE)
                ex.then_inc(e_ready, 1)
                nc.scalar.activation(f[:, u], df[:, u], ACT.Exp, scale=SCALE).then_inc(f_ready, 1)
                if index_next:
                    act.wait_ge(gathered[u], i * (16 * G) + 16 * G)
                    index(i + 1, u)
                if not last:
                    take_rows(*behind(i, u, 1))

            for u in range(U):
                index(0, u)
            take_rows(0, 0)
            with act.Fori(0, NG // U - 1) as i:
                for u in range(U):
                    step(i, u)
            for u in range(U):
                step(NG // U - 1, u, last=u == U - 1, index_next=False)

        @block.tensor
        def _(pe):
            def turn_rows(i, u):
                pe.wait_ge(gathered[u], i * (16 * G) + 16 * G)
                for k in range(G):
                    last = nc.tensor.transpose(p_g[u % 2][:, k * P:(k + 1) * P], g[:, u, k, 0:F], C.ident[:])
                last.then_inc(turned, 1)

            def multiply(i, u):
                pe.wait_ge(pen_ready, nth(i, u))
                pe.wait_ge(gt_ready, nth(i, u))
                for s in range(2):
                    half = slice(s * HS, (s + 1) * HS)
                    last = nc.tensor.matmul(p_l[:, half], hts[:, u % 2, s, :], gt[:, u % 2, half], start=True, stop=True)
                last.then_inc(products, 1)

            def sums(i, u):
                pe.wait_ge(wt_ready, nth(i, u))
                half_sums(nc, ps[u % 2], wt[:, u % 2], g[:, u], W).then_inc(acc_done, 1)

            def step(i, u, first=False, last=False):
                multiply(i, u)
                if not first:
                    sums(*behind(i, u, -1))
                if not last:
                    turn_rows(*behind(i, u, 1))
                pe.wait_ge(e_ready, nth(i, u))
                for k in range(G):
                    lastk = nc.tensor.transpose(p_w[u % 2][:, k, :], e[:, u % 2, k * P:(k + 1) * P], C.ident[:])
                lastk.then_inc(weights_turned, 1)

            pe.wait_ge(opened, 1)
            turn_rows(0, 0)
            turns(pe, step)
            sums(NG // U - 1, U - 1)


def turn_nodes(nc, C, name, h, ht):
    with Phase(nc, name) as ph:
        p_h = [ph.ps(f"p_h{q}", [P, 512]) for q in range(2)]
        turned, taken = ph.sem("turned"), ph.sem("taken")
        block = ph.block()

        @block.tensor
        def _(pe):
            for t in range(NT):
                if t % 4 == 0 and t >= 8:
                    pe.wait_ge(taken, t // 4 - 1)
                nc.tensor.transpose(p_h[t // 4 % 2][:, t % 4 * P:(t % 4 + 1) * P], h[:, t, :], C.ident[:]).then_inc(turned, 1)

        @block.scalar
        def _(act):
            for t in range(0, NT, 4):
                n = min(4, NT - t)
                act.wait_ge(turned, t + n)
                nc.scalar.copy(ht[:, t:t + n, :], p_h[t // 4 % 2][:, 0:n * P].rearrange("p (t n) -> p t n", n=P)).then_inc(taken, 1)


def linear(nc, C, name, parts, M, finish):
    with Phase(nc, name) as ph:
        K = len(parts)
        xs = ph.sb("xs", [P, K, NB, F])
        xt = ph.sb("xt", [P, K, NB, P])
        p_t = [ph.ps(f"p_t{q}", [P, 8, P]) for q in range(min(K, 2))]
        p_y = ph.ps("p_y", [P, 8, 256])
        staged, turned, xt_ready, multiplied, finished = (
            ph.sem(x) for x in ("staged", "turned", "xt_ready", "multiplied", "finished"))
        block = ph.block()

        @block.vector
        def _(dve):
            with dve.Fori(0, NT // NB) as i:
                for q, (x, _) in enumerate(parts):
                    nc.vector.tensor_copy(xs[:, q], x[:, bass.ds(i * NB, NB), :]).then_inc(staged, 1)
                wait_apart(dve, multiplied, i + 1)
                finish(i, p_y[:, 0:NB, 0:M]).then_inc(finished, 1)

        @block.scalar
        def _(act):
            with act.Fori(0, NT // NB) as i:
                for q in range(K):
                    act.wait_ge(turned, i * K + q + 1)
                    nc.scalar.copy(xt[:, q], p_t[q % 2][:, 0:NB, :]).then_inc(xt_ready, 1)

        @block.tensor
        def _(pe):
            with pe.Fori(0, NT // NB) as i:
                for q in range(K):
                    pe.wait_ge(staged, i * K + q + 1)
                    if q >= 2:
                        pe.wait_ge(xt_ready, i * K + q - 1)
                    for k in range(NB):
                        last = nc.tensor.transpose(p_t[q % 2][:, k, :], xs[:, q, k, :], C.ident[:])
                    last.then_inc(turned, 1)
                pe.wait_ge(xt_ready, i * K + K)
                for k in range(NB):
                    for q, (_, w) in enumerate(parts):
                        last = nc.tensor.matmul(p_y[:, k, 0:M], xt[:, q, k, :], w, start=(q == 0), stop=(q == K - 1))
                last.then_inc(multiplied, 1)


def per_node(v):
    return v.unsqueeze(2).to_broadcast([P, NT, F])


def per_feature(v):
    return v.unsqueeze(1).to_broadcast([P, NT, F])


class Vector:

    def __init__(self, nc, dve, sem):
        self.v, self.link = nc.vector, Chain(dve, sem)

    def tt(self, out, a, b, op):
        self.link(self.v.tensor_tensor(out, a, b, op))

    def ts(self, out, a, s1, op0, s2=None, op1=ALU.bypass):
        if s2 is None:
            self.link(self.v.tensor_scalar(out, a, s1, None, op0))
        else:
            self.link(self.v.tensor_scalar(out, a, s1, s2, op0, op1))

    def stt(self, out, a, s, b, op0, op1):
        self.link(self.v.scalar_tensor_tensor(out, a, s, b, op0, op1))

    def inverse_root(self, v, root, tmp):
        self.link(self.v.reciprocal(root, root))
        self.tt(tmp, root, root, ALU.mult)
        self.tt(tmp, tmp, v, ALU.mult)
        self.ts(tmp, tmp, -0.5, ALU.mult, 1.5, ALU.add)
        self.tt(root, root, tmp, ALU.mult)

    def bf16_terms(self, terms, a):
        for t in terms[:-1]:
            self.link(self.v.tensor_copy(t, a))
            self.tt(a, a, t, ALU.subtract)
        self.link(self.v.tensor_copy(terms[-1], a))

    def sum(self, out, a):
        self.link(self.v.tensor_reduce(out, a, AX.X, ALU.add))


def roots(nc, act, v, root, asked, rooted, times=1):
    for k in range(times):
        act.wait_ge(asked, k + 1)
        nc.scalar.activation(root, v, ACT.Sqrt).then_inc(rooted, 1)


def normalized_relu(V, dve, x, h, tmp, stat, to_root, rooted):
    V.sum(stat[:, 0], x[:])
    V.ts(stat[:, 0], stat[:, 0], 1.0 / F, ALU.mult)
    V.tt(h[:], x[:], per_node(stat[:, 0]), ALU.subtract)
    V.tt(tmp[:], h[:], h[:], ALU.mult)
    V.sum(stat[:, 1], tmp[:])
    V.v.tensor_scalar(stat[:, 1], stat[:, 1], 1.0 / F, EPS, ALU.mult, ALU.add).then_inc(to_root, 1)
    dve.wait_ge(rooted, 1)
    V.inverse_root(stat[:, 1], stat[:, 0], stat[:, 2])
    V.stt(h[:], h[:], 0.0, per_node(stat[:, 0]), ALU.max, ALU.mult)


def save_table(nc, C, name, rows, table):
    with Phase(nc, name) as ph:
        stored = ph.sem("stored")
        block = ph.block()

        @block.sync
        def _(sp):
            sp.dma_start(table.rearrange("(t p) w -> p t w", p=P), rows).then_inc(stored, 16)
            sp.wait_ge(stored, 16)


def gat_layer(nc, C, name, a, W, Wt, asrc, atrg, atp, b, Wskip, H, x, h, table, last_x=None):
    D, WD = F // H, F + H
    with Phase(nc, name) as top:
        tab = top.sb("tab", [P, NT, WD])
        skip = top.sb("skip", [P, NT, F]) if Wskip is not None else h
        acc = top.sb("acc", [P, NT, WD])
        strg = top.sb("strg", [P, NT, H])
        strg3 = top.sb("strg3", [P, 3, NT, H], BF16)
        stp = top.sb("stp", [P, T, H])
        macc = top.sb("macc", [P, NT])
        negm = top.sb("negm", [P, 1])
        rows = top.sb("rows", [P, 5, F])
        M = 2 * F if Wskip is not None else F
        w = top.sb("w", [P, M])
        ch = top.sb("ch", [P, H])
        pen = top.sb("pen", [P, T])
        with Phase(nc, name + "a") as ph:
            tmp = ph.sb("tmp", [P, F])
            loaded, chain = ph.sem("loaded"), ph.sem("chain")
            block = ph.block()

            @block.sync
            def _(sp):
                sp.dma_start(w[:, 0:F], W).then_inc(loaded, 16)
                if Wskip is not None:
                    sp.dma_start(w[:, F:M], Wskip).then_inc(loaded, 16)
                for k, v in enumerate((Wt, asrc, atrg, atp, b)):
                    sp.dma_start(rows[:, k, :], v.partition_broadcast(P)).then_inc(loaded, 16)

            @block.vector
            def _(dve):
                V = Vector(nc, dve, chain)
                dve.wait_ge(loaded, 16 * (6 + (Wskip is not None)))
                V.tt(tmp[:], rows[:, 0, :], rows[:, 3, :], ALU.mult)
                V.sum(ch[:], tmp[:].rearrange("p (h d) -> p h d", h=H))
                V.ts(pen[:], C.rec["D"][:, :, 1], 0.0, ALU.is_lt, -BIG, ALU.mult)
                V.tt(stp[:], C.rec["D"][:, :, 2].unsqueeze(2).to_broadcast([P, T, H]),
                     ch[:].unsqueeze(1).to_broadcast([P, T, H]), ALU.mult)
                V.tt(stp[:], stp[:], pen[:].unsqueeze(2).to_broadcast([P, T, H]), ALU.add)

        def finish(i, y):
            if Wskip is not None:
                nc.vector.tensor_copy(skip[:, bass.ds(i * NB, NB), :], y[:, :, F:M])
            return nc.vector.tensor_copy(tab[:, bass.ds(i * NB, NB), 0:F], y[:, :, 0:F])

        linear(nc, C, name + "l", [(h, w[:])], M, finish)
        with Phase(nc, name + "b") as ph:
            tmp = ph.sb("tmp", [P, NT, F])
            chain = ph.sem("chain")
            block = ph.block()

            @block.vector
            def _(dve):
                V = Vector(nc, dve, chain)
                for k, to in ((1, tab[:, :, F:WD]), (2, strg[:])):
                    V.tt(tmp[:], tab[:, :, 0:F], per_feature(rows[:, k, :]), ALU.mult)
                    V.sum(to, tmp[:].rearrange("p t (h d) -> p t h d", h=H))
                V.bf16_terms([strg3[:, q] for q in range(3)], strg[:])
        save_table(nc, C, name + "s", tab[:], table)
        gat_pass(nc, C, name + "p", table, H, strg3, stp, acc, macc, negm)
        with Phase(nc, name + "c") as ph:
            fac = ph.sb("fac", [P, NT])
            den = ph.sb("den", [P, NT, H])
            low = ph.sb("low", [P, NT, F])
            chain, asked, given = ph.sem("chain"), ph.sem("asked"), ph.sem("given")
            block = ph.block()

            @block.scalar
            def _(act):
                nc.scalar.activation(fac[:], macc[:], ACT.Exp, bias=negm[:]).then_inc(given, 1)
                act.wait_ge(asked, 1)
                nc.scalar.activation(low[:], low[:], ACT.Exp).then_inc(given, 1)

            @block.vector
            def _(dve):
                V = Vector(nc, dve, chain)
                dve.wait_ge(given, 1)
                bc = fac[:].unsqueeze(2).to_broadcast([P, NT, H])
                V.tt(den[:], acc[:, :, F:WD], bc, ALU.mult)
                V.ts(den[:], den[:], 1e-16, ALU.add)
                V.link(nc.vector.reciprocal(den[:], den[:]))
                V.tt(den[:], den[:], bc, ALU.mult)
                y = tab[:, :, 0:F]
                V.tt(y.rearrange("p t (h d) -> p t h d", h=H), acc[:, :, 0:F].rearrange("p t (h d) -> p t h d", h=H),
                     den[:].unsqueeze(3).to_broadcast([P, NT, H, D]), ALU.mult)
                V.tt(y, y, skip[:], ALU.add)
                V.tt(y, y, per_feature(rows[:, 4, :]), ALU.add)
                nc.vector.tensor_scalar(low[:], y, 0.0, None, ALU.min).then_inc(asked, 1)
                dve.wait_ge(given, 2)
                V.stt(h[:], y, 0.0, low[:], ALU.max, ALU.add)
                V.ts(h[:], h[:], -1.0, ALU.add)
                if last_x is not None:
                    V.tt(last_x[:], last_x[:], h[:], ALU.add)


def norm_phase(nc, C, name, x, h):
    with Phase(nc, name) as ph:
        tmp = ph.sb("tmp", [P, NT, F])
        stat = ph.sb("stat", [P, 3, NT])
        chain, to_root, rooted = ph.sem("chain"), ph.sem("to_root"), ph.sem("rooted")
        block = ph.block()

        @block.scalar
        def _(act):
            roots(nc, act, stat[:, 1], stat[:, 0], to_root, rooted)

        @block.vector
        def _(dve):
            normalized_relu(Vector(nc, dve, chain), dve, x, h, tmp, stat, to_root, rooted)


def gcn_layers(nc, C, name, a, x, h, table):
    L = 3
    with Phase(nc, name) as top:
        xc = [h] + [top.sb(f"xc{i}", [P, NT, F]) for i in range(1, L + 1)]
        ws = top.sb("ws", [P, L, F])
        bs = top.sb("bs", [P, L + 1, F])
        wout = top.sb("wout", [P, L + 1, F])
        gb = top.sb("gb", [P, 2, (L + 1), F])
        dinv = top.sb("dinv", [P, NT])
        ocnt = top.sb("ocnt", [P, NT])
        real = top.sb("real", [P, NT])
        with Phase(nc, name + "a") as ph:
            deg = ph.sb("deg", [P, 2, NT])
            loaded, chain, to_root, rooted = (ph.sem(v) for v in ("loaded", "chain", "to_root", "rooted"))
            block = ph.block()

            @block.scalar
            def _(act):
                roots(nc, act, deg[:, 0], dinv[:], to_root, rooted)

            @block.sync
            def _(sp):
                sp.dma_start(ws[:], a["L1_gnn_Ws"].rearrange("l k m -> k l m")).then_inc(loaded, 16)
                sp.dma_start(wout[:], a["L1_gnn_Wout"].rearrange("(l k) m -> k l m", k=P)).then_inc(loaded, 16)
                sp.dma_start(bs[:, 0:L, :], a["L1_gnn_bs"].partition_broadcast(P)).then_inc(loaded, 16)
                sp.dma_start(bs[:, L, :], a["L1_gnn_bout"].partition_broadcast(P)).then_inc(loaded, 16)
                for k, v in enumerate(("bn_gamma", "bn_beta")):
                    sp.dma_start(gb[:, k], a["L1_gnn_" + v].rearrange("(l f) -> l f", f=F).partition_broadcast(P)).then_inc(loaded, 16)
                sp.wait_ge(loaded, 96)

            @block.vector
            def _(dve):
                V = Vector(nc, dve, chain)
                nc.vector.tensor_scalar(deg[:, 0], C.cnt["D"][:], 1.0, None, ALU.add).then_inc(to_root, 1)
                dve.wait_ge(rooted, 1)
                V.inverse_root(deg[:, 0], dinv[:], deg[:, 1])
                V.ts(ocnt[:], C.cnt["S"][:], 1.0, ALU.max)
                V.link(nc.vector.reciprocal(ocnt[:], ocnt[:]))
                V.link(nc.vector.memset(real[:], 1.0))
                V.ts(real[:, NT - 1:NT], C.iota_col[:], float(LAST), ALU.is_lt)
        for l in range(L):
            with Phase(nc, f"{name}{l}") as lay:
                hd = lay.sb("hd", [P, NT, F])
                tau = lay.sb("tau", [P, NT, F])

                def finish(i, y):
                    d = dinv[:, bass.ds(i * NB, NB)].unsqueeze(2).to_broadcast([P, NB, F])
                    return nc.vector.tensor_tensor(hd[:, bass.ds(i * NB, NB), :], y, d, ALU.mult)

                linear(nc, C, f"{name}{l}l", [(xc[l], ws[:, l, :])], F, finish)
                save_table(nc, C, f"{name}{l}s", hd[:], table)
                sum_pass(nc, C, f"{name}{l}d", "D", table, tau)
                with Phase(nc, f"{name}{l}b") as ph:
                    chain = ph.sem("chain")
                    block = ph.block()

                    @block.vector
                    def _(dve):
                        V = Vector(nc, dve, chain)
                        V.tt(tau[:], tau[:], hd[:], ALU.add)
                        V.tt(tau[:], tau[:], per_node(dinv[:]), ALU.mult)
                        V.tt(tau[:], tau[:], per_feature(bs[:, l, :]), ALU.add)
                        V.ts(tau[:], tau[:], 0.0, ALU.max)
                save_table(nc, C, f"{name}{l}t", tau[:], table)
                with Phase(nc, f"{name}{l}g") as ph2:
                    acc = ph2.sb("acc", [P, NT, 2 * F])
                    sum_pass(nc, C, f"{name}{l}e", "S", table, acc, squares=True)
                    with Phase(nc, f"{name}{l}c") as ph:
                        chain, asked, given = ph.sem("chain"), ph.sem("asked"), ph.sem("given")
                        block = ph.block()

                        @block.scalar
                        def _(act):
                            act.wait_ge(asked, 1)
                            nc.scalar.activation(hd[:], hd[:], ACT.Tanh).then_inc(given, 1)

                        @block.vector
                        def _(dve):
                            V = Vector(nc, dve, chain)
                            V.tt(hd[:], tau[:], per_node(C.cnt["S"][:]), ALU.mult)
                            V.stt(hd[:], acc[:, :, 0:F], -2.0, hd[:], ALU.mult, ALU.add)
                            V.tt(hd[:], hd[:], tau[:], ALU.mult)
                            V.tt(hd[:], hd[:], acc[:, :, F:2 * F], ALU.add)
                            nc.vector.tensor_tensor(hd[:], hd[:], per_node(ocnt[:]), ALU.mult).then_inc(asked, 1)
                            dve.wait_ge(given, 1)
                            V.tt(tau[:], tau[:], xc[l][:], ALU.subtract)
                            V.tt(tau[:], tau[:], hd[:], ALU.mult)
                            V.tt(tau[:], tau[:], xc[l][:], ALU.add)
                            V.tt(xc[l + 1][:], tau[:], per_node(real[:]), ALU.mult)
        with Phase(nc, name + "n") as ph:
            tmp = ph.sb("tmp", [P, NT, F])
            part = ph.sb("part", [P, 2 * (L + 1), F])
            stat = ph.sb("stat", [P, F])
            var = ph.sb("var", [P, 2, F])
            p_s = ph.ps("p_s", [P, F])
            chain, asked, given, to_root, rooted = (ph.sem(v) for v in ("chain", "asked", "given", "to_root", "rooted"))
            block = ph.block()

            @block.scalar
            def _(act):
                roots(nc, act, var[:, 0], stat[:], to_root, rooted, L + 1)

            @block.vector
            def _(dve):
                V = Vector(nc, dve, chain)
                V.tt(h[:], h[:], per_node(real[:]), ALU.mult)
                for q in range(L + 1):
                    y = xc[q]
                    for s in range(2):
                        src = y if s == 0 else tmp
                        nc.vector.tensor_reduce(part[:, 2 * q + s, :], src[:].rearrange("p t f -> p f t"), AX.X,
                                                ALU.add).then_inc(asked, 1)
                        dve.wait_ge(given, 2 * q + s + 1)
                        if s == 0:
                            V.ts(stat[:], p_s[:], 1.0 / N, ALU.mult)
                            V.tt(y[:], y[:], per_feature(stat[:]), ALU.subtract)
                            V.tt(y[:], y[:], per_node(real[:]), ALU.mult)
                            V.tt(tmp[:], y[:], y[:], ALU.mult)
                        else:
                            nc.vector.tensor_scalar(var[:, 0], p_s[:], 1.0 / N, EPS, ALU.mult, ALU.add).then_inc(to_root, 1)
                            dve.wait_ge(rooted, q + 1)
                            V.inverse_root(var[:, 0], stat[:], var[:, 1])
                            V.tt(stat[:], stat[:], gb[:, 0, q, :], ALU.mult)
                            V.tt(y[:], y[:], per_feature(stat[:]), ALU.mult)
                            V.tt(y[:], y[:], per_feature(gb[:, 1, q, :]), ALU.add)

            @block.tensor
            def _(pe):
                for k in range(2 * (L + 1)):
                    pe.wait_ge(asked, k + 1)
                    nc.tensor.matmul(p_s[:], C.ones[:], part[:, k, :], start=True, stop=True).then_inc(given, 1)

        with Phase(nc, name + "o") as ph:
            y1 = ph.sb("y1", [P, NB, F])
            added = ph.sem("added")

            def finish(i, y):
                nc.vector.tensor_tensor(y1[:], y, bs[:, L, :].unsqueeze(1).to_broadcast([P, NB, F]), ALU.add).then_inc(added, 1)
                nc.vector.wait_ge(added, i + 1)
                at = x[:, bass.ds(i * NB, NB), :]
                return nc.vector.tensor_tensor(at, at, y1[:], ALU.add)

            linear(nc, C, name + "l", [(xc[q], wout[:, q, :]) for q in range(L + 1)], F, finish)


def attention_layer(nc, C, name, a, x, h):
    table = a["edge_attr_256"].rearrange("e (s f) -> (e s) f", s=2)
    with Phase(nc, name) as top:
        acc = top.sb("acc", [P, NT, F + 1])
        agg = top.sb("agg", [P, NT, F])
        ht = top.sb("ht", [P, NT, F])
        m = top.sb("m", [P, NT])
        w = top.sb("w", [P, 2, F])
        b = top.sb("b", [P, F])
        turn_nodes(nc, C, name + "t", h, ht)
        attention_pass(nc, C, name + "d", "D", table, ht, acc, m, True)
        attention_pass(nc, C, name + "s", "S", table, ht, acc, m, False)
        with Phase(nc, name + "a") as ph:
            den = ph.sb("den", [P, NT])
            loaded, chain = ph.sem("loaded"), ph.sem("chain")
            block = ph.block()

            @block.sync
            def _(sp):
                sp.dma_start(w[:], a["L2_gnn_W"].rearrange("(l k) m -> k l m", k=P)).then_inc(loaded, 16)
                sp.dma_start(b[:], a["L2_gnn_b"].partition_broadcast(P)).then_inc(loaded, 16)
                sp.wait_ge(loaded, 32)

            @block.vector
            def _(dve):
                V = Vector(nc, dve, chain)
                V.ts(den[:], acc[:, :, F], 1e-30, ALU.max)
                V.link(nc.vector.reciprocal(den[:], den[:]))
                V.tt(agg[:], acc[:, :, 0:F], per_node(den[:]), ALU.mult)

        with Phase(nc, name + "o") as ph:
            y1 = ph.sb("y1", [P, NB, F])
            added = ph.sem("added")

            def finish(i, y):
                nc.vector.tensor_tensor(y1[:], y, b[:].unsqueeze(1).to_broadcast([P, NB, F]), ALU.add).then_inc(added, 1)
                nc.vector.wait_ge(added, i + 1)
                at = x[:, bass.ds(i * NB, NB), :]
                return nc.vector.tensor_tensor(at, at, y1[:], ALU.add)

            linear(nc, C, name + "l", [(agg, w[:, 0, :]), (h, w[:, 1, :])], F, finish)


def filter_layer(nc, C, name, a, x, h, table):
    with Phase(nc, name) as top:
        agg = top.sb("agg", [P, NT, F])
        wt = top.sb("wt", [P, T])
        w = top.sb("w", [P, F])
        save_table(nc, C, name + "s", h[:], table)
        with Phase(nc, name + "a") as ph:
            sc = ph.sb("sc", [P, 4])
            v = ph.sb("v", [P, 3, T])
            ok = ph.sb("ok", [P, T])
            oki = ph.sb("oki", [P, T], dt.uint32)
            loaded, chain, asked, given = (ph.sem(x) for x in ("loaded", "chain", "asked", "given"))
            block = ph.block()

            @block.sync
            def _(sp):
                for k, n in enumerate(("log_scale", "filter_w", "filter_b")):
                    sp.dma_start(sc[:, k:k + 1], a["L3_gnn_" + n].partition_broadcast(P)).then_inc(loaded, 16)
                sp.dma_start(w[:], a["L3_gnn_W_mix"]).then_inc(loaded, 16)
                sp.wait_ge(loaded, 64)

            @block.scalar
            def _(act):
                act.wait_ge(loaded, 64)
                nc.scalar.activation(sc[:, 3:4], sc[:, 0:1], ACT.Exp).then_inc(given, 1)
                act.wait_ge(asked, 1)
                nc.scalar.activation(v[:, 0], v[:, 0], ACT.Exp, scale=-1.0).then_inc(given, 1)
                act.wait_ge(asked, 2)
                nc.scalar.activation(v[:, 1], v[:, 1], ACT.Exp, scale=-1.0).then_inc(given, 1)

            @block.vector
            def _(dve):
                V = Vector(nc, dve, chain)
                dve.wait_ge(loaded, 64)
                dve.wait_ge(given, 1)
                length = C.rec["D"][:, :, 3]
                V.ts(sc[:, 3:4], sc[:, 3:4], 1e-6, ALU.add)
                V.link(nc.vector.reciprocal(sc[:, 3:4], sc[:, 3:4]))
                V.ts(v[:, 2], length, sc[:, 3:4], ALU.mult, 0.0, ALU.max)
                nc.vector.tensor_tensor(v[:, 0], v[:, 2], v[:, 2], ALU.mult).then_inc(asked, 1)
                nc.vector.tensor_scalar(v[:, 1], length, sc[:, 1:2], sc[:, 2:3], ALU.mult, ALU.add).then_inc(asked, 1)
                dve.wait_ge(given, 3)
                V.ts(v[:, 1], v[:, 1], 1.0, ALU.add)
                V.link(nc.vector.reciprocal(v[:, 1], v[:, 1]))
                V.tt(v[:, 0], v[:, 0], v[:, 1], ALU.mult)
                V.ts(ok[:], v[:, 0], 3.4e38, ALU.is_le)
                V.ts(v[:, 1], v[:, 0], -3.4e38, ALU.is_ge)
                V.tt(oki[:], ok[:], v[:, 1], ALU.mult)
                V.link(nc.vector.memset(wt[:], 0.0))
                V.link(nc.vector.copy_predicated(wt[:], oki[:], v[:, 0]))

        sum_pass(nc, C, name + "d", "D", table, agg, weights=wt)
        with Phase(nc, name + "b") as ph:
            deg = ph.sb("deg", [P, NT])
            chain = ph.sem("chain")
            block = ph.block()

            @block.vector
            def _(dve):
                V = Vector(nc, dve, chain)
                V.ts(deg[:], C.cnt["D"][:], 1.0, ALU.max)
                V.link(nc.vector.reciprocal(deg[:], deg[:]))
                V.tt(agg[:], agg[:], per_node(deg[:]), ALU.mult)
                V.tt(x[:], x[:], h[:], ALU.add)

        def finish(i, y):
            at = x[:, bass.ds(i * NB, NB), :]
            return nc.vector.tensor_tensor(at, at, y, ALU.add)

        linear(nc, C, name + "l", [(agg, w[:])], F, finish)


class Shared:
    pass


def program(nc, a, out, upto=99):
    ctx = ExitStack()
    with ctx:
        def sb(name, shape, d=F32):
            return ctx.enter_context(nc.sbuf_tensor(name, shape, d))

        C = Shared()
        C.iota_row = sb("iota_row", [P, P])
        C.iota_col = sb("iota_col", [P, 1])
        C.ident = sb("ident", [P, P])
        C.ones = sb("ones", [P, P])
        C.before = sb("before", [P, P])
        C.zerosb = sb("zerosb", [P, P], BF16)
        PASSED[:] = [nc.alloc_semaphore("passed")]
        constants(nc, C)
        C.rec, C.nt, C.cnt, C.loc = {}, {}, {}, {}
        for s, key, other, row in (("D", "dst", "src", 0), ("S", "src", "dst", 1)):
            C.rec[s] = sb(f"rec{s}", [P, T, RW])
            C.nt[s] = sb(f"nt{s}", [P, NH], I32)
            C.cnt[s] = sb(f"cnt{s}", [P, NT])
            C.loc[s] = nc.dram_tensor(f"loc{s}", [T, P], F32).ap()
            recd = nc.dram_tensor(f"recd{s}", [SLOTS, RW], F32).ap()
            sort_edges(nc, C, f"sort{s}", a[key], a[other], row, a["edge_weight1"], a["edge_weight"], C.rec[s], C.nt[s],
                       C.cnt[s], C.loc[s], recd)
        x = sb("x_now", [P, NT, F])
        h = sb("h_now", [P, NT, F])
        t136 = nc.dram_tensor("table_heads", [NP, F + 8], F32).ap()
        t129 = nc.dram_tensor("table_head", [NP, F + 1], F32).ap()
        table = nc.dram_tensor("table", [NP, F], F32).ap()
        with Phase(nc, "in") as ph:
            loaded, cleared = ph.sem("loaded"), ph.sem("cleared")
            block = ph.block()

            @block.vector
            def _(dve):
                nc.vector.memset(x[:, NT - 1, :], 0.0).then_inc(cleared, 1)

            @block.sync
            def _(sp):
                sp.wait_ge(cleared, 1)
                whole = (NT - 1) * P
                sp.dma_start(x[:, 0:NT - 1, :], a["x"][0:whole, :].rearrange("(t p) f -> p t f", p=P)).then_inc(loaded, 16)
                sp.dma_start(x[0:LAST, NT - 1, :], a["x"][whole:N, :]).then_inc(loaded, 16)
                sp.wait_ge(loaded, 32)

        clear_semaphores(nc)
        norm_phase(nc, C, "ln0", x, h)
        g = lambda n: a["L0_gnn_" + n]
        if upto >= 2:
            gat_layer(nc, C, "gatA", a, g("W1"), g("Wt1"), g("a_src1"), g("a_trg1"), g("a_tp1"), g("b1"), g("Wskip1"), 8, x, h, t136)
            clear_semaphores(nc)
        if upto >= 3:
            gat_layer(nc, C, "gatB", a, g("W2"), g("Wt2"), g("a_src2"), g("a_trg2"), g("a_tp2"), g("b2"), None, 1, x, h, t129, x)
            clear_semaphores(nc)
            norm_phase(nc, C, "ln1", x, h)
        if upto >= 4:
            gcn_layers(nc, C, "gcn", a, x, h, table)
            clear_semaphores(nc)
            norm_phase(nc, C, "ln2", x, h)
        if upto >= 5:
            attention_layer(nc, C, "att", a, x, h)
            clear_semaphores(nc)
            norm_phase(nc, C, "ln3", x, h)
        if upto >= 6:
            filter_layer(nc, C, "fil", a, x, h, table)
        with Phase(nc, "out") as ph:
            stored = ph.sem("stored")
            block = ph.block()

            @block.sync
            def _(sp):
                whole = (NT - 1) * P
                sp.dma_start(out[0:whole, :].rearrange("(t p) f -> p t f", p=P), x[:, 0:NT - 1, :]).then_inc(stored, 16)
                sp.dma_start(out[whole:N, :], x[0:LAST, NT - 1, :]).then_inc(stored, 16)
                if upto < 6:
                    sp.dma_start(a["o_h"].rearrange("(t p) f -> p t f", p=P), h[:]).then_inc(stored, 16)
                sp.wait_ge(stored, 32 if upto >= 6 else 48)


_FLAT = ("edge_weight1", "L0_gnn_Wt1", "L0_gnn_a_src1", "L0_gnn_a_trg1", "L0_gnn_a_tp1", "L0_gnn_Wt2", "L0_gnn_a_src2",
         "L0_gnn_a_trg2", "L0_gnn_a_tp2", "L3_gnn_log_scale", "L3_gnn_filter_w", "L3_gnn_filter_b")


def kernel(**inputs):
    import numpy as _np
    import concourse.bacc as _bacc
    from concourse import mybir as _mybir
    from concourse.bass_utils import run_bass_kernel_spmd as _run

    nc = _bacc.Bacc("TRN2", target_bir_lowering=False, num_devices=1)
    arrays, aps = {}, {}
    for name, value in inputs.items():
        v = _np.ascontiguousarray(value)
        if name in _FLAT:
            v = v.reshape(-1)
        arrays[f"in_{name}"] = v
        aps[name] = nc.dram_tensor(f"in_{name}", v.shape, _mybir.dt.from_np(v.dtype), kind="ExternalInput").ap()
    out = nc.dram_tensor("out_x", (N, F), F32, kind="ExternalOutput").ap()
    program(nc, aps, out)
    r = _run(nc, [arrays], core_ids=[0])
    return r.results[0]["out_x"]
```

```python
import concourse.bass as bass
from concourse import mybir
from contextlib import ExitStack

dt = mybir.dt
F32, I32, BF16 = dt.float32, dt.int32, dt.bfloat16
ALU = mybir.AluOpType
ACT = mybir.ActivationFunctionType
AX = mybir.AxisListType

P = 128
N, E, F = 3125, 50000, 128
NT = -(-N // P)
NP = NT * P
LAST = N - (NT - 1) * P
G = 4
GS = G * P
U = 8
NG = -(-((E + NT * (P - 1)) // P) // (G * U)) * U
T = NG * G
TR = [(t, min(P, T - t)) for t in range(0, T, P)]
SLOTS = T * P
EC = E // P
ER = E - EC * P
CB = 14
CC = -(-(EC + 1) // (2 * CB)) * 2 * CB
RW = 8
BIG = 1.0e30
HUGE_SLOT = 1.0e6
NB = 5
EPS = 1e-5


class Chain:

    def __init__(self, eng, sem, base=0):
        self.eng, self.sem, self.base, self.n = eng, sem, base, 0

    def __call__(self, ins, wait=True):
        self.n += 1
        ins.then_inc(self.sem, 1)
        if wait:
            self.eng.wait_ge(self.sem, self.base + self.n)


def wait_apart(eng, sem, value):
    eng.wait_ge(sem, value)
    eng.sem_inc(PASSED[0], 1)


PASSED = []
SPENT = []


def clear_semaphores(nc):
    nc.clear_and_free_semaphores(SPENT)
    nc.all_engine_barrier()
    SPENT.clear()


class Phase:

    def __init__(self, nc, name):
        self.nc, self.name, self.ctx, self.sems = nc, name, ExitStack(), []

    def __enter__(self):
        self.ctx.__enter__()
        return self

    def __exit__(self, *e):
        return self.ctx.__exit__(*e)

    def sb(self, name, shape, d=F32):
        return self.ctx.enter_context(self.nc.sbuf_tensor(f"{self.name}_{name}", shape, d))

    def ps(self, name, shape, d=F32):
        return self.ctx.enter_context(self.nc.psum_tensor(f"{self.name}_{name}", shape, d))

    def sem(self, name):
        s = self.nc.alloc_semaphore(f"{self.name}_{name}")
        SPENT.append(s)
        return s

    def block(self):
        return self.ctx.enter_context(self.nc.Block())


def constants(nc, C):
    with Phase(nc, "cst") as ph:
        made = ph.sem("made")
        block = ph.block()

        @block.gpsimd
        def _(pool):
            link = Chain(pool, made)
            link(nc.gpsimd.iota(C.iota_row[:], [[1, P]], base=0, channel_multiplier=0,
                                allow_small_or_imprecise_dtypes=True))
            link(nc.gpsimd.iota(C.iota_col[:], [[0, 1]], base=0, channel_multiplier=1,
                                allow_small_or_imprecise_dtypes=True))
            link(nc.gpsimd.memset(C.ones[:], 1.0))
            link(nc.gpsimd.memset(C.ident[:], 0.0))
            link(nc.gpsimd.affine_select(out=C.ident[:], in_=C.ident[:], compare_op=ALU.not_equal, fill=1.0,
                                         base=0, pattern=[[-1, P]], channel_multiplier=1))
            link(nc.gpsimd.affine_select(out=C.before[:], in_=C.ones[:], compare_op=ALU.is_ge, fill=0.0,
                                         base=-1, pattern=[[1, P]], channel_multiplier=-1))
            link(nc.gpsimd.memset(C.zerosb[:], 0.0))


class SortedSide:

    def __init__(self, ph, side, key, other, attr_row, rec, ntile, count, loc_dram, rec_dram):
        self.key, self.other, self.attr_row = key, other, attr_row
        self.rec, self.ntile, self.count, self.loc_dram, self.rec_dram = rec, ntile, count, loc_dram, rec_dram

        def sb(name, shape, d=F32):
            return ph.sb(name + side, shape, d)

        self.keyi = sb("keyi", [P, CC], I32)
        self.otheri = sb("otheri", [P, CC], I32)
        self.w1f = sb("w1f", [P, CC])
        self.wf = sb("wf", [P, CC])
        self.bucket = sb("bucket", [P, CC], I32)
        self.bucketf = sb("bucketf", [P, CC])
        self.locf = sb("locf", [P, CC])
        self.slot = sb("slot", [P, CC])
        self.sloti = sb("sloti", [P, CC], I32)
        self.part = sb("part", [P, CC], I32)
        self.addr = sb("addr", [P, CC], I32)
        self.r = sb("r", [P, CC, RW])
        self.nta = sb("nta", [P, T])
        self.ring = sb("ring", [P, 2, CB], I32)
        self.rring = sb("rring", [P, 2, CB, RW])
        self.loct = sb("loct", [P, len(TR), P])
        self.p_tot = ph.ps("p_tot" + side, [P, 2, NT])
        self.p_cnt = ph.ps("p_cnt" + side, [P, NT])
        self.p_tr = ph.ps("p_tr" + side, [P, 4, P])
        names = ("loaded tot_ready tot_done low_ready counted filled made addr_ready ring_ready rec_loaded tr_ready "
                 "tr_done pad_stored loc_stored pads")
        (self.loaded, self.tot_ready, self.tot_done, self.low_ready, self.counted, self.filled, self.made,
         self.addr_ready, self.ring_ready, self.rec_loaded, self.tr_ready, self.tr_done, self.pad_stored,
         self.loc_stored, self.pads) = (ph.sem(x + side) for x in names.split())
        self.scattered = [ph.sem(f"scattered{side}{k}") for k in range(2)]


def sort_edges(nc, C, sides, w1, w):
    with Phase(nc, "sort") as ph:
        jobs = [SortedSide(ph, *what) for what in sides]
        zero = ph.sb("zero", [P, CC])
        mask = ph.sb("mask", [P, CC])
        cum = ph.sb("cum", [P, NT, CC])
        maskb = ph.sb("maskb", [P, CC, NT], BF16)
        low = ph.sb("low", [P, 2, CB, P], BF16)
        tot = ph.sb("tot", [P, NT])
        tots = ph.sb("tots", [P, 2, NT])
        toti = ph.sb("toti", [P, NT], I32)
        first = ph.sb("first", [P, NT])
        base = ph.sb("base", [P, NT])
        giota = ph.sb("giota", [P, T])
        chain, tiles_made = ph.sem("chain"), ph.sem("tiles_made")
        block = ph.block()
        blocks = CC // CB

        @block.sync
        def _(sp):
            for j in jobs:
                sp.wait_ge(j.filled, 1)
                for to, frm in ((j.keyi, j.key), (j.otheri, j.other), (j.w1f, w1), (j.wf, w)):
                    sp.dma_start(to[:, 0:EC], frm[0:EC * P].rearrange("(p c) -> p c", p=P)).then_inc(j.loaded, 16)
                    sp.dma_start(to[0:ER, EC:EC + 1], frm[EC * P:E].unsqueeze(1)).then_inc(j.loaded, 16)
            for j in jobs:
                sp.wait_ge(j.pads, 1)
                sp.dma_start(j.rec_dram.rearrange("(p t) w -> p (t w)", p=P),
                             j.rec[:].rearrange("p t w -> p (t w)")).then_inc(j.pad_stored, 16)
            for j in jobs:
                for k in range(2):
                    sp.wait_ge(j.scattered[k], 16 * CC // 2)
                sp.dma_start(j.rec[:].rearrange("p t w -> p (t w)"),
                             j.rec_dram.rearrange("(p t) w -> p (t w)", p=P)).then_inc(j.rec_loaded, 16)
                sp.wait_ge(j.tr_done, 1)
                for k, (t, n) in enumerate(TR):
                    sp.dma_start(j.loc_dram[t:t + n, :], j.loct[0:n, k, :]).then_inc(j.loc_stored, 16)
                sp.wait_ge(j.loc_stored, 16 * len(TR))

        @block.gpsimd
        def _(pool):
            nc.gpsimd.iota(giota[:], [[1, T]], base=0, channel_multiplier=0,
                           allow_small_or_imprecise_dtypes=True).then_inc(tiles_made, 1)
            for j in jobs:
                pool.wait_ge(j.filled, 1)
                nc.gpsimd.iota(j.r[:, 0:EC, 4].bitcast(I32), [[2, EC]], base=j.attr_row,
                               channel_multiplier=2 * EC).then_inc(j.made, 1)
                nc.gpsimd.iota(j.r[:, EC:EC + 1, 4].bitcast(I32), [[0, 1]], base=j.attr_row + 2 * EC * P,
                               channel_multiplier=2).then_inc(j.made, 1)
                pool.wait_ge(j.loaded, 8 * 16)
                nc.gpsimd.tensor_copy(j.r[:, :, 0].bitcast(I32), j.otheri[:]).then_inc(j.made, 1)
                nc.gpsimd.tensor_copy(j.r[:, :, 2], j.w1f[:]).then_inc(j.made, 1)
                nc.gpsimd.tensor_copy(j.r[:, :, 3], j.wf[:]).then_inc(j.made, 1)
                pool.wait_ge(j.made, 5)
            for j in jobs:
                pool.wait_ge(j.addr_ready, 1)
                pool.wait_ge(j.pad_stored, 16)

                def scatter(i, u):
                    c0 = i * (2 * CB) + u * CB
                    nc.gpsimd.tensor_copy(j.ring[:, u, :], j.addr[:, bass.ds(c0, CB)]).then_inc(j.ring_ready, 1)
                    nc.gpsimd.tensor_copy(j.rring[:, u, :, :], j.r[:, bass.ds(c0, CB), :]).then_inc(j.ring_ready, 1)
                    wait_apart(pool, j.ring_ready, i * 4 + 2 * u + 2)
                    for k in range(CB):
                        pool.indirect_dma_start(j.rec_dram, bass.IndirectOffsetOnAxis(ap=j.ring[:, u, k:k + 1], axis=0),
                                                j.rring[:, u, k, :], None, bounds_check=SLOTS - 1,
                                                oob_is_err=False).then_inc(j.scattered[u], 16)

                scatter(0, 0)
                scatter(0, 1)
                with pool.Fori(0, blocks // 2 - 1) as i:
                    for u in range(2):
                        wait_apart(pool, j.scattered[u], i * (16 * CB) + 16 * CB)
                        scatter(i + 1, u)

        @block.vector
        def _(dve):
            link = Chain(dve, chain)
            link(nc.vector.memset(zero[:], 0.0))
            for j in jobs:
                link(nc.vector.memset(j.keyi[:], NT * P))
                link(nc.vector.memset(j.otheri[:], 0))
                link(nc.vector.memset(j.w1f[:], 0.0))
                link(nc.vector.memset(j.wf[:], 0.0))
                link(nc.vector.memset(j.r[:], 0.0))
                nc.vector.tensor_copy(j.slot[:], zero[:]).then_inc(j.filled, 1)
                link(nc.vector.memset(j.nta[:], 0.0))
                link(nc.vector.memset(j.rec[:], 0.0))
                nc.vector.memset(j.rec[:, :, 1], -1.0).then_inc(j.pads, 1)
            for j in jobs:
                dve.wait_ge(j.filled, 1)
                dve.wait_ge(j.loaded, 8 * 16)
                link(nc.vector.tensor_single_scalar(j.bucket[:], j.keyi[:], 7, ALU.logical_shift_right))
                link(nc.vector.tensor_single_scalar(j.part[:], j.keyi[:], P - 1, ALU.bitwise_and))
                link(nc.vector.tensor_copy(j.bucketf[:], j.bucket[:]))
                link(nc.vector.tensor_copy(j.locf[:], j.part[:]))
                link(nc.vector.tensor_copy(j.r[:, :, 1], j.part[:]))
                for b in range(NT):
                    nc.vector.tensor_scalar(maskb[:, :, b], j.bucketf[:], float(b), None, ALU.is_equal)
                    link(nc.vector.tensor_scalar(mask[:], j.bucketf[:], float(b), None, ALU.is_equal))
                    link(nc.vector.tensor_tensor_scan(cum[:, b, :], mask[:], zero[:], 0.0, ALU.add, ALU.add))
                link(nc.vector.tensor_copy(tot[:], cum[:, :, CC - 1]))
                nc.vector.memset(low[:], 0.0).then_inc(j.tot_ready, 1)
                dve.wait_ge(j.tot_done, 1)
                link(nc.vector.tensor_copy(tots[:], j.p_tot[:]))
                link(nc.vector.tensor_scalar(first[:], tots[:, 1, :], float(P - 1), None, ALU.add))
                link(nc.vector.tensor_copy(toti[:], first[:]))
                link(nc.vector.tensor_single_scalar(toti[:], toti[:], P.bit_length() - 1, ALU.logical_shift_right))
                link(nc.vector.tensor_copy(tot[:], toti[:]))
                link(nc.vector.tensor_tensor_scan(first[:], tot[:], zero[:, 0:NT], 0.0, ALU.add, ALU.add))
                link(nc.vector.tensor_tensor(first[:], first[:], tot[:], ALU.subtract))
                link(nc.vector.scalar_tensor_tensor(base[:], first[:], float(P), tots[:, 0, :], ALU.mult, ALU.add))
                link(nc.vector.tensor_scalar(base[:], base[:], -1.0, None, ALU.add))
                for b in range(NT):
                    link(nc.vector.scalar_tensor_tensor(cum[:, b, :], cum[:, b, :], base[:, b:b + 1], maskb[:, :, b],
                                                        ALU.add, ALU.mult))
                    link(nc.vector.tensor_tensor(j.slot[:], j.slot[:], cum[:, b, :], ALU.add))
                link(nc.vector.tensor_copy(j.sloti[:], j.slot[:]))
                link(nc.vector.tensor_single_scalar(j.part[:], j.sloti[:], P - 1, ALU.bitwise_and))
                link(nc.vector.tensor_single_scalar(j.sloti[:], j.sloti[:], 7, ALU.logical_shift_right))
                link(nc.vector.tensor_copy(j.slot[:], j.part[:]))
                link(nc.vector.tensor_copy(mask[:], j.sloti[:]))
                link(nc.vector.scalar_tensor_tensor(j.slot[:], j.slot[:], float(T), mask[:], ALU.mult, ALU.add))
                link(nc.vector.tensor_scalar(mask[:], j.bucketf[:], float(NT), HUGE_SLOT, ALU.is_ge, ALU.mult))
                link(nc.vector.tensor_tensor(j.slot[:], j.slot[:], mask[:], ALU.add))
                nc.vector.tensor_copy(j.addr[:], j.slot[:]).then_inc(j.addr_ready, 1)
                dve.wait_ge(tiles_made, 1)
                for b in range(1, NT):
                    link(nc.vector.scalar_tensor_tensor(j.nta[:], giota[:], first[:, b:b + 1], j.nta[:], ALU.is_ge, ALU.add))
                link(nc.vector.tensor_copy(j.ntile[:], j.nta[:]))

                with dve.Fori(0, blocks // 2) as i:
                    for u in range(2):
                        dve.wait_ge(j.counted, i * 2 + u + 1)
                        nc.vector.tensor_tensor(low[:, u, :, :], C.iota_row[:].unsqueeze(1).to_broadcast([P, CB, P]),
                                                j.locf[:, bass.ds(i * (2 * CB) + u * CB, CB)].unsqueeze(2).to_broadcast([P, CB, P]),
                                                ALU.is_equal).then_inc(j.low_ready, 1)
                dve.wait_ge(j.counted, blocks + 3)
                link(nc.vector.tensor_copy(j.count[:], j.p_cnt[:]))
            for j in jobs:
                dve.wait_ge(j.tr_ready, 1)
                for k, (t, n) in enumerate(TR):
                    last = nc.vector.tensor_copy(j.loct[0:n, k, :], j.p_tr[0:n, k, :])
                last.then_inc(j.tr_done, 1)

        @block.tensor
        def _(pe):
            for j in jobs:
                pe.wait_ge(j.tot_ready, 1)
                nc.tensor.matmul(j.p_tot[:, 0, :], C.before[:], tot[:], start=True, stop=True)
                nc.tensor.matmul(j.p_tot[:, 1, :], C.ones[:], tot[:], start=True, stop=True).then_inc(j.tot_done, 1)
                nc.tensor.matmul(j.p_cnt[:], low[:, 0, 0, :], maskb[:, 0, :], start=True, stop=False).then_inc(j.counted, 1)
                pe.wait_ge(j.counted, 1)
                nc.tensor.nop().then_inc(j.counted, 1)
                with pe.Fori(0, blocks // 2) as i:
                    for u in range(2):
                        pe.wait_ge(j.low_ready, i * 2 + u + 1)
                        for k in range(CB):
                            last = nc.tensor.matmul(j.p_cnt[:], low[:, u, k, :],
                                                    maskb[:, bass.ds(i * (2 * CB) + u * CB + k, 1), :].squeeze(1),
                                                    start=False, stop=False)
                        last.then_inc(j.counted, 1)
                nc.tensor.matmul(j.p_cnt[:], C.zerosb[:], maskb[:, 0, :], start=False, stop=True).then_inc(j.counted, 1)
            for j in jobs:
                pe.wait_ge(j.rec_loaded, 16)
                for k, (t, n) in enumerate(TR):
                    last = nc.tensor.transpose(j.p_tr[0:n, k, :], j.rec[:, t:t + n, 1], C.ident[:])
                last.then_inc(j.tr_ready, 1)


def behind(i, u, d):
    return (i + (u + d) // U if (u + d) // U else i), (u + d) % U


def nth(i, u, per=1):
    return i * (U * per) + (u + 1) * per


def tiles(i, u):
    return bass.ds(i * (U * G) + u * G, G)


def gather_groups(nc, pool, ring, indexed, table, rows, gathered, used):
    def issue(i, u):
        wait_apart(pool, indexed, nth(i, u))
        for k in range(G):
            pool.indirect_dma_start(rows(u, k), None, table,
                                    bass.IndirectOffsetOnAxis(ap=ring[:, u, k:k + 1], axis=0)).then_inc(gathered[u], 16)

    for u in range(U):
        issue(0, u)
    with pool.Fori(1, NG // U) as i:
        for u in range(U):
            wait_apart(pool, used, nth(i - 1, u))
            issue(i, u)


def index_ring(nc, act, rec, word, ring, indexed):
    def index(i, u):
        nc.scalar.copy(ring[:, u, :], rec[:, tiles(i, u), word].bitcast(I32)).then_inc(indexed, 1)
    return index


def load_key_rows(sp, loc, rowb, loaded, used):
    def issue(i, u):
        keys = loc[tiles(i, u), :].rearrange("t p -> (t p)").partition_broadcast(P)
        sp.dma_start(rowb[:, u, :], keys).then_inc(loaded[u], 16)

    for u in range(U):
        issue(0, u)
    with sp.Fori(1, NG // U) as i:
        for u in range(U):
            sp.wait_ge(used, nth(i - 1, u))
            issue(i, u)


NODE_TILE_LOADS = [0]


def node_tiles(eng, C, side, i, u):
    NODE_TILE_LOADS[0] += 1
    regs = [eng.alloc_register(f"node_tile{NODE_TILE_LOADS[0]}_{s}") for s in range(G)]
    eng.load(regs, C.nt[side][0:1, tiles(i, u)])
    return [eng.snap(r, donate=True, min_val=0, max_val=NT - 1) for r in regs]


def one_hot(nc, C, side, out, i, u):
    keys = C.rec[side][:, tiles(i, u), 1].unsqueeze(2).to_broadcast([P, G, P])
    return nc.vector.tensor_tensor(out, C.iota_row[:].unsqueeze(1).to_broadcast([P, G, P]), keys, ALU.is_equal)


def turns(eng, step):
    for u in range(U):
        step(0, u, before=u)
    with eng.Fori(1, NG // U - 1) as i:
        for u in range(U):
            step(i, u)
    for u in range(U):
        step(NG // U - 1, u, left=U - 1 - u)


def tile_sums(nc, at, oh, rows):
    for k in range(G):
        last = nc.tensor.matmul(at(k), oh[:, k, :], rows[:, k, :], start=True, stop=True)
    return last


def sum_pass(nc, C, name, side, table, acc, squares=False, weights=None):
    W = 2 * F if squares else F
    with Phase(nc, name) as ph:
        g = ph.sb("g", [P, U, G, W])
        oh = ph.sb("oh", [P, U, G, P])
        ring = ph.sb("ring", [P, U, G], I32)
        ps = [ph.ps(f"ps{u % 2}", [P, G, 256]) for u in range(2)] * (U // 2)
        indexed, oh_ready, raw_ready, acc_done, acc_set, squared = (
            ph.sem(x) for x in ("indexed", "oh_ready", "raw_ready", "acc_done", "acc_set", "squared"))
        gathered = [ph.sem(f"gathered{u}") for u in range(U)]
        block = ph.block()

        @block.gpsimd
        def _(pool):
            gather_groups(nc, pool, ring, indexed, table, lambda u, k: g[:, u, k, 0:F], gathered, acc_done)

        @block.scalar
        def _(act):
            index = index_ring(nc, act, C.rec[side], 0, ring, indexed)

            def step(i, u, before=U, left=U):
                act.wait_ge(gathered[u], i * (16 * G) + 16 * G)
                if squares:
                    nc.scalar.activation(g[:, u, :, F:W], g[:, u, :, 0:F], ACT.Square).then_inc(squared, 1)

            for u in range(U):
                index(0, u)
            with act.Fori(0, NG // U - 1) as i:
                for u in range(U):
                    step(i, u)
                    index(i + 1, u)
            if squares:
                for u in range(U):
                    step(NG // U - 1, u)

        @block.vector
        def _(dve):
            nc.vector.memset(acc[:], 0.0).then_inc(acc_set, 1)

            def build(i, u):
                if weights is None:
                    one_hot(nc, C, side, oh[:, u], i, u).then_inc(oh_ready, 1)
                    return
                one_hot(nc, C, side, oh[:, u], i, u).then_inc(raw_ready, 1)
                dve.wait_ge(raw_ready, nth(i, u))
                w = weights[:, tiles(i, u)].unsqueeze(2).to_broadcast([P, G, P])
                nc.vector.tensor_tensor(oh[:, u], oh[:, u], w, ALU.mult).then_inc(oh_ready, 1)

            def step(i, u, before=U, left=U):
                if left:
                    build(*behind(i, u, 1))
                nt = node_tiles(dve, C, side, i, u)
                dve.wait_ge(acc_done, nth(i, u))
                for s in range(G):
                    dve.wait_ge(acc_set, nth(i, u, G) - G + 1 + s)
                    here = acc[:, bass.ds(nt[s], 1), :].squeeze(1)
                    nc.vector.tensor_tensor(here, here, ps[u][:, s, 0:W], ALU.add).then_inc(acc_set, 1)

            build(0, 0)
            turns(dve, step)

        @block.tensor
        def _(pe):
            with pe.Fori(0, NG // U) as i:
                for u in range(U):
                    pe.wait_ge(oh_ready, nth(i, u))
                    pe.wait_ge(gathered[u], i * (16 * G) + 16 * G)
                    if squares:
                        pe.wait_ge(squared, nth(i, u))
                    tile_sums(nc, lambda k: ps[u][:, k, 0:W], oh[:, u], g[:, u]).then_inc(acc_done, 1)


def gat_pass(nc, C, name, table, H, strg3, stp, acc, negm):
    W, D = F + H, F // H
    with Phase(nc, name) as ph:
        g = ph.sb("g", [P, U, G, W])
        msg = ph.sb("msg", [P, U, G, W])
        oh = ph.sb("oh", [P, U, G, P])
        oht = ph.sb("oht", [P, U, GS], BF16)
        rowb = ph.sb("rowb", [P, U, GS])
        ring = ph.sb("ring", [P, U, G], I32)
        z = ph.sb("z", [P, U, G, H])
        rm = ph.sb("rm", [P, 1])
        rrun = ph.sb("rrun", [P, 1])
        m1 = ph.sb("m1", [1, 1])
        nm = ph.sb("nm", [P, U])
        f = ph.sb("f", [P, U])
        ps = [ph.ps(f"ps{u % 2}", [P, G, 256]) for u in range(2)] * (U // 2)
        p_st = ph.ps("p_st", [P, 512])
        p_t = ph.ps("p_t", [P, P])
        p_m = ph.ps("p_m", [P, 1])
        names = ("indexed oht_ready oh_ready chain strg_done max_ready turned m1_ready spread negm_ready ex_ready "
                 "f_ready msg_ready acc_done acc_set")
        (indexed, oht_ready, oh_ready, chain, strg_done, max_ready, turned, m1_ready, spread, negm_ready, ex_ready,
         f_ready, msg_ready, acc_done, acc_set) = (ph.sem(x) for x in names.split())
        gathered = [ph.sem(f"gathered{u}") for u in range(U)]
        rows_loaded = [ph.sem(f"rows_loaded{u}") for u in range(U)]
        block = ph.block()

        @block.gpsimd
        def _(pool):
            gather_groups(nc, pool, ring, indexed, table, lambda u, k: g[:, u, k, :], gathered, msg_ready)

        @block.sync
        def _(sp):
            load_key_rows(sp, C.loc["D"], rowb, rows_loaded, oht_ready)

        @block.vector
        def _(dve):
            LINKS = 5
            nc.vector.memset(rrun[:], -BIG)
            nc.vector.memset(nm[:], BIG)
            nc.vector.memset(acc[:], 0.0).then_inc(acc_set, 1)
            dve.wait_ge(acc_set, 1)

            def turn_keys(i, u):
                dve.wait_ge(rows_loaded[u], i * 16 + 16)
                nc.vector.tensor_scalar(oht[:, u], rowb[:, u], C.iota_col[:], None, ALU.is_equal).then_inc(oht_ready, 1)

            def score(i, u):
                link = Chain(dve, chain, nth(i, u, LINKS) - LINKS)
                dve.wait_ge(gathered[u], i * (16 * G) + 16 * G)
                dve.wait_ge(strg_done, nth(i, u))
                terms = p_st[:, 0:G * 3 * H].rearrange("p (g q h) -> p g h q", g=G, q=3)
                link(nc.vector.tensor_reduce(z[:, u], terms, AX.X, ALU.add))
                link(nc.vector.tensor_tensor(z[:, u], z[:, u], g[:, u, :, F:W], ALU.add))
                link(nc.vector.tensor_tensor(z[:, u], z[:, u], stp[:, tiles(i, u), :], ALU.add))
                link(nc.vector.scalar_tensor_tensor(z[:, u], z[:, u], 0.2, z[:, u], ALU.mult, ALU.max))
                link(nc.vector.tensor_reduce(rm[:], z[:, u], AX.XY, ALU.max))
                nc.vector.tensor_tensor(rrun[:], rrun[:], rm[:], ALU.max).then_inc(max_ready, 1)

            def greatest(i, u):
                dve.wait_ge(turned, nth(i, u))
                nc.vector.tensor_reduce(m1[:], p_t[0:1, :], AX.X, ALU.max).then_inc(m1_ready, 1)

            def take_greatest(i, u):
                dve.wait_ge(spread, nth(i, u))
                nc.vector.tensor_scalar(nm[:, u:u + 1], p_m[:], -1.0, None, ALU.mult).then_inc(negm_ready, 1)

            def add(i, u, nt, s):
                if s == 0:
                    dve.wait_ge(acc_done, nth(i, u))
                    dve.wait_ge(f_ready, nth(i, u))
                dve.wait_ge(acc_set, nth(i, u, G) - G + 1 + s)
                here = acc[:, bass.ds(nt[s], 1), :].squeeze(1)
                if s == 0:
                    put = nc.vector.scalar_tensor_tensor(here, here, f[:, u:u + 1], ps[u][:, s, 0:W], ALU.mult, ALU.add)
                else:
                    put = nc.vector.tensor_tensor(here, here, ps[u][:, s, 0:W], ALU.add)
                put.then_inc(acc_set, 1)

            def match_keys(i, u):
                one_hot(nc, C, "D", oh[:, u], i, u).then_inc(oh_ready, 1)

            def step(i, u, before=U, left=U):
                dve.wait_ge(ex_ready, nth(i, u))
                nc.vector.tensor_tensor(msg[:, u, :, 0:F].rearrange("p g (h d) -> p g h d", h=H),
                                        g[:, u, :, 0:F].rearrange("p g (h d) -> p g h d", h=H),
                                        msg[:, u, :, F:W].unsqueeze(3).to_broadcast([P, G, H, D]),
                                        ALU.mult).then_inc(msg_ready, 1)
                if before >= 1:
                    last_group = behind(i, u, -1)
                    nt = node_tiles(dve, C, "D", *last_group)
                    add(*last_group, nt, 0)
                if left >= 1:
                    greatest(*behind(i, u, 1))
                if before >= 1:
                    add(*last_group, nt, 1)
                if left >= 3:
                    turn_keys(*behind(i, u, 3))
                if before >= 1:
                    add(*last_group, nt, 2)
                if left >= 1:
                    match_keys(*behind(i, u, 1))
                if before >= 1:
                    add(*last_group, nt, 3)
                if left >= 1:
                    take_greatest(*behind(i, u, 1))
                if left >= 2:
                    score(*behind(i, u, 2))

            turn_keys(0, 0)
            score(0, 0)
            greatest(0, 0)
            turn_keys(0, 1)
            take_greatest(0, 0)
            score(0, 1)
            turn_keys(0, 2)
            match_keys(0, 0)
            turns(dve, step)
            nt = node_tiles(dve, C, "D", NG // U - 1, U - 1)
            for s in range(G):
                add(NG // U - 1, U - 1, nt, s)

        @block.scalar
        def _(act):
            index = index_ring(nc, act, C.rec["D"], 0, ring, indexed)

            def step(i, u):
                act.wait_ge(negm_ready, nth(i, u))
                nc.scalar.activation(msg[:, u, :, F:W], z[:, u], ACT.Exp, bias=nm[:, u:u + 1]).then_inc(ex_ready, 1)
                nc.scalar.activation(f[:, u:u + 1], nm[:, (u - 1) % U:(u - 1) % U + 1], ACT.Exp, bias=nm[:, u:u + 1],
                                     scale=-1.0).then_inc(f_ready, 1)
                nc.scalar.copy(negm[:, bass.ds(i * U + u, 1)], nm[:, u:u + 1])

            for u in range(U):
                index(0, u)
            with act.Fori(0, NG // U - 1) as i:
                for u in range(U):
                    step(i, u)
                    index(i + 1, u)
            for u in range(U):
                step(NG // U - 1, u)

        @block.tensor
        def _(pe):
            def ahead(i, u):
                nt = node_tiles(pe, C, "D", i, u)
                pe.wait_ge(oht_ready, nth(i, u))
                for k in range(G):
                    last = nc.tensor.matmul(p_st[:, k * 3 * H:(k + 1) * 3 * H], oht[:, u, k * P:(k + 1) * P],
                                            strg3[:, bass.ds(nt[k], 1), :].squeeze(1), start=True, stop=True)
                last.then_inc(strg_done, 1)

            def turn_max(i, u):
                pe.wait_ge(max_ready, nth(i, u))
                nc.tensor.transpose(p_t[0:1, :], rrun[:], C.ident[:]).then_inc(turned, 1)

            def spread_max(i, u):
                pe.wait_ge(m1_ready, nth(i, u))
                nc.tensor.matmul(p_m[:], C.ones[0:1, :], m1[:], start=True, stop=True).then_inc(spread, 1)

            def step(i, u, before=U, left=U):
                if left >= 2:
                    ahead(*behind(i, u, 2))
                if left >= 1:
                    spread_max(*behind(i, u, 1))
                pe.wait_ge(oh_ready, nth(i, u))
                pe.wait_ge(msg_ready, nth(i, u))
                tile_sums(nc, lambda k: ps[u][:, k, 0:W], oh[:, u], msg[:, u]).then_inc(acc_done, 1)
                if left >= 2:
                    turn_max(*behind(i, u, 2))

            ahead(0, 0)
            turn_max(0, 0)
            spread_max(0, 0)
            ahead(0, 1)
            turn_max(0, 1)
            turns(pe, step)


def attention_pass(nc, C, name, side, table, ht, acc, run, cont):
    W = F + 1
    SCALE = float(F) ** -0.5
    with Phase(nc, name) as ph:
        g = ph.sb("g", [P, U, G, W])
        gt = ph.sb("gt", [P, 2, GS])
        hts = ph.sb("hts", [P, 2, G, P])
        pen = ph.sb("pen", [P, 2, GS])
        low = ph.sb("low", [P, 2, GS])
        e = ph.sb("e", [P, 2, GS])
        wt = ph.sb("wt", [P, 2, G, P])
        rowb = ph.sb("rowb", [P, U, GS])
        ring = ph.sb("ring", [P, U, G], I32)
        mt = ph.sb("mt", [P, G])
        old = ph.sb("old", [P, G])
        nmn = ph.sb("nmn", [P, U, G])
        df = ph.sb("df", [P, U, G])
        f = ph.sb("f", [P, U, G])
        ps = [ph.ps(f"ps{u % 2}", [P, G, 256]) for u in range(2)] * (U // 2)
        p_g = [ph.ps(f"p_g{u}", [P, GS]) for u in range(2)]
        p_l = ph.ps("p_l", [P, GS])
        p_w = ph.ps("p_w", [P, G, P])
        names = ("indexed opened chain turned gt_ready hts_ready pen_ready products m_ready f_ready e_ready "
                 "weights_turned wt_ready acc_done acc_set")
        (indexed, opened, chain, turned, gt_ready, hts_ready, pen_ready, products, m_ready, f_ready, e_ready,
         weights_turned, wt_ready, acc_done, acc_set) = (ph.sem(x) for x in names.split())
        gathered = [ph.sem(f"gathered{u}") for u in range(U)]
        rows_loaded = [ph.sem(f"rows_loaded{u}") for u in range(U)]
        block = ph.block()

        @block.gpsimd
        def _(pool):
            gather_groups(nc, pool, ring, indexed, table, lambda u, k: g[:, u, k, 0:F], gathered, acc_done)

        @block.sync
        def _(sp):
            load_key_rows(sp, C.loc[side], rowb, rows_loaded, pen_ready)

        @block.vector
        def _(dve):
            START, LINKS = 3, 3
            nc.vector.memset(g[:, :, :, F:W], 1.0).then_inc(opened, 1)
            nc.vector.memset(run[:, 0:1], -BIG)
            link = Chain(dve, chain)
            link(nc.vector.memset(cont[:], 0.0))
            link(nc.vector.tensor_tensor(cont[:, 1:T], C.nt[side][:, 1:T], C.nt[side][:, 0:T - 1], ALU.not_equal))
            link(nc.vector.tensor_scalar(cont[:], cont[:], -2.0 * BIG, None, ALU.mult))
            nc.vector.memset(acc[:], 0.0).then_inc(acc_set, 1)
            dve.wait_ge(acc_set, 1)

            def penalty(i, u):
                dve.wait_ge(rows_loaded[u], i * 16 + 16)
                nc.vector.tensor_scalar(pen[:, u % 2], rowb[:, u], C.iota_col[:], -4.0 * BIG, ALU.not_equal,
                                        ALU.mult).then_inc(pen_ready, 1)

            def add(i, u, nt, s):
                if s == 0:
                    dve.wait_ge(acc_done, nth(i, u))
                    dve.wait_ge(f_ready, nth(i, u))
                dve.wait_ge(acc_set, nth(i, u, G) - G + 1 + s)
                here = acc[:, bass.ds(nt[s], 1), :].squeeze(1)
                nc.vector.scalar_tensor_tensor(here, here, f[:, u, s:s + 1], ps[u][:, s, 0:W], ALU.mult,
                                               ALU.add).then_inc(acc_set, 1)

            def take_weights(i, u):
                dve.wait_ge(weights_turned, nth(i, u))
                nc.vector.tensor_copy(wt[:, u % 2], p_w[:]).then_inc(wt_ready, 1)

            def greatest(i, u, add_last):
                done = nth(i, u, LINKS) - LINKS + START
                dve.wait_ge(pen_ready, nth(i, u))
                wait_apart(dve, products, nth(i, u))
                for k in range(G):
                    tile = slice(k * P, (k + 1) * P)
                    most = nc.vector.tensor_tensor_reduce(out=low[:, u % 2, tile], in0=p_l[:, tile], in1=pen[:, u % 2, tile],
                                                          scale=1.0, scalar=-BIG, op0=ALU.add, op1=ALU.max,
                                                          accum_out=mt[:, k:k + 1])
                most.then_inc(chain, 1)
                add_last()
                t0 = i * (U * G) + u * G
                dve.wait_ge(chain, done + 1)
                nc.vector.tensor_tensor_scan(run[:, bass.ds(t0 + 1, G)], cont[:, bass.ds(t0, G)], mt[:],
                                             run[:, bass.ds(t0, 1)], ALU.add, ALU.max).then_inc(chain, 1)
                dve.wait_ge(chain, done + 2)
                nc.vector.tensor_tensor(old[:], run[:, bass.ds(t0, G)], cont[:, bass.ds(t0, G)], ALU.add).then_inc(chain, 1)
                nc.vector.tensor_scalar(nmn[:, u], run[:, bass.ds(t0 + 1, G)], -SCALE, None, ALU.mult)
                dve.wait_ge(chain, done + 3)
                nc.vector.tensor_tensor(df[:, u], old[:], run[:, bass.ds(t0 + 1, G)], ALU.subtract).then_inc(m_ready, 1)

            def step(i, u, before=U, left=U):
                adding = before >= 3
                if adding:
                    back = behind(i, u, -3)
                    nt = node_tiles(dve, C, side, *back)
                    add(*back, nt, 0)
                if left >= 1:
                    penalty(*behind(i, u, 1))
                if adding:
                    add(*back, nt, 1)
                greatest(i, u, lambda: add(*back, nt, 2) if adding else None)
                if adding:
                    add(*back, nt, 3)
                if before >= 1:
                    take_weights(*behind(i, u, -1))

            penalty(0, 0)
            turns(dve, step)
            for u in (U - 3, U - 2, U - 1):
                if u == U - 1:
                    take_weights(NG // U - 1, U - 1)
                nt = node_tiles(dve, C, side, NG // U - 1, u)
                for s in range(G):
                    add(NG // U - 1, u, nt, s)

        @block.scalar
        def _(act):
            index = index_ring(nc, act, C.rec[side], 4, ring, indexed)

            def take_rows(i, u):
                act.wait_ge(turned, nth(i, u))
                nc.scalar.copy(gt[:, u % 2], p_g[u % 2][:]).then_inc(gt_ready, 1)

            def take_nodes(i, u):
                nt = node_tiles(act, C, side, i, u)
                for k in range(G):
                    last = nc.scalar.copy(hts[:, u % 2, k, :], ht[:, bass.ds(nt[k], 1), :].squeeze(1))
                last.then_inc(hts_ready, 1)

            def step(i, u, before=U, left=U, index_next=True):
                if left >= 1:
                    take_nodes(*behind(i, u, 1))
                    take_rows(*behind(i, u, 1))
                act.wait_ge(m_ready, nth(i, u))
                for k in range(G):
                    tile = slice(k * P, (k + 1) * P)
                    ex = nc.scalar.activation(e[:, u % 2, tile], low[:, u % 2, tile], ACT.Exp, bias=nmn[:, u, k:k + 1], scale=SCALE)
                ex.then_inc(e_ready, 1)
                nc.scalar.activation(f[:, u], df[:, u], ACT.Exp, scale=SCALE).then_inc(f_ready, 1)
                if index_next:
                    act.wait_ge(gathered[u], i * (16 * G) + 16 * G)
                    index(i + 1, u)

            for u in range(U):
                index(0, u)
            take_nodes(0, 0)
            take_rows(0, 0)
            with act.Fori(0, NG // U - 1) as i:
                for u in range(U):
                    step(i, u)
            for u in range(U):
                step(NG // U - 1, u, left=U - 1 - u, index_next=False)

        @block.tensor
        def _(pe):
            def turn_rows(i, u):
                pe.wait_ge(gathered[u], i * (16 * G) + 16 * G)
                for k in range(G):
                    last = nc.tensor.transpose(p_g[u % 2][:, k * P:(k + 1) * P], g[:, u, k, 0:F], C.ident[:])
                last.then_inc(turned, 1)

            def turn_weights(i, u):
                pe.wait_ge(e_ready, nth(i, u))
                for k in range(G):
                    last = nc.tensor.transpose(p_w[:, k, :], e[:, u % 2, k * P:(k + 1) * P], C.ident[:])
                last.then_inc(weights_turned, 1)

            def multiply(i, u):
                pe.wait_ge(hts_ready, nth(i, u))
                pe.wait_ge(gt_ready, nth(i, u))
                for k in range(G):
                    tile = slice(k * P, (k + 1) * P)
                    last = nc.tensor.matmul(p_l[:, tile], hts[:, u % 2, k, :], gt[:, u % 2, tile], start=True, stop=True)
                last.then_inc(products, 1)

            def sums(i, u):
                pe.wait_ge(wt_ready, nth(i, u))
                tile_sums(nc, lambda k: ps[u][:, k, 0:W], wt[:, u % 2], g[:, u]).then_inc(acc_done, 1)

            def step(i, u, before=U, left=U):
                if before >= 1:
                    pe.wait_ge(m_ready, nth(*behind(i, u, -1)))
                multiply(i, u)
                if left >= 1:
                    turn_rows(*behind(i, u, 1))
                if before >= 2:
                    sums(*behind(i, u, -2))
                if before >= 1:
                    turn_weights(*behind(i, u, -1))

            pe.wait_ge(opened, 1)
            turn_rows(0, 0)
            turns(pe, step)
            sums(NG // U - 1, U - 2)
            turn_weights(NG // U - 1, U - 1)
            sums(NG // U - 1, U - 1)


def turn_nodes(nc, C, name, h, ht):
    with Phase(nc, name) as ph:
        p_h = [ph.ps(f"p_h{q}", [P, 512]) for q in range(2)]
        turned, taken = ph.sem("turned"), ph.sem("taken")
        block = ph.block()

        @block.tensor
        def _(pe):
            for t in range(NT):
                if t % 4 == 0 and t >= 8:
                    pe.wait_ge(taken, t // 4 - 1)
                nc.tensor.transpose(p_h[t // 4 % 2][:, t % 4 * P:(t % 4 + 1) * P], h[:, t, :], C.ident[:]).then_inc(turned, 1)

        @block.scalar
        def _(act):
            for t in range(0, NT, 4):
                n = min(4, NT - t)
                act.wait_ge(turned, t + n)
                nc.scalar.copy(ht[:, t:t + n, :], p_h[t // 4 % 2][:, 0:n * P].rearrange("p (t n) -> p t n", n=P)).then_inc(taken, 1)


def linear(nc, C, name, parts, M, finish, store=None):
    with Phase(nc, name) as ph:
        K = len(parts)
        BATCHES = NT // NB
        xs = ph.sb("xs", [P, K, NB, F])
        xt = ph.sb("xt", [P, K, NB, P])
        p_t = [ph.ps(f"p_t{q}", [P, 8, P]) for q in range(min(K, 2))]
        p_y = ph.ps("p_y", [P, 8, 256])
        staged, turned, xt_ready, multiplied, finished, stored = (
            ph.sem(x) for x in ("staged", "turned", "xt_ready", "multiplied", "finished", "stored"))
        block = ph.block()

        if store is not None:
            @block.sync
            def _(sp):
                rows, table = store
                with sp.Fori(0, BATCHES) as i:
                    sp.wait_ge(finished, i + 1)
                    sp.dma_start(table.rearrange("(t p) w -> p t w", p=P)[:, bass.ds(i * NB, NB), :],
                                 rows[:, bass.ds(i * NB, NB), :]).then_inc(stored, 16)
                sp.wait_ge(stored, 16 * BATCHES)

        @block.vector
        def _(dve):
            def stage(i):
                for q, (x, _) in enumerate(parts):
                    nc.vector.tensor_copy(xs[:, q], x[:, bass.ds(i * NB, NB), :]).then_inc(staged, 1)

            stage(0)
            with dve.Fori(0, BATCHES - 1) as i:
                wait_apart(dve, turned, i * K + K)
                stage(i + 1)
                wait_apart(dve, multiplied, i + 1)
                finish(i, p_y[:, 0:NB, 0:M]).then_inc(finished, 1)
            dve.wait_ge(multiplied, BATCHES)
            finish(BATCHES - 1, p_y[:, 0:NB, 0:M]).then_inc(finished, 1)

        @block.scalar
        def _(act):
            def take(i):
                for q in range(K):
                    act.wait_ge(turned, i * K + q + 1)
                    nc.scalar.copy(xt[:, q], p_t[q % 2][:, 0:NB, :]).then_inc(xt_ready, 1)

            take(0)
            with act.Fori(1, BATCHES) as i:
                wait_apart(act, multiplied, i)
                take(i)

        @block.tensor
        def _(pe):
            def turn(i):
                for q in range(K):
                    pe.wait_ge(staged, i * K + q + 1)
                    if q >= 2:
                        pe.wait_ge(xt_ready, i * K + q - 1)
                    for k in range(NB):
                        last = nc.tensor.transpose(p_t[q % 2][:, k, :], xs[:, q, k, :], C.ident[:])
                    last.then_inc(turned, 1)

            def multiply():
                for k in range(NB):
                    for q, (_, w) in enumerate(parts):
                        last = nc.tensor.matmul(p_y[:, k, 0:M], xt[:, q, k, :], w, start=(q == 0), stop=(q == K - 1))
                last.then_inc(multiplied, 1)

            turn(0)
            pe.wait_ge(xt_ready, K)
            if K <= 2:
                turn(1)
            multiply()
            if K > 2:
                turn(1)
            with pe.Fori(1, BATCHES - 1) as i:
                pe.wait_ge(xt_ready, i * K + K)
                if K <= 2:
                    turn(i + 1)
                pe.wait_ge(finished, i)
                multiply()
                if K > 2:
                    turn(i + 1)
            pe.wait_ge(xt_ready, BATCHES * K)
            pe.wait_ge(finished, BATCHES - 1)
            multiply()


def per_node(v):
    return v.unsqueeze(2).to_broadcast([P, NT, F])


def per_feature(v):
    return v.unsqueeze(1).to_broadcast([P, NT, F])


class Vector:

    def __init__(self, nc, dve, sem):
        self.v, self.link = nc.vector, Chain(dve, sem)

    def tt(self, out, a, b, op):
        self.link(self.v.tensor_tensor(out, a, b, op))

    def ts(self, out, a, s1, op0, s2=None, op1=ALU.bypass):
        if s2 is None:
            self.link(self.v.tensor_scalar(out, a, s1, None, op0))
        else:
            self.link(self.v.tensor_scalar(out, a, s1, s2, op0, op1))

    def stt(self, out, a, s, b, op0, op1):
        self.link(self.v.scalar_tensor_tensor(out, a, s, b, op0, op1))

    def inverse_root(self, v, root, tmp):
        self.link(self.v.reciprocal(root, root))
        self.tt(tmp, root, root, ALU.mult)
        self.tt(tmp, tmp, v, ALU.mult)
        self.ts(tmp, tmp, -0.5, ALU.mult, 1.5, ALU.add)
        self.tt(root, root, tmp, ALU.mult)

    def bf16_terms(self, terms, a):
        for t in terms[:-1]:
            self.link(self.v.tensor_copy(t, a))
            self.tt(a, a, t, ALU.subtract)
        self.link(self.v.tensor_copy(terms[-1], a))

    def sum(self, out, a):
        self.link(self.v.tensor_reduce(out, a, AX.X, ALU.add))


def roots(nc, act, v, root, asked, rooted, times=1):
    for k in range(times):
        act.wait_ge(asked, k + 1)
        nc.scalar.activation(root, v, ACT.Sqrt).then_inc(rooted, 1)


def normalized_relu(V, dve, x, h, tmp, stat, to_root, rooted):
    V.sum(stat[:, 0], x[:])
    V.ts(stat[:, 0], stat[:, 0], 1.0 / F, ALU.mult)
    V.tt(h[:], x[:], per_node(stat[:, 0]), ALU.subtract)
    V.tt(tmp[:], h[:], h[:], ALU.mult)
    V.sum(stat[:, 1], tmp[:])
    V.v.tensor_scalar(stat[:, 1], stat[:, 1], 1.0 / F, EPS, ALU.mult, ALU.add).then_inc(to_root, 1)
    dve.wait_ge(rooted, 1)
    V.inverse_root(stat[:, 1], stat[:, 0], stat[:, 2])
    V.stt(h[:], h[:], 0.0, per_node(stat[:, 0]), ALU.max, ALU.mult)


def save_table(nc, C, name, rows, table):
    with Phase(nc, name) as ph:
        stored = ph.sem("stored")
        block = ph.block()

        @block.sync
        def _(sp):
            sp.dma_start(table.rearrange("(t p) w -> p t w", p=P), rows).then_inc(stored, 16)
            sp.wait_ge(stored, 16)


def gat_layer(nc, C, name, a, W, Wt, asrc, atrg, atp, b, Wskip, H, x, h, table, last_x=None):
    D, WD = F // H, F + H
    with Phase(nc, name) as top:
        tab = top.sb("tab", [P, NT, WD])
        skip = top.sb("skip", [P, NT, F]) if Wskip is not None else h
        acc = top.sb("acc", [P, NT, WD])
        strg = top.sb("strg", [P, NT, H])
        strg3 = top.sb("strg3", [P, NT, 3 * H], BF16)
        negm = top.sb("negm", [P, NG])
        stp = top.sb("stp", [P, T, H])
        rows = top.sb("rows", [P, 5, F])
        M = 2 * F if Wskip is not None else F
        w = top.sb("w", [P, M])
        ch = top.sb("ch", [P, H])
        pen = top.sb("pen", [P, T])
        with Phase(nc, name + "a") as ph:
            tmp = ph.sb("tmp", [P, F])
            loaded, chain = ph.sem("loaded"), ph.sem("chain")
            block = ph.block()

            @block.sync
            def _(sp):
                sp.dma_start(w[:, 0:F], W).then_inc(loaded, 16)
                if Wskip is not None:
                    sp.dma_start(w[:, F:M], Wskip).then_inc(loaded, 16)
                for k, v in enumerate((Wt, asrc, atrg, atp, b)):
                    sp.dma_start(rows[:, k, :], v.partition_broadcast(P)).then_inc(loaded, 16)

            @block.vector
            def _(dve):
                V = Vector(nc, dve, chain)
                dve.wait_ge(loaded, 16 * (6 + (Wskip is not None)))
                V.tt(tmp[:], rows[:, 0, :], rows[:, 3, :], ALU.mult)
                V.sum(ch[:], tmp[:].rearrange("p (h d) -> p h d", h=H))
                V.ts(pen[:], C.rec["D"][:, :, 1], 0.0, ALU.is_lt, -BIG, ALU.mult)
                V.tt(stp[:], C.rec["D"][:, :, 2].unsqueeze(2).to_broadcast([P, T, H]),
                     ch[:].unsqueeze(1).to_broadcast([P, T, H]), ALU.mult)
                V.tt(stp[:], stp[:], pen[:].unsqueeze(2).to_broadcast([P, T, H]), ALU.add)

        def finish(i, y):
            if Wskip is not None:
                nc.vector.tensor_copy(skip[:, bass.ds(i * NB, NB), :], y[:, :, F:M])
            return nc.vector.tensor_copy(tab[:, bass.ds(i * NB, NB), 0:F], y[:, :, 0:F])

        linear(nc, C, name + "l", [(h, w[:])], M, finish)
        with Phase(nc, name + "b") as ph:
            tmp = ph.sb("tmp", [P, NT, F])
            chain = ph.sem("chain")
            block = ph.block()

            @block.vector
            def _(dve):
                V = Vector(nc, dve, chain)
                for k, to in ((1, tab[:, :, F:WD]), (2, strg[:])):
                    V.tt(tmp[:], tab[:, :, 0:F], per_feature(rows[:, k, :]), ALU.mult)
                    V.sum(to, tmp[:].rearrange("p t (h d) -> p t h d", h=H))
                V.bf16_terms([strg3[:, :, q * H:(q + 1) * H] for q in range(3)], strg[:])
        save_table(nc, C, name + "s", tab[:], table)
        gat_pass(nc, C, name + "p", table, H, strg3, stp, acc, negm)
        with Phase(nc, name + "c") as ph:
            fac = ph.sb("fac", [P, NT])
            start = ph.sb("start", [P, NG])
            late = ph.sb("late", [P, NT, NG])
            den = ph.sb("den", [P, NT, H])
            low = ph.sb("low", [P, NT, F])
            chain, asked, given = ph.sem("chain"), ph.sem("asked"), ph.sem("given")
            block = ph.block()

            @block.scalar
            def _(act):
                act.wait_ge(asked, 1)
                nc.scalar.activation(fac[:], fac[:], ACT.Exp, bias=negm[:, NG - 1:NG], scale=-1.0).then_inc(given, 1)
                act.wait_ge(asked, 2)
                nc.scalar.activation(low[:], low[:], ACT.Exp).then_inc(given, 1)

            @block.vector
            def _(dve):
                V = Vector(nc, dve, chain)
                V.link(nc.vector.tensor_copy(start[:], C.nt["D"][:].rearrange("p (j g) -> p j g", g=G)[:, :, 0]))
                V.tt(late[:], start[:].unsqueeze(1).to_broadcast([P, NT, NG]),
                     C.iota_row[:, 0:NT].unsqueeze(2).to_broadcast([P, NT, NG]), ALU.is_gt)
                V.stt(late[:], late[:], BIG, negm[:].unsqueeze(1).to_broadcast([P, NT, NG]), ALU.mult, ALU.add)
                nc.vector.tensor_reduce(fac[:], late[:], AX.X, ALU.min).then_inc(asked, 1)
                dve.wait_ge(given, 1)
                bc = fac[:].unsqueeze(2).to_broadcast([P, NT, H])
                V.tt(den[:], acc[:, :, F:WD], bc, ALU.mult)
                V.ts(den[:], den[:], 1e-16, ALU.add)
                V.link(nc.vector.reciprocal(den[:], den[:]))
                V.tt(den[:], den[:], bc, ALU.mult)
                y = tab[:, :, 0:F]
                V.tt(y.rearrange("p t (h d) -> p t h d", h=H), acc[:, :, 0:F].rearrange("p t (h d) -> p t h d", h=H),
                     den[:].unsqueeze(3).to_broadcast([P, NT, H, D]), ALU.mult)
                V.tt(y, y, skip[:], ALU.add)
                V.tt(y, y, per_feature(rows[:, 4, :]), ALU.add)
                nc.vector.tensor_scalar(low[:], y, 0.0, None, ALU.min).then_inc(asked, 1)
                dve.wait_ge(given, 2)
                V.stt(h[:], y, 0.0, low[:], ALU.max, ALU.add)
                V.ts(h[:], h[:], -1.0, ALU.add)
                if last_x is not None:
                    V.tt(last_x[:], last_x[:], h[:], ALU.add)


def norm_phase(nc, C, name, x, h):
    with Phase(nc, name) as ph:
        tmp = ph.sb("tmp", [P, NT, F])
        stat = ph.sb("stat", [P, 3, NT])
        chain, to_root, rooted = ph.sem("chain"), ph.sem("to_root"), ph.sem("rooted")
        block = ph.block()

        @block.scalar
        def _(act):
            roots(nc, act, stat[:, 1], stat[:, 0], to_root, rooted)

        @block.vector
        def _(dve):
            normalized_relu(Vector(nc, dve, chain), dve, x, h, tmp, stat, to_root, rooted)


def gcn_layers(nc, C, name, a, x, h, table):
    L = 3
    with Phase(nc, name) as top:
        xc = [h] + [top.sb(f"xc{i}", [P, NT, F]) for i in range(1, L + 1)]
        ws = top.sb("ws", [P, L, F])
        bs = top.sb("bs", [P, L + 1, F])
        wout = top.sb("wout", [P, L + 1, F])
        gb = top.sb("gb", [P, 2, (L + 1), F])
        dinv = top.sb("dinv", [P, NT])
        ocnt = top.sb("ocnt", [P, NT])
        real = top.sb("real", [P, 1])

        def clear_padding(V, y):
            V.ts(y[:, NT - 1, :], y[:, NT - 1, :], real[:], ALU.mult)

        with Phase(nc, name + "a") as ph:
            deg = ph.sb("deg", [P, 2, NT])
            loaded, chain, to_root, rooted = (ph.sem(v) for v in ("loaded", "chain", "to_root", "rooted"))
            block = ph.block()

            @block.scalar
            def _(act):
                roots(nc, act, deg[:, 0], dinv[:], to_root, rooted)

            @block.sync
            def _(sp):
                sp.dma_start(ws[:], a["L1_gnn_Ws"].rearrange("l k m -> k l m")).then_inc(loaded, 16)
                sp.dma_start(wout[:], a["L1_gnn_Wout"].rearrange("(l k) m -> k l m", k=P)).then_inc(loaded, 16)
                sp.dma_start(bs[:, 0:L, :], a["L1_gnn_bs"].partition_broadcast(P)).then_inc(loaded, 16)
                sp.dma_start(bs[:, L, :], a["L1_gnn_bout"].partition_broadcast(P)).then_inc(loaded, 16)
                for k, v in enumerate(("bn_gamma", "bn_beta")):
                    sp.dma_start(gb[:, k], a["L1_gnn_" + v].rearrange("(l f) -> l f", f=F).partition_broadcast(P)).then_inc(loaded, 16)
                sp.wait_ge(loaded, 96)

            @block.vector
            def _(dve):
                V = Vector(nc, dve, chain)
                nc.vector.tensor_scalar(deg[:, 0], C.cnt["D"][:], 1.0, None, ALU.add).then_inc(to_root, 1)
                dve.wait_ge(rooted, 1)
                V.inverse_root(deg[:, 0], dinv[:], deg[:, 1])
                V.ts(ocnt[:], C.cnt["S"][:], 1.0, ALU.max)
                V.link(nc.vector.reciprocal(ocnt[:], ocnt[:]))
                V.ts(real[:], C.iota_col[:], float(LAST), ALU.is_lt)
        for l in range(L):
            with Phase(nc, f"{name}{l}") as lay:
                hd = lay.sb("hd", [P, NT, F])
                tau = lay.sb("tau", [P, NT, F])

                def finish(i, y):
                    d = dinv[:, bass.ds(i * NB, NB)].unsqueeze(2).to_broadcast([P, NB, F])
                    return nc.vector.tensor_tensor(hd[:, bass.ds(i * NB, NB), :], y, d, ALU.mult)

                linear(nc, C, f"{name}{l}l", [(xc[l], ws[:, l, :])], F, finish, (hd, table))
                sum_pass(nc, C, f"{name}{l}d", "D", table, tau)
                with Phase(nc, f"{name}{l}b") as ph:
                    chain = ph.sem("chain")
                    block = ph.block()

                    @block.vector
                    def _(dve):
                        V = Vector(nc, dve, chain)
                        V.tt(tau[:], tau[:], hd[:], ALU.add)
                        V.tt(tau[:], tau[:], per_node(dinv[:]), ALU.mult)
                        V.tt(tau[:], tau[:], per_feature(bs[:, l, :]), ALU.add)
                        V.ts(tau[:], tau[:], 0.0, ALU.max)
                save_table(nc, C, f"{name}{l}t", tau[:], table)
                with Phase(nc, f"{name}{l}g") as ph2:
                    acc = ph2.sb("acc", [P, NT, 2 * F])
                    sum_pass(nc, C, f"{name}{l}e", "S", table, acc, squares=True)
                    with Phase(nc, f"{name}{l}c") as ph:
                        chain, asked, given = ph.sem("chain"), ph.sem("asked"), ph.sem("given")
                        block = ph.block()

                        @block.scalar
                        def _(act):
                            act.wait_ge(asked, 1)
                            nc.scalar.activation(hd[:], hd[:], ACT.Tanh).then_inc(given, 1)

                        @block.vector
                        def _(dve):
                            V = Vector(nc, dve, chain)
                            V.tt(hd[:], tau[:], per_node(C.cnt["S"][:]), ALU.mult)
                            V.stt(hd[:], acc[:, :, 0:F], -2.0, hd[:], ALU.mult, ALU.add)
                            V.tt(hd[:], hd[:], tau[:], ALU.mult)
                            V.tt(hd[:], hd[:], acc[:, :, F:2 * F], ALU.add)
                            nc.vector.tensor_tensor(hd[:], hd[:], per_node(ocnt[:]), ALU.mult).then_inc(asked, 1)
                            dve.wait_ge(given, 1)
                            V.tt(tau[:], tau[:], xc[l][:], ALU.subtract)
                            V.tt(tau[:], tau[:], hd[:], ALU.mult)
                            V.tt(xc[l + 1][:], tau[:], xc[l][:], ALU.add)
                            clear_padding(V, xc[l + 1])
        with Phase(nc, name + "n") as ph:
            squared = ph.sb("squared", [P, 2, NT, F])
            stat = ph.sb("stat", [P, F])
            var = ph.sb("var", [P, 2, F])
            p_sum = [ph.ps(f"p_sum{q}", [P, 512]) for q in range(2 * (L + 1))]
            chain, asked, given, to_root, rooted = (ph.sem(v) for v in ("chain", "asked", "given", "to_root", "rooted"))
            block = ph.block()

            @block.scalar
            def _(act):
                roots(nc, act, var[:, 0], stat[:], to_root, rooted, L + 1)

            @block.vector
            def _(dve):
                V = Vector(nc, dve, chain)

                def normalize(q):
                    y = xc[q]
                    dve.wait_ge(given, L + 1 + q + 1)
                    nc.vector.tensor_scalar(var[:, 0], p_sum[L + 1 + q][:, 0:F], 1.0 / N, EPS, ALU.mult,
                                            ALU.add).then_inc(to_root, 1)
                    dve.wait_ge(rooted, q + 1)
                    V.inverse_root(var[:, 0], stat[:], var[:, 1])
                    V.tt(stat[:], stat[:], gb[:, 0, q, :], ALU.mult)
                    V.tt(y[:], y[:], per_feature(stat[:]), ALU.mult)
                    V.tt(y[:], y[:], per_feature(gb[:, 1, q, :]), ALU.add)

                nc.vector.tensor_scalar(h[:, NT - 1, :], h[:, NT - 1, :], real[:], None, ALU.mult).then_inc(asked, 1)
                for q in range(L + 1):
                    y = xc[q]
                    dve.wait_ge(given, q + 1)
                    V.ts(stat[:], p_sum[q][:, 0:F], 1.0 / N, ALU.mult)
                    V.tt(y[:], y[:], per_feature(stat[:]), ALU.subtract)
                    clear_padding(V, y)
                    nc.vector.tensor_tensor(squared[:, q % 2], y[:], y[:], ALU.mult).then_inc(asked, 1)
                    if q >= 1:
                        normalize(q - 1)
                normalize(L)

            @block.tensor
            def _(pe):
                def column_sums(k, y):
                    for t in range(NT):
                        last = nc.tensor.matmul(p_sum[k][:, 0:F], C.ones[:], y[:, t, :], start=(t == 0), stop=(t == NT - 1))
                    last.then_inc(given, 1)

                pe.wait_ge(asked, 1)
                for q in range(L + 1):
                    column_sums(q, xc[q])
                for q in range(L + 1):
                    pe.wait_ge(asked, q + 2)
                    column_sums(L + 1 + q, squared[:, q % 2])

        with Phase(nc, name + "o") as ph:
            y1 = ph.sb("y1", [P, NB, F])
            added = ph.sem("added")

            def finish(i, y):
                nc.vector.tensor_tensor(y1[:], y, bs[:, L, :].unsqueeze(1).to_broadcast([P, NB, F]), ALU.add).then_inc(added, 1)
                nc.vector.wait_ge(added, i + 1)
                at = x[:, bass.ds(i * NB, NB), :]
                return nc.vector.tensor_tensor(at, at, y1[:], ALU.add)

            linear(nc, C, name + "l", [(xc[q], wout[:, q, :]) for q in range(L + 1)], F, finish)


def attention_layer(nc, C, name, a, x, h):
    table = a["edge_attr_256"].rearrange("e (s f) -> (e s) f", s=2)
    with Phase(nc, name) as top:
        accs = {side: top.sb("acc" + side, [P, NT, F + 1]) for side in "DS"}
        run = {side: top.sb("run" + side, [P, T + 1]) for side in "DS"}
        cont = {side: top.sb("cont" + side, [P, T]) for side in "DS"}
        agg = top.sb("agg", [P, NT, F])
        ht = top.sb("ht", [P, NT, F])
        w = top.sb("w", [P, 2, F])
        b = top.sb("b", [P, F])
        turn_nodes(nc, C, name + "t", h, ht)
        for side in "DS":
            attention_pass(nc, C, name + side, side, table, ht, accs[side], run[side], cont[side])
        with Phase(nc, name + "a") as ph:
            den = ph.sb("den", [P, NT])
            low = ph.sb("low", [P, T])
            m = ph.sb("m", [P, 2, NT])
            most = ph.sb("most", [P, NT])
            scaled = ph.sb("scaled", [P, NT, F + 1])
            loaded, chain, asked, given = (ph.sem(x) for x in ("loaded", "chain", "asked", "given"))
            block = ph.block()

            @block.scalar
            def _(act):
                act.wait_ge(asked, 1)
                nc.scalar.activation(m[:], m[:], ACT.Exp, scale=float(F) ** -0.5).then_inc(given, 1)

            @block.sync
            def _(sp):
                sp.dma_start(w[:], a["L2_gnn_W"].rearrange("(l k) m -> k l m", k=P)).then_inc(loaded, 16)
                sp.dma_start(b[:], a["L2_gnn_b"].partition_broadcast(P)).then_inc(loaded, 16)
                sp.wait_ge(loaded, 32)

            @block.vector
            def _(dve):
                V = Vector(nc, dve, chain)
                for k, side in enumerate("DS"):
                    for b_ in range(NT):
                        V.ts(low[:], C.nt[side][:], float(b_), ALU.not_equal, -4.0 * BIG, ALU.mult)
                        V.link(nc.vector.tensor_tensor_reduce(out=low[:], in0=low[:], in1=run[side][:, 1:T + 1], scale=1.0,
                                                              scalar=-BIG, op0=ALU.add, op1=ALU.max,
                                                              accum_out=m[:, k, b_:b_ + 1]))
                V.tt(most[:], m[:, 0], m[:, 1], ALU.max)
                nc.vector.tensor_tensor(m[:], m[:], most[:].unsqueeze(1).to_broadcast([P, 2, NT]),
                                        ALU.subtract).then_inc(asked, 1)
                dve.wait_ge(given, 1)
                for k, side in enumerate("DS"):
                    V.tt(accs[side][:], accs[side][:], m[:, k].unsqueeze(2).to_broadcast([P, NT, F + 1]), ALU.mult)
                acc = scaled
                V.tt(acc[:], accs["D"][:], accs["S"][:], ALU.add)
                V.ts(den[:], acc[:, :, F], 1e-30, ALU.max)
                V.link(nc.vector.reciprocal(den[:], den[:]))
                V.tt(agg[:], acc[:, :, 0:F], per_node(den[:]), ALU.mult)

        with Phase(nc, name + "o") as ph:
            y1 = ph.sb("y1", [P, NB, F])
            added = ph.sem("added")

            def finish(i, y):
                nc.vector.tensor_tensor(y1[:], y, b[:].unsqueeze(1).to_broadcast([P, NB, F]), ALU.add).then_inc(added, 1)
                nc.vector.wait_ge(added, i + 1)
                at = x[:, bass.ds(i * NB, NB), :]
                return nc.vector.tensor_tensor(at, at, y1[:], ALU.add)

            linear(nc, C, name + "l", [(agg, w[:, 0, :]), (h, w[:, 1, :])], F, finish)


def filter_layer(nc, C, name, a, x, h, table):
    with Phase(nc, name) as top:
        agg = top.sb("agg", [P, NT, F])
        wt = top.sb("wt", [P, T])
        w = top.sb("w", [P, F])
        save_table(nc, C, name + "s", h[:], table)
        with Phase(nc, name + "a") as ph:
            sc = ph.sb("sc", [P, 4])
            v = ph.sb("v", [P, 3, T])
            ok = ph.sb("ok", [P, T])
            oki = ph.sb("oki", [P, T], dt.uint32)
            loaded, chain, asked, given = (ph.sem(x) for x in ("loaded", "chain", "asked", "given"))
            block = ph.block()

            @block.sync
            def _(sp):
                for k, n in enumerate(("log_scale", "filter_w", "filter_b")):
                    sp.dma_start(sc[:, k:k + 1], a["L3_gnn_" + n].partition_broadcast(P)).then_inc(loaded, 16)
                sp.dma_start(w[:], a["L3_gnn_W_mix"]).then_inc(loaded, 16)
                sp.wait_ge(loaded, 64)

            @block.scalar
            def _(act):
                act.wait_ge(loaded, 64)
                nc.scalar.activation(sc[:, 3:4], sc[:, 0:1], ACT.Exp).then_inc(given, 1)
                act.wait_ge(asked, 1)
                nc.scalar.activation(v[:, 0], v[:, 0], ACT.Exp, scale=-1.0).then_inc(given, 1)
                act.wait_ge(asked, 2)
                nc.scalar.activation(v[:, 1], v[:, 1], ACT.Exp, scale=-1.0).then_inc(given, 1)

            @block.vector
            def _(dve):
                V = Vector(nc, dve, chain)
                dve.wait_ge(loaded, 64)
                dve.wait_ge(given, 1)
                length = C.rec["D"][:, :, 3]
                V.ts(sc[:, 3:4], sc[:, 3:4], 1e-6, ALU.add)
                V.link(nc.vector.reciprocal(sc[:, 3:4], sc[:, 3:4]))
                V.ts(v[:, 2], length, sc[:, 3:4], ALU.mult, 0.0, ALU.max)
                nc.vector.tensor_tensor(v[:, 0], v[:, 2], v[:, 2], ALU.mult).then_inc(asked, 1)
                nc.vector.tensor_scalar(v[:, 1], length, sc[:, 1:2], sc[:, 2:3], ALU.mult, ALU.add).then_inc(asked, 1)
                dve.wait_ge(given, 3)
                V.ts(v[:, 1], v[:, 1], 1.0, ALU.add)
                V.link(nc.vector.reciprocal(v[:, 1], v[:, 1]))
                V.tt(v[:, 0], v[:, 0], v[:, 1], ALU.mult)
                V.ts(ok[:], v[:, 0], 3.4e38, ALU.is_le)
                V.ts(v[:, 1], v[:, 0], -3.4e38, ALU.is_ge)
                V.tt(oki[:], ok[:], v[:, 1], ALU.mult)
                V.link(nc.vector.memset(wt[:], 0.0))
                V.link(nc.vector.copy_predicated(wt[:], oki[:], v[:, 0]))

        sum_pass(nc, C, name + "d", "D", table, agg, weights=wt)
        with Phase(nc, name + "b") as ph:
            deg = ph.sb("deg", [P, NT])
            chain = ph.sem("chain")
            block = ph.block()

            @block.vector
            def _(dve):
                V = Vector(nc, dve, chain)
                V.ts(deg[:], C.cnt["D"][:], 1.0, ALU.max)
                V.link(nc.vector.reciprocal(deg[:], deg[:]))
                V.tt(agg[:], agg[:], per_node(deg[:]), ALU.mult)
                V.tt(x[:], x[:], h[:], ALU.add)

        def finish(i, y):
            at = x[:, bass.ds(i * NB, NB), :]
            return nc.vector.tensor_tensor(at, at, y, ALU.add)

        linear(nc, C, name + "l", [(agg, w[:])], F, finish)


class Shared:
    pass


def program(nc, a, out):
    ctx = ExitStack()
    with ctx:
        def sb(name, shape, d=F32):
            return ctx.enter_context(nc.sbuf_tensor(name, shape, d))

        C = Shared()
        C.iota_row = sb("iota_row", [P, P])
        C.iota_col = sb("iota_col", [P, 1])
        C.ident = sb("ident", [P, P])
        C.ones = sb("ones", [P, P])
        C.before = sb("before", [P, P])
        C.zerosb = sb("zerosb", [P, P], BF16)
        PASSED[:] = [nc.alloc_semaphore("passed")]
        constants(nc, C)
        C.rec, C.nt, C.cnt, C.loc = {}, {}, {}, {}
        sides = []
        for s, key, other, row in (("D", "dst", "src", 0), ("S", "src", "dst", 1)):
            C.rec[s] = sb(f"rec{s}", [P, T, RW])
            C.nt[s] = sb(f"nt{s}", [P, T], I32)
            C.cnt[s] = sb(f"cnt{s}", [P, NT])
            C.loc[s] = nc.dram_tensor(f"loc{s}", [T, P], F32).ap()
            records = nc.dram_tensor(f"records{s}", [SLOTS, RW], F32).ap()
            sides.append((s, a[key], a[other], row, C.rec[s], C.nt[s], C.cnt[s], C.loc[s], records))
        sort_edges(nc, C, sides, a["edge_weight1"], a["edge_weight"])
        x = sb("x_now", [P, NT, F])
        h = sb("h_now", [P, NT, F])
        t136 = nc.dram_tensor("table_heads", [NP, F + 8], F32).ap()
        t129 = nc.dram_tensor("table_head", [NP, F + 1], F32).ap()
        table = nc.dram_tensor("table", [NP, F], F32).ap()
        with Phase(nc, "in") as ph:
            loaded, cleared = ph.sem("loaded"), ph.sem("cleared")
            block = ph.block()

            @block.vector
            def _(dve):
                nc.vector.memset(x[:, NT - 1, :], 0.0).then_inc(cleared, 1)

            @block.sync
            def _(sp):
                sp.wait_ge(cleared, 1)
                whole = (NT - 1) * P
                sp.dma_start(x[:, 0:NT - 1, :], a["x"][0:whole, :].rearrange("(t p) f -> p t f", p=P)).then_inc(loaded, 16)
                sp.dma_start(x[0:LAST, NT - 1, :], a["x"][whole:N, :]).then_inc(loaded, 16)
                sp.wait_ge(loaded, 32)

        clear_semaphores(nc)
        norm_phase(nc, C, "ln0", x, h)
        g = lambda n: a["L0_gnn_" + n]
        gat_layer(nc, C, "gatA", a, g("W1"), g("Wt1"), g("a_src1"), g("a_trg1"), g("a_tp1"), g("b1"), g("Wskip1"), 8, x, h, t136)
        clear_semaphores(nc)
        gat_layer(nc, C, "gatB", a, g("W2"), g("Wt2"), g("a_src2"), g("a_trg2"), g("a_tp2"), g("b2"), None, 1, x, h, t129, x)
        clear_semaphores(nc)
        norm_phase(nc, C, "ln1", x, h)
        gcn_layers(nc, C, "gcn", a, x, h, table)
        clear_semaphores(nc)
        norm_phase(nc, C, "ln2", x, h)
        attention_layer(nc, C, "att", a, x, h)
        clear_semaphores(nc)
        norm_phase(nc, C, "ln3", x, h)
        filter_layer(nc, C, "fil", a, x, h, table)
        with Phase(nc, "out") as ph:
            stored = ph.sem("stored")
            block = ph.block()

            @block.sync
            def _(sp):
                whole = (NT - 1) * P
                sp.dma_start(out[0:whole, :].rearrange("(t p) f -> p t f", p=P), x[:, 0:NT - 1, :]).then_inc(stored, 16)
                sp.dma_start(out[whole:N, :], x[0:LAST, NT - 1, :]).then_inc(stored, 16)
                sp.wait_ge(stored, 32)


_FLAT = ("edge_weight1", "L0_gnn_Wt1", "L0_gnn_a_src1", "L0_gnn_a_trg1", "L0_gnn_a_tp1", "L0_gnn_Wt2", "L0_gnn_a_src2",
         "L0_gnn_a_trg2", "L0_gnn_a_tp2", "L3_gnn_log_scale", "L3_gnn_filter_w", "L3_gnn_filter_b")


def kernel(**inputs):
    import numpy as _np
    import concourse.bacc as _bacc
    from concourse import mybir as _mybir
    from concourse.bass_utils import run_bass_kernel_spmd as _run

    nc = _bacc.Bacc("TRN2", target_bir_lowering=False, num_devices=1)
    arrays, aps = {}, {}
    for name, value in inputs.items():
        v = _np.ascontiguousarray(value)
        if name in _FLAT:
            v = v.reshape(-1)
        arrays[f"in_{name}"] = v
        aps[name] = nc.dram_tensor(f"in_{name}", v.shape, _mybir.dt.from_np(v.dtype), kind="ExternalInput").ap()
    out = nc.dram_tensor("out_x", (N, F), F32, kind="ExternalOutput").ap()
    program(nc, aps, out)
    r = _run(nc, [arrays], core_ids=[0])
    return r.results[0]["out_x"]
```
